# Optimizing a Trainium2 kernel written in Bass

```python
import numpy as np
import jax
import jax.numpy as jnp

def _softmax(x, axis=-1):
    return jax.nn.softmax(x, axis=axis)

def _gelu(x):
    return jax.nn.gelu(x, approximate=True)

def _silu(x):
    return jax.nn.silu(x)

def _sigmoid(x):
    return jax.nn.sigmoid(x)

def _layernorm(x, axis=-1, eps=1e-05):
    m = jnp.mean(x, axis=axis, keepdims=True)
    v = jnp.var(x, axis=axis, keepdims=True)
    return (x - m) / jnp.sqrt(v + eps)

def _scatter_add(tgt, idx, src, axis=0):
    return tgt.at[idx].add(src)

def _segment_sum(src, seg, n):
    return jax.ops.segment_sum(src, seg, n)
kernel_name = 'mk_perceiver_d1_seqx_r4_af63d5'

def setup_inputs(seed: int=0):
    np.random.seed(seed)
    _w = jnp.asarray

    def _rec_inputs():
        import jax
        import jax.numpy as jnp
        _rk = jax.random.key(seed)
        x = 7.22e-05 + 1 * jax.random.normal(jax.random.fold_in(_rk, 1), (32, 64, 256), jnp.float32)
        _lenS = 64 - jax.random.randint(jax.random.fold_in(_rk, 7), (32,), 0, max(1, 64 // 4) + 1, jnp.int32)
        _lenS2 = 256 - jax.random.randint(jax.random.fold_in(_rk, 8), (32,), 0, max(1, 256 // 4) + 1, jnp.int32)
        _ctx_1024P = jax.random.normal(jax.random.fold_in(_rk, 11), (32, 16, 256), jnp.float32)
        _ctx_1024c = jax.random.dirichlet(jax.random.fold_in(_rk, 511), 0.3 * jnp.ones((16,), jnp.float32), (32, 256))
        _ctx_1024t = jnp.einsum('bsk,bkd->bsd', _ctx_1024c, _ctx_1024P)
        _ctx_1024t = _ctx_1024t * jax.lax.rsqrt(jnp.mean(jnp.square(_ctx_1024t)) + 1e-12) * 0.953939
        ctx_1024 = 4.13588e-05 + 0.999923 * (_ctx_1024t + 0.3 * jax.random.normal(jax.random.fold_in(_rk, 611), (32, 256, 256), jnp.float32))
        return (x, ctx_1024)
    x, ctx_1024 = _rec_inputs()

    def _L0_xattn_setup():
        import jax, jax.numpy as jnp
        import numpy as np
        N_HEAD = 16
        key = jax.random.key(seed)
        ks = jax.random.split(key, 5)
        b, l, d = (4, 512, 256)
        dh = d // N_HEAD
        return {'q': jax.random.normal(ks[0], (b, l, d), dtype=jnp.float32), 'kv': jax.random.normal(ks[1], (b, l, d), dtype=jnp.float32), 'Wq': jax.random.normal(ks[2], (d, d), dtype=jnp.float32) * 0.02, 'Wkv': jax.random.normal(ks[3], (2 * dh, d), dtype=jnp.float32) * 0.02, 'Wc': jax.random.normal(ks[4], (d, d), dtype=jnp.float32) * 0.02}
    _L0_xattn_all = _L0_xattn_setup()
    _L0_xattn_in = {k: v for k, v in _L0_xattn_all.items() if k in ('Wq', 'Wkv', 'Wc')}
    del _L0_xattn_all

    def _L0_attn_setup():
        import jax, jax.numpy as jnp
        import numpy as np
        B, S, D, H, A = (2, 512, 256, 16, 64)
        INIT_STD = 0.02
        key = jax.random.key(seed)
        ks = jax.random.split(key, 5)
        return {'residual': jax.random.normal(ks[0], (B, S, D), dtype=jnp.float32), 'Wq': jax.random.normal(ks[1], (H, D, A), dtype=jnp.float32) * INIT_STD, 'Wk': jax.random.normal(ks[2], (H, D, A), dtype=jnp.float32) * INIT_STD, 'Wv': jax.random.normal(ks[3], (H, D, A), dtype=jnp.float32) * INIT_STD, 'Wo': jax.random.normal(ks[4], (H, A, D), dtype=jnp.float32) * INIT_STD, 'bq': jnp.zeros((H, A), dtype=jnp.float32), 'bk': jnp.zeros((H, A), dtype=jnp.float32), 'bv': jnp.zeros((H, A), dtype=jnp.float32), 'bo': jnp.zeros((D,), dtype=jnp.float32)}
    _L0_attn_all = _L0_attn_setup()
    _L0_attn_in = {k: v for k, v in _L0_attn_all.items() if k in ('Wq', 'Wk', 'Wv', 'Wo', 'bq', 'bk', 'bv', 'bo')}
    del _L0_attn_all

    def _L0_ffn_setup():
        import jax, jax.numpy as jnp
        import numpy as np
        B, S, D, F, E = (2, 512, 256, 1024, 8)
        LN_EPS = 1e-05

        def _layer_norm(x, gamma, beta):
            mu = jnp.mean(x, axis=-1, keepdims=True)
            var = jnp.mean(jnp.square(x - mu), axis=-1, keepdims=True)
            return (x - mu) * jax.lax.rsqrt(var + LN_EPS) * gamma + beta
        key = jax.random.key(seed)
        ks = jax.random.split(key, 8)

        def xavier(k, shape):
            fan_in, fan_out = (shape[-1], shape[-2])
            a = jnp.sqrt(6.0 / (fan_in + fan_out))
            return jax.random.uniform(k, shape, jnp.float32, -a, a)
        return {'tgt': jax.random.normal(ks[0], (B, S, D), jnp.float32), 'Wr': xavier(ks[1], (E, D)), 'br': jnp.zeros((E,), jnp.float32), 'W1': xavier(ks[2], (E, F, D)), 'b1': jnp.zeros((E, F), jnp.float32), 'W2': xavier(ks[3], (E, D, F)), 'b2': jnp.zeros((E, D), jnp.float32), 'gamma': jnp.ones((D,), jnp.float32), 'beta': jnp.zeros((D,), jnp.float32)}
    _L0_ffn_all = _L0_ffn_setup()
    _L0_ffn_in = {k: v for k, v in _L0_ffn_all.items() if k in ('Wr', 'br', 'W1', 'b1', 'W2', 'b2', 'gamma', 'beta')}
    del _L0_ffn_all
    return {'x': x, 'ctx_1024': ctx_1024, 'L0_xattn_Wq': _L0_xattn_in['Wq'], 'L0_xattn_Wkv': _L0_xattn_in['Wkv'], 'L0_xattn_Wc': _L0_xattn_in['Wc'], 'L0_attn_Wq': _L0_attn_in['Wq'], 'L0_attn_Wk': _L0_attn_in['Wk'], 'L0_attn_Wv': _L0_attn_in['Wv'], 'L0_attn_Wo': _L0_attn_in['Wo'], 'L0_attn_bq': _L0_attn_in['bq'], 'L0_attn_bk': _L0_attn_in['bk'], 'L0_attn_bv': _L0_attn_in['bv'], 'L0_attn_bo': _L0_attn_in['bo'], 'L0_ffn_Wr': _L0_ffn_in['Wr'], 'L0_ffn_br': _L0_ffn_in['br'], 'L0_ffn_W1': _L0_ffn_in['W1'], 'L0_ffn_b1': _L0_ffn_in['b1'], 'L0_ffn_W2': _L0_ffn_in['W2'], 'L0_ffn_b2': _L0_ffn_in['b2'], 'L0_ffn_gamma': _L0_ffn_in['gamma'], 'L0_ffn_beta': _L0_ffn_in['beta']}

def reference(x, ctx_1024, L0_xattn_Wq, L0_xattn_Wkv, L0_xattn_Wc, L0_attn_Wq, L0_attn_Wk, L0_attn_Wv, L0_attn_Wo, L0_attn_bq, L0_attn_bk, L0_attn_bv, L0_attn_bo, L0_ffn_Wr, L0_ffn_br, L0_ffn_W1, L0_ffn_b1, L0_ffn_W2, L0_ffn_b2, L0_ffn_gamma, L0_ffn_beta):
    import jax
    import jax.numpy as jnp

    def _L0_xattn_ref(q, kv, Wq, Wkv, Wc):
        import jax, jax.numpy as jnp
        import numpy as np
        N_HEAD = 16
        b, l, d = q.shape
        h = N_HEAD
        dh = d // h
        qp = jnp.einsum('bld,ed->ble', q, Wq)
        scores = jnp.einsum('bld,bmd->blm', qp, kv)
        idx = jnp.argmax(scores, axis=-1)
        mem = jnp.take_along_axis(kv, idx[..., None], axis=1)
        mkv = jnp.einsum('bld,ed->ble', mem, Wkv)
        mk, mv = jnp.split(mkv, 2, axis=-1)
        qh = qp.reshape(b, l, h, dh).transpose(0, 2, 1, 3)
        scale = 1.0 / np.sqrt(dh).astype(np.float32)
        logits = jnp.einsum('bhld,bmd->bhlm', qh, mk) * scale
        attn = jax.nn.softmax(logits, axis=-1)
        out = jnp.einsum('bhlm,bmd->bhld', attn, mv)
        out = out.transpose(0, 2, 1, 3).reshape(b, l, d)
        return jnp.einsum('bld,ed->ble', out, Wc)

    def _L0_attn_ref(residual, Wq, Wk, Wv, Wo, bq, bk, bv, bo):
        import jax, jax.numpy as jnp
        import numpy as np
        B, S, D, H, A = (2, 512, 256, 16, 64)
        INIT_STD = 0.02
        q = jnp.einsum('bsd,hda->bhsa', residual, Wq) + bq[None, :, None, :]
        k = jnp.einsum('bsd,hda->bhsa', residual, Wk) + bk[None, :, None, :]
        v = jnp.einsum('bsd,hda->bhsa', residual, Wv) + bv[None, :, None, :]
        scale = 1.0 / jnp.sqrt(jnp.float32(q.shape[-1]))
        scores = jnp.einsum('bhsa,bhta->bhst', q, k) * scale
        s = scores.shape[-1]
        causal = jnp.tril(jnp.ones((s, s), dtype=bool))
        masked = jnp.where(causal, scores, jnp.float32(-100000.0))
        pattern = jax.nn.softmax(masked, axis=-1)
        z = jnp.einsum('bhst,bhta->bshа'.replace('а', 'a'), pattern, v)
        out = jnp.einsum('bsha,had->bsd', z, Wo) + bo
        return out

    def _L0_ffn_ref(tgt, Wr, br, W1, b1, W2, b2, gamma, beta):
        import jax, jax.numpy as jnp
        import numpy as np
        B, S, D, F, E = (2, 512, 256, 1024, 8)
        LN_EPS = 1e-05

        def _layer_norm(x, gamma, beta):
            mu = jnp.mean(x, axis=-1, keepdims=True)
            var = jnp.mean(jnp.square(x - mu), axis=-1, keepdims=True)
            return (x - mu) * jax.lax.rsqrt(var + LN_EPS) * gamma + beta
        logits = jnp.einsum('bsd,ed->bse', tgt, Wr) + br
        top_v, top_i = jax.lax.top_k(logits, 2)
        top_w = jax.nn.softmax(top_v, axis=-1)
        n_exp = logits.shape[-1]
        router_w = jnp.sum(jax.nn.one_hot(top_i, n_exp, dtype=top_w.dtype) * top_w[..., None], axis=-2)
        h = jnp.einsum('bsd,efd->bsef', tgt, W1) + b1
        h = jax.nn.relu(h)
        o = jnp.einsum('bsef,edf->bsed', h, W2) + b2
        tgt2 = jnp.einsum('bsed,bse->bsd', o, router_w)
        return _layer_norm(tgt + tgt2, gamma, beta)
    x = x + _L0_xattn_ref(_layernorm(x, axis=-1), ctx_1024, L0_xattn_Wq, L0_xattn_Wkv, L0_xattn_Wc)
    x = x + _L0_attn_ref(_layernorm(x, axis=-1), L0_attn_Wq, L0_attn_Wk, L0_attn_Wv, L0_attn_Wo, L0_attn_bq, L0_attn_bk, L0_attn_bv, L0_attn_bo)
    x = x + _L0_ffn_ref(_layernorm(x, axis=-1), L0_ffn_Wr, L0_ffn_br, L0_ffn_W1, L0_ffn_b1, L0_ffn_W2, L0_ffn_b2, L0_ffn_gamma, L0_ffn_beta)
    return x

_drawn_inputs = setup_inputs


def setup_inputs(seed=0):
    import zlib

    import numpy as np

    out = dict(_drawn_inputs(seed))
    spreads = {'L0_attn_bq': (0.0, 0.8),
     'L0_attn_bk': (0.0, 0.8),
     'L0_attn_bv': (0.0, 0.1),
     'L0_attn_bo': (0.0, 0.1),
     'L0_ffn_br': (0.0, 0.1),
     'L0_ffn_b1': (0.0, 0.1),
     'L0_ffn_b2': (0.0, 0.1),
     'L0_ffn_gamma': (1.0, 0.2),
     'L0_ffn_beta': (0.0, 0.1)}
    factors = {'L0_attn_Wq': 7.152, 'L0_attn_Wk': 5.564}
    for name, (base, spread) in spreads.items():
        noise = np.random.default_rng([zlib.crc32(name.encode()), seed]).standard_normal(out[name].shape)
        drawn = base * np.exp(spread * noise) if base else spread * noise
        out[name] = jnp.asarray(drawn.astype(out[name].dtype))
    for name, factor in factors.items():
        out[name] = (out[name] * factor).astype(out[name].dtype)
    return out
```

```python
from contextlib import ExitStack

import concourse.bass as bass
from concourse import mybir

F32 = mybir.dt.float32
I32 = mybir.dt.int32
U32 = mybir.dt.uint32
ALU = mybir.AluOpType
ACT = mybir.ActivationFunctionType
AX_X = mybir.AxisListType.X
P = 128


class Steps:

    def __init__(self, engine, sem, per_block):
        self.engine, self.sem, self.per_block = engine, sem, per_block

    def begin(self, n):
        self.base, self.count = n * self.per_block, 0

    def did(self, instruction):
        self.count += 1
        instruction.then_inc(self.sem, 1)

    def wait_last(self):
        self.engine.wait_ge(self.sem, self.base + self.count)

    def hold_last(self, beside):
        self.wait_last()
        if not isinstance(self.base, int):
            self.engine.sem_inc(beside, 1)

    def end(self):
        assert self.count == self.per_block, (self.sem, self.count)


def perceiver_layer(nc, x, ctxT, xWqT, xWkvT, xWcT, aWq, aWk, aWv, aWo, bq, bk, bv, bo,
                    WrT, br, W1T, b1, W2T, b2, gamma, beta, out):
    NB, S, D = x.shape
    M = ctxT.shape[2]
    TOK = NB * S
    BLK = TOK // P
    BB = P // S
    KD = D // P
    KM = M // P
    H = 16
    XD = D // H
    HA = aWq.shape[1]
    A = HA // H
    HP = HA // P
    E = WrT.shape[1]
    F = W1T.shape[2]
    KF = F // P
    FH = F // 512
    ROW = D + 2
    REG = TOK + P
    TILES = 2 * TOK // P + E - 1
    EPS = 1e-5
    MASKED = -100000.0 * float(A) ** 0.5
    FAR = 1 << 24

    routed = nc.dram_tensor("routed", (E * REG + P, ROW), F32, kind="Internal").ap()
    target = nc.dram_tensor("target", (TOK, D), F32, kind="Internal").ap()
    expert_out = nc.dram_tensor("expert_out", (2 * TOK, D), F32, kind="Internal").ap()

    ctx = ExitStack()
    with ctx:
        def sb(name, shape, dt=F32):
            return ctx.enter_context(nc.sbuf_tensor(name, shape, dt))

        def sem(name):
            return ctx.enter_context(nc.semaphore(name))

        w1 = sb("w1", [P, E, KD, F])
        xall = sb("xall", [P, BLK, D])
        xwq, xwkv, xwc = sb("xwq", [P, KD, D]), sb("xwkv", [P, KD, 2 * XD]), sb("xwc", [P, KD, D])
        awq, awk, awv = (sb(n, [P, KD, HA]) for n in ("awq", "awk", "awv"))
        awo = sb("awo", [P, HP, D])
        bqT, bkT, bvT = (sb(n, [P, HP]) for n in ("bqT", "bkT", "bvT"))
        bo_all = sb("bo_all", [P, D])
        wr, br_all = sb("wr", [P, KD, E]), sb("br_all", [P, E])
        b1T = sb("b1T", [P, E * KF])
        b2_all = sb("b2_all", [P, E * D])
        gamma_all, beta_all = xwq[:, 0, :], xwq[:, 1, :]
        ident = sb("ident", [P, P])
        iota_m = sb("iota_m", [P, M])
        iota_e = sb("iota_e", [P, E])
        region = sb("region", [P, E])
        causal = sb("causal", [P, S])
        headmask = sb("headmask", [P, P // XD])
        before = sb("before", [P, P])
        ones = sb("ones", [P, P])
        minus_half = sb("minus_half", [P, 1])
        dest = sb("dest", [P, BLK, 2])
        meta = sb("meta", [P, TILES, 2])
        target_row = sb("target_row", [P, 1], U32)
        row0, row1 = sb("row0", [P, ROW]), sb("row1", [P, ROW])
        x3T, lgr = sb("x3T", [P, KD, P]), sb("lgr", [P, E])
        st1, st2, st3 = (sb(n, [P, 16]) for n in ("st1", "st2", "st3"))
        lg, rv8, ri8 = sb("lg", [P, E]), sb("rv8", [P, 8]), sb("ri8", [P, 8], U32)
        oh0, oh1, ohs, pos = (sb(n, [P, E]) for n in ("oh0", "oh1", "ohs", "pos"))
        run = sb("run", [P, E])
        rtmp, rsc = sb("rtmp", [P, E]), sb("rsc", [P, 8])
        slot = sb("slot", [P, 2], U32)
        pad = sb("pad", [P, ROW])
        iota_t = sb("iota_t", [P, TILES])
        tiles_i, tiles, cum, cum2 = sb("tiles_i", [P, E], I32), sb("tiles", [P, E]), sb("cum", [P, E]), sb("cum2", [P, E])
        padrow_i = sb("padrow_i", [P, E], I32)
        tile_e, tile_s, tile_idle = (sb(n, [P, TILES]) for n in ("tile_e", "tile_s", "tile_idle"))
        tile_ei, tile_ri = sb("tile_ei", [P, TILES], I32), sb("tile_ri", [P, TILES], I32)
        with nc.sbuf_tensor("w2", [P, E, KF, D], F32) as w2:
            pass
        ctxb = sb("ctxb", [P, BB, KD, M])
        xn, xT, qpT = sb("xn", [P, D]), sb("xT", [P, KD, P]), sb("qpT", [P, KD, P])
        sc, ohT = sb("sc", [P, M]), sb("ohT", [P, KM, P])
        onehot = sc
        kvr, kvv = sb("kvr", [P, BB, KM, P // XD, XD]), sb("kvv", [P, BB, KM, XD])
        mkb = sb("mkb", [P, BB, P // XD, S])
        mvb = sb("mvb", [P, XD + 1])
        xs = sb("xs", [P, H, S])
        xprob = sb("xprob", [P, H, P])
        xpT = sb("xpT", [P, H, P])
        ao, aoT = sb("ao", [P, H, XD]), sb("aoT", [P, KD, P])
        xn2, x2T = sb("xn2", [P, D]), sb("x2T", [P, KD, P])
        qT, kT = sb("qT", [P, HP, P]), sb("kT", [P, HP, P])
        vs = sb("vs", [P, H, A + 1])
        as_ = sb("as_", [P, H, S])
        aprob = sb("aprob", [P, H, P])
        apT = sb("apT", [P, H, P])
        z = qT[:].rearrange("p c t -> p (c t)").rearrange("p (h a) -> p h a", a=A)
        zT = kT
        mx8, ix8 = sb("mx8", [P, 8]), sb("ix8", [P, 8], U32)
        amx, arc = sb("amx", [P, H]), sb("arc", [P, H])
        bmx, brc = sb("bmx", [P, H]), sb("brc", [P, H])
        hs, hT = awv[:, 0, :], awv[:, 1, :].rearrange("p (c t) -> p c t", t=P)
        spare = awo[:].rearrange("p c d -> p (c d)")
        passed, passed_tiles = (awv[:, j, 0:TILES * (E - 1)].rearrange("p (t e) -> p t e", e=E - 1) for j in range(2))
        xg, xgT = spare[:, 0:ROW], spare[:, 512:768].rearrange("p (k t) -> p k t", t=P)
        yb, yw = spare[:, 768:1024], spare[:, 1024:1280]
        YG = BLK // 4
        tgt = [w[:].rearrange("p k f -> p (k f)").rearrange("p (n d) -> p n d", d=D) for w in (awq, awk)]
        ypair = [w.rearrange("p (n k d) -> p n k d", k=2, d=D)
                 for w in (awv[:].rearrange("p k f -> p (k f)"), spare)]

        bank = [ctx.enter_context(nc.psum_tensor(f"bank{i}", [P, 512], F32)) for i in range(8)]

        ld_x, ld_ctx, ld_xw, ld_aw, ld_small = (sem(n) for n in ("ld_x", "ld_ctx", "ld_xw", "ld_aw", "ld_small"))
        const_ready = sem("const_ready")
        bo_ps, bo_done, bvrep_done = sem("bo_ps"), sem("bo_done"), sem("bvrep_done")
        a_dve, b_dve, c_dve, k_pool = sem("a_dve"), sem("b_dve"), sem("c_dve"), sem("k_pool")
        names_a = ("a_var", "a_rstd", "a_xn", "a_xT_ps", "a_xT", "a_qpT_ps", "a_qpT", "a_sc_ps", "a_sc", "a_kv_ps", "a_kv",
                   "a_onehot", "a_ohT_ps", "a_ohT", "a_mem_ps", "a_mkb", "a_log_ps", "a_xs", "a_prob", "a_pT_ps",
                   "a_pT_v", "a_pT_s", "a_av_ps", "a_ao", "a_aoT_ps", "a_aoT", "a_wc_ps", "a_x1")
        names_b = ("b_var", "b_rstd", "b_xn", "b_xb", "b_xT_ps", "b_xT", "b_q_ps", "b_q", "b_v_ps", "b_v", "b_s_ps", "b_mask",
                   "b_as", "b_prob", "b_pT_ps", "b_pT_v", "b_pT_s", "b_av_ps", "b_z", "b_zT_ps", "b_zT", "b_o_ps", "b_x2")
        names_c = ("c_var", "c_rstd", "c_xn", "c_xT_ps", "c_xT", "c_lg_ps", "c_lg", "c_d", "c_exp", "c_ohs", "c_pos_ps", "c_pos",
                   "c_row1", "c_weight", "c_scatter", "c_target")
        names_m = ("m_hist", "m_plan", "m_pads", "m_w1", "m_w2", "m_tgt", "m_gb", "m_bx")
        names_f = ("f_xg", "f_meta", "f_xT_ps", "f_xT", "f_h_ps", "f_hs_s", "f_hs_v", "f_hT_ps", "f_hT_s", "f_hT_v",
                   "f_o_ps", "f_yb", "f_yw", "f_row", "f_out")
        names_y = ("y_pair0", "y_pair1", "y_sum", "y_var", "y_rstd", "y_out", "y_store")
        s = {n: sem(n) for n in names_a + names_b + names_c + names_m + names_f + names_y}
        passed_by = {e: sem(f"passed_by_{e}") for e in ("dve", "pool", "pe")}
        m_dve, f_dve, y_dve = sem("m_dve"), sem("f_dve"), sem("y_dve")
        LAST = TILES - 1
        K_POOL = 23
        block = ctx.enter_context(nc.Block())

        def wait(engine, semaphore, value):
            if not isinstance(value, int) or value > 0:
                engine.wait_ge(semaphore, value)

        def hold(engine, name, semaphore, value):
            if not isinstance(value, int):
                engine.wait_ge(semaphore, value)
                engine.sem_inc(passed_by[name], 1)
            else:
                wait(engine, semaphore, value)

        def pipeline(engine, iteration):
            iteration(a=0)
            iteration(a=1, b=0)
            with engine.Fori(2, BLK) as n:
                iteration(a=n, b=n - 1, c=n - 2)
            iteration(b=BLK - 1, c=BLK - 2)
            iteration(c=BLK - 1)

        @block.sync
        def _(sp):
            def load_ctx(n):
                sp.dma_start(ctxb[:], ctxT[bass.ds(n * BB, BB)].rearrange("b (k p) m -> p b k m", p=P)).then_inc(ld_ctx, 16)

            xv = x.rearrange("(n b) s d -> (b s) n d", b=BB)
            sp.dma_start(xall[:, 0, :], xv[:, 0, :]).then_inc(ld_x, 16)
            load_ctx(0)
            for dst, src in ((xwq, xWqT), (xwkv, xWkvT), (xwc, xWcT)):
                sp.dma_start(dst[:], src.rearrange("(k p) e -> p k e", p=P)).then_inc(ld_xw, 16)
            sp.dma_start(xall[:, 1:BLK, :], xv[:, 1:BLK, :]).then_inc(ld_x, 16)
            for dst, src in ((awq, aWq), (awk, aWk), (awv, aWv), (awo, aWo), (wr, WrT)):
                sp.dma_start(dst[:], src.rearrange("(k p) e -> p k e", p=P)).then_inc(ld_aw, 16)
            with nc.allow_non_contiguous_dma(reason="small biases, once"):
                for dst, src in ((bqT, bq), (bkT, bk), (bvT, bv)):
                    sp.dma_start(dst[:], src.rearrange("(k p) -> p k", p=P)).then_inc(ld_small, 16)
                sp.dma_start(b1T[:], b1.rearrange("(k p) -> p k", p=P)).then_inc(ld_small, 16)
            for dst, src in ((bo_all, bo), (br_all, br), (b2_all, b2)):
                sp.dma_start(dst[:], src.partition_broadcast(P)).then_inc(ld_small, 16)
            for e in range(E):
                sp.dma_start(w1[:, e], W1T[e].rearrange("(k p) f -> p k f", p=P)).then_inc(s["m_w1"], 16)
            sp.wait_ge(k_pool, K_POOL)
            sp.dma_start(routed[E * REG:E * REG + P, :], pad[:]).then_inc(s["m_pads"], 16)

            def store_target(n):
                sp.wait_ge(s["c_xn"], n + 1)
                sp.dma_start(target[bass.ds(n * P, P), :], row0[:, 0:D]).then_inc(s["c_target"], 16)

            def iteration(a=None, b=None, c=None):
                if a is not None and (not isinstance(a, int) or a > 0):
                    sp.wait_ge(s["a_kv_ps"], a)
                    sp.wait_ge(s["a_sc_ps"], a)
                    load_ctx(a)
                if c is not None:
                    store_target(c)
            pipeline(sp, iteration)

            def load_w2(e):
                sp.dma_start(w2[:, e], W2T[e].rearrange("(k p) d -> p k d", p=P)).then_inc(s["m_w2"], 16)
            sp.wait_ge(s["a_wc_ps"], BLK)
            for e in range(E // 2):
                load_w2(e)
            sp.wait_ge(s["b_x2"], BLK)
            for e in range(E // 2, E):
                load_w2(e)
            sp.dma_start(gamma_all, gamma.partition_broadcast(P)).then_inc(s["m_gb"], 16)
            sp.dma_start(beta_all, beta.partition_broadcast(P)).then_inc(s["m_gb"], 16)
            sp.wait_ge(s["m_plan"], 1)
            for e in range(E):
                behind = sp.value_load(padrow_i[0:1, e:e + 1], min_val=e * REG, max_val=e * REG + TOK)
                sp.dma_start(routed[bass.ds(behind, P), :], pad[:]).then_inc(s["m_pads"], 16)
            sp.wait_ge(s["m_pads"], 16 * (E + 1))
            sp.wait_ge(s["c_scatter"], 32 * BLK)

            def load_tile(t):
                first = sp.value_load(tile_ri[0:1, bass.ds(t, 1)], min_val=0, max_val=E * REG)
                sp.dma_start(xg, routed[bass.ds(first, P), :]).then_inc(s["f_xg"], 16)

            load_tile(0)
            sp.wait_ge(s["c_target"], 16 * BLK)
            for half in range(2):
                sp.dma_start(tgt[half], target[half * TOK // 2:(half + 1) * TOK // 2, :]
                             .rearrange("(n p) d -> p n d", p=P)).then_inc(s["m_tgt"], 16)
            with sp.Fori(1, TILES) as t:
                sp.wait_ge(s["f_xT_ps"], t)
                sp.wait_ge(s["f_meta"], t)
                load_tile(t)

            sp.wait_ge(s["f_out"], 16 * TILES)
            sp.wait_ge(s["f_yw"], TILES)
            pairs = expert_out.rearrange("(n p k) d -> p n k d", p=P, k=2)

            def load_pairs(g):
                sp.dma_start(ypair[g % 2], pairs[:, g * YG:(g + 1) * YG]).then_inc(s[f"y_pair{g % 2}"], 16)
            for g in range(2):
                load_pairs(g)
            for g in range(4):
                sp.wait_ge(s["y_out"], YG * (g + 1))
                if g + 2 < 4:
                    load_pairs(g + 2)
                sp.dma_start(out.rearrange("(n b) s d -> (b s) n d", b=BB)[:, g * YG:(g + 1) * YG],
                             xall[:, g * YG:(g + 1) * YG, :]).then_inc(s["y_store"], 16)
            sp.wait_ge(s["y_store"], 64)
        N_SMALL = 7 * 16

        @block.gpsimd
        def _(g):
            cst = Steps(g, k_pool, K_POOL)
            cst.begin(0)

            def once(ins):
                cst.did(ins)
                cst.wait_last()
            once(g.memset(ident[:], 0.0))
            once(g.affine_select(out=ident[:], in_=ident[:], compare_op=ALU.not_equal, fill=1.0, base=0,
                                 pattern=[[-1, P]], channel_multiplier=1))
            once(g.memset(minus_half[:], -0.5))
            once(g.iota(iota_m[:], pattern=[[1, M]], base=0, channel_multiplier=0, allow_small_or_imprecise_dtypes=True))
            once(g.memset(headmask[:], 1.0))
            once(g.affine_select(out=headmask[:], in_=headmask[:], compare_op=ALU.is_ge, fill=0.0, base=0,
                                 pattern=[[-XD, P // XD]], channel_multiplier=1))
            once(g.affine_select(out=headmask[:], in_=headmask[:], compare_op=ALU.is_ge, fill=0.0, base=XD - 1,
                                 pattern=[[XD, P // XD]], channel_multiplier=-1))
            once(g.memset(mvb[:, XD:XD + 1], 1.0))
            once(g.memset(xprob[:], 0.0))
            once(g.memset(vs[:, :, A:A + 1], 1.0))
            once(g.memset(causal[:], 3e38))
            for b in range(BB):
                once(g.affine_select(out=causal[b * S:(b + 1) * S, :], in_=causal[b * S:(b + 1) * S, :], compare_op=ALU.is_ge,
                                     fill=MASKED, base=0, pattern=[[-1, S]], channel_multiplier=1))
            once(g.memset(aprob[:], 0.0))
            once(g.iota(iota_e[:], pattern=[[1, E]], base=0, channel_multiplier=0, allow_small_or_imprecise_dtypes=True))
            once(g.iota(region[:], pattern=[[REG, E]], base=0, channel_multiplier=0, allow_small_or_imprecise_dtypes=True))
            once(g.memset(ones[:], 1.0))
            once(g.affine_select(out=before[:], in_=ones[:], compare_op=ALU.is_ge, fill=0.0, base=-1,
                                 pattern=[[1, P]], channel_multiplier=-1))
            once(g.memset(run[:], 0.0))
            once(g.iota(dest[:], pattern=[[2 * P, BLK], [1, 2]], base=0, channel_multiplier=2,
                        allow_small_or_imprecise_dtypes=True))
            once(g.iota(iota_t[:], pattern=[[1, TILES]], base=0, channel_multiplier=0, allow_small_or_imprecise_dtypes=True))
            once(g.memset(pad[:], 0.0))
            once(g.memset(pad[:, D + 1:D + 2], float(FAR)))
            cst.end()

            def rstd(st, ready, done, n):
                hold(g, "pool", s[ready], n + 1)
                g.tensor_scalar(st[:, 8:9], st[:, 7:8], EPS, None, ALU.add).then_inc(s[done], 1)
                g.wait_ge(s[done], 2 * n + 1)
                g.tensor_tensor(st[:, 9:10], st[:, 8:9], minus_half[:], ALU.pow).then_inc(s[done], 1)

            def iteration(a=None, b=None, c=None):
                if a is not None:
                    rstd(st1, "a_var", "a_rstd", a)
                if c is not None:
                    g.wait_ge(s["c_row1"], c + 1)
                    hold(g, "pool", s["c_weight"], c + 1)
                    for k, row in enumerate((row0, row1)):
                        g.indirect_dma_start(routed[:, :], bass.IndirectOffsetOnAxis(ap=slot[:, k:k + 1], axis=0),
                                             row[:, :], None).then_inc(s["c_scatter"], 16)
                if a is not None:
                    rstd(st2, "b_var", "b_rstd", a)
                    xa = xall[:, bass.ds(a, 1), :].rearrange("p a d -> p (a d)")
                    g.wait_ge(s["b_xn"], a + 1)
                    g.wait_ge(bo_done, 1)
                    g.tensor_tensor(xa, xa, bo_all[:], ALU.add).then_inc(s["b_xb"], 1)
                if b is not None:
                    rstd(st3, "c_var", "c_rstd", b)
                    wait(g, s["c_scatter"], 32 * b)
                    hold(g, "pool", s["c_xn"], b + 1)
                    g.tensor_copy(row1[:, 0:D], row0[:, 0:D]).then_inc(s["c_row1"], 1)

            pipeline(g, iteration)

            g.wait_ge(s["m_gb"], 32)
            g.wait_ge(s["b_x2"], BLK)
            g.wait_ge(s["c_xn"], BLK)
            g.tensor_tensor(xall[:], xall[:], beta_all.unsqueeze(1).broadcast_to((P, BLK, D)), ALU.add)\
                .then_inc(s["m_bx"], 1)

            def scatter_results(t):
                g.wait_ge(s["f_row"], t + 1)
                hold(g, "pool", s["f_yw"], t + 1)
                g.indirect_dma_start(expert_out[:, :], bass.IndirectOffsetOnAxis(ap=target_row[:], axis=0),
                                     yw, None, bounds_check=2 * TOK - 1, oob_is_err=False).then_inc(s["f_out"], 16)
            with g.Fori(0, TILES) as t:
                scatter_results(t)

            for n in range(BLK):
                g.wait_ge(s[f"y_pair{n // YG % 2}"], 16 * (n // YG // 2 + 1))
                y = ypair[n // YG % 2][:, n % YG]
                g.tensor_tensor(y[:, 0, :], y[:, 0, :], y[:, 1, :], ALU.add).then_inc(s["y_sum"], 1)
                rstd(st1 if n % 2 else st2, "y_var", "y_rstd", n)

        @block.scalar
        def _(act):
            def bv_columns():
                act.wait_ge(ld_small, N_SMALL)
                act.activation(zT[:], bvT[:].unsqueeze(2).broadcast_to((P, HP, P)), ACT.Copy).then_inc(bvrep_done, 1)

            def iteration(a=None, b=None, c=None):
                if a is not None:
                    act.wait_ge(s["a_kv_ps"], a + 1)
                    kv = bank[1][:, 256:256 + BB * KM * 2 * XD].rearrange("p (c e) -> p c e", e=2 * XD)
                    act.activation(kvr[:].rearrange("p b k r d -> p (b k) r d"),
                                   kv[:, :, 0:XD].unsqueeze(2).broadcast_to((P, BB * KM, P // XD, XD)), ACT.Copy)
                    act.activation(kvv[:].rearrange("p b k d -> p (b k) d"), kv[:, :, XD:], ACT.Copy).then_inc(s["a_kv"], 1)
                if b is not None:
                    act.wait_ge(s["b_xT_ps"], b + 1)
                    act.activation(x2T[:], bank[6][:, 0:D], ACT.Copy).then_inc(s["b_xT"], 1)
                if c is not None:
                    act.wait_ge(s["c_xT_ps"], c + 1)
                if a is not None:
                    act.wait_ge(s["a_xT_ps"], a + 1)
                    act.activation(xT[:], bank[0][:, 0:D], ACT.Copy).then_inc(s["a_xT"], 1)
                if c is not None:
                    act.activation(x3T[:], bank[0][:, D:2 * D], ACT.Copy).then_inc(s["c_xT"], 1)
                    act.wait_ge(s["c_lg_ps"], c + 1)
                if a is not None:
                    act.wait_ge(s["a_qpT_ps"], a + 1)
                    act.activation(qpT[:], bank[1][:, 0:D], ACT.Copy).then_inc(s["a_qpT"], 1)
                if c is not None:
                    act.activation(lgr[:], bank[1][:, 384:384 + E], ACT.Copy).then_inc(s["c_lg"], 1)
                if a is not None:
                    act.wait_ge(s["a_sc_ps"], a + 1)
                    act.activation(sc[:], bank[0][:, 0:M], ACT.Copy).then_inc(s["a_sc"], 1)
                    act.wait_ge(s["a_ohT_ps"], a + 1)
                    act.activation(ohT[:], bank[0][:, 0:M], ACT.Copy).then_inc(s["a_ohT"], 1)

                def values(j):
                    act.wait_ge(s["b_v_ps"], 2 * b + j + 1)
                    act.activation(vs[:, j * H // 2:(j + 1) * H // 2, 0:A],
                                   bank[6 + j][:].rearrange("p (h a) -> p h a", a=A), ACT.Copy).then_inc(s["b_v"], 1)
                if b is not None:
                    values(0)
                if c is not None:
                    act.wait_ge(s["c_d"], c + 1)
                    act.activation(rsc[:, 1:2], rsc[:, 0:1], ACT.Exp).then_inc(s["c_exp"], 1)
                if b is not None:
                    act.wait_ge(s["b_as"], b + 1)
                    for i in range(BB):
                        act.activation(aprob[i * S:(i + 1) * S, :, i * S:(i + 1) * S], as_[i * S:(i + 1) * S], ACT.Exp,
                                       scale=float(A) ** -0.5).then_inc(s["b_prob"], 1)
                    values(1)
                    for q in (1, 3):
                        act.wait_ge(s["b_pT_ps"], 4 * b + q + 1)
                        act.activation(apT[:, 4 * q:4 * q + 4, :], bank[5][:], ACT.Copy).then_inc(s["b_pT_s"], 1)
                if a is not None:
                    act.wait_ge(s["a_xs"], a + 1)
                    for i in range(BB):
                        act.activation(xprob[i * S:(i + 1) * S, :, i * S:(i + 1) * S], xs[i * S:(i + 1) * S], ACT.Exp,
                                       scale=float(XD) ** -0.5).then_inc(s["a_prob"], 1)
                    for q in (1, 3):
                        act.wait_ge(s["a_pT_ps"], 4 * a + q + 1)
                        act.activation(xpT[:, 4 * q:4 * q + 4, :], bank[3][:], ACT.Copy).then_inc(s["a_pT_s"], 1)
                if b is not None:
                    for j in range(2):
                        act.wait_ge(s["b_zT_ps"], 2 * b + j + 1)
                        act.activation(zT[:, 4 * j:4 * j + 4, :], bank[6 + j][:], ACT.Copy).then_inc(s["b_zT"], 1)
                if a is not None:
                    act.wait_ge(s["a_aoT_ps"], a + 1)
                    act.activation(aoT[:], bank[1][:, 0:D], ACT.Copy).then_inc(s["a_aoT"], 1)

            bv_columns()
            pipeline(act, iteration)

            def hidden_out(t):
                act.wait_ge(s["f_h_ps"], 2 * t + 1)
                act.activation(hs[:, 0:512], bank[2][:], ACT.Copy).then_inc(s["f_hs_s"], 1)

            def hidden_relu(t):
                e = act.value_load(tile_ei[0:1, bass.ds(t, 1)], min_val=0, max_val=E - 1)
                act.wait_ge(s["f_hT_ps"], 2 * t + 1)
                for c in range(4):
                    i = act.activation(hT[:, c, :], bank[4][:, c * P:(c + 1) * P], ACT.Relu,
                                       bias=b1T[:, bass.ds(e * KF + c, 1)])
                i.then_inc(s["f_hT_s"], 1)

            def weigh(t):
                act.wait_ge(s["f_yb"], t + 1)
                wait(act, s["f_out"], 16 * t)
                act.activation(yw, yb, ACT.Copy, scale=meta[:, bass.ds(t, 1), 0]).then_inc(s["f_yw"], 1)

            act.wait_ge(s["m_plan"], 1)
            hidden_out(0)
            hidden_relu(0)
            hidden_out(1)
            weigh(0)
            hidden_relu(1)
            with act.Fori(2, TILES) as t:
                hidden_out(t)
                weigh(t - 1)
                hidden_relu(t)
            weigh(LAST)

        @block.vector
        def _(v):
            va, vb, vc = Steps(v, a_dve, 8), Steps(v, b_dve, 6), Steps(v, c_dve, 14)

            def xblk(n):
                return xall[:, bass.ds(n, 1), :].rearrange("p a d -> p (a d)")

            def norm(steps, n, src, st, var, rstd, dst, xn_sem):
                steps.did(v.bn_stats(st[:, 0:6], src))
                steps.hold_last(passed_by["dve"])
                v.bn_aggr(st[:, 6:8], st[:, 0:6]).then_inc(s[var], 1)
                v.wait_ge(s[rstd], 2 * n + 2)
                v.tensor_scalar(dst, src, st[:, 6:7], st[:, 9:10], ALU.subtract, ALU.mult).then_inc(s[xn_sem], 1)

            def softmax_shift(steps, n, parts, mx, dst, done):
                hh = H // len(parts)
                for j, part in enumerate(parts):
                    steps.did(v.tensor_reduce(mx[:, j * hh:(j + 1) * hh], part, AX_X, ALU.max))
                steps.wait_last()
                for j, part in enumerate(parts):
                    i = v.tensor_tensor(dst[:, j * hh:(j + 1) * hh, :], part,
                                        mx[:, j * hh:(j + 1) * hh].unsqueeze(2).broadcast_to((P, hh, S)), ALU.subtract)
                    if j == len(parts) - 1:
                        i.then_inc(s[done], 1)

            def argmax(n):
                hold(v, "dve", s["a_sc"], n + 1)
                va.did(v.max(mx8[:], sc[:]))
                va.hold_last(passed_by["dve"])
                va.did(v.max_index(ix8[:], mx8[:], sc[:]))
                va.wait_last()
                va.did(v.tensor_copy(mx8[:, 0:1], ix8[:, 0:1]))
                va.wait_last()
                v.tensor_scalar(onehot[:], iota_m[:], mx8[:, 0:1], None, ALU.is_equal).then_inc(s["a_onehot"], 1)

            def memory(n):
                v.wait_ge(s["a_mem_ps"], n + 1)
                for b in range(BB):
                    v.tensor_tensor(mkb[:, b], bank[1][:, b * S:(b + 1) * S].unsqueeze(1).broadcast_to((P, P // XD, S)),
                                    headmask[:].unsqueeze(2).broadcast_to((P, P // XD, S)), ALU.mult)
                v.tensor_copy(mvb[:, 0:XD], bank[1][:, 128:128 + XD]).then_inc(s["a_mkb"], 1)

            def project(n, c):
                v.wait_ge(s["b_q_ps"], 4 * n + c + 1)
                dst, bias = ((qT, bqT), (kT, bkT))[c // 2]
                hp = slice(4 * (c % 2), 4 * (c % 2) + 4)
                v.tensor_tensor(dst[:, hp, :], bank[6 + c % 2][:].rearrange("p (h t) -> p h t", t=P),
                                bias[:, hp].unsqueeze(2).broadcast_to((P, 4, P)), ALU.add).then_inc(s["b_q"], 1)

            def masked(n):
                v.wait_ge(s["b_s_ps"], n + 1)
                for j in range(2):
                    i = v.tensor_tensor(as_[:, 8 * j:8 * j + 8, :], bank[4 + j][:].rearrange("p (h t) -> p h t", t=S),
                                        causal[:].unsqueeze(1).broadcast_to((P, 8, S)), ALU.min)
                i.then_inc(s["b_mask"], 1)
                v.wait_ge(s["b_mask"], n + 1)

            def route_weights(n):
                vc.begin(n)
                v.wait_ge(s["c_lg"], n + 1)
                vc.did(v.tensor_tensor(lg[:], lgr[:], br_all[:], ALU.add))
                vc.hold_last(passed_by["dve"])
                vc.did(v.max(rv8[:], lg[:]))
                vc.hold_last(passed_by["dve"])
                v.tensor_tensor(rsc[:, 0:1], rv8[:, 1:2], rv8[:, 0:1], ALU.subtract).then_inc(s["c_d"], 1)
                vc.did(v.max_index(ri8[:], rv8[:], lg[:]))
                vc.wait_last()
                vc.did(v.tensor_copy(rsc[:, 4:6], ri8[:, 0:2]))
                vc.wait_last()
                vc.did(v.tensor_scalar(oh0[:], iota_e[:], rsc[:, 4:5], None, ALU.is_equal))
                vc.did(v.tensor_scalar(oh1[:], iota_e[:], rsc[:, 5:6], None, ALU.is_equal))
                vc.wait_last()
                v.tensor_tensor(ohs[:], oh0[:], oh1[:], ALU.add).then_inc(s["c_ohs"], 1)

            def route_rows(n):
                v.wait_ge(s["c_exp"], n + 1)
                v.wait_ge(s["c_row1"], n + 1)
                vc.did(v.tensor_scalar(rsc[:, 2:3], rsc[:, 1:2], 1.0, None, ALU.add))
                vc.wait_last()
                vc.did(v.reciprocal(row0[:, D:D + 1], rsc[:, 2:3]))
                vc.wait_last()
                v.tensor_tensor(row1[:, D:D + 1], rsc[:, 1:2], row0[:, D:D + 1], ALU.mult)
                v.tensor_copy(row0[:, D + 1:D + 2], dest[:, bass.ds(n, 1), 0])
                v.tensor_copy(row1[:, D + 1:D + 2], dest[:, bass.ds(n, 1), 1])
                v.wait_ge(s["c_pos_ps"], n + 1)
                vc.did(v.tensor_tensor(pos[:], bank[0][:, 272:272 + E], run[:], ALU.add))
                vc.wait_last()
                v.tensor_tensor(run[:], run[:], bank[0][:, 288:288 + E], ALU.add).then_inc(s["c_pos"], 1)
                vc.did(v.tensor_tensor(pos[:], pos[:], region[:], ALU.add))
                vc.wait_last()
                for k, oh in enumerate((oh0, oh1)):
                    vc.did(v.tensor_tensor(rtmp[:], pos[:], oh[:], ALU.mult))
                    vc.wait_last()
                    vc.did(v.tensor_reduce(rsc[:, 6 + k:7 + k], rtmp[:], AX_X, ALU.add))
                    vc.wait_last()
                v.tensor_copy(slot[:], rsc[:, 6:8]).then_inc(s["c_weight"], 1)

            def iteration(a=None, b=None, c=None):
                if a is not None:
                    va.begin(a)
                    norm(va, a, xblk(a), st1, "a_var", "a_rstd", xn[:], "a_xn")
                if b is not None:
                    for q in range(3):
                        project(b, q)
                if a is not None:
                    argmax(a)
                if b is not None:
                    project(b, 3)
                if a is not None:
                    memory(a)
                if c is not None:
                    route_weights(c)
                if b is not None:
                    vb.begin(b)
                    masked(b)
                    softmax_shift(vb, b, [as_[:]], bmx, as_, "b_as")
                if a is not None:
                    v.wait_ge(s["a_log_ps"], a + 1)
                    softmax_shift(va, a, [bank[2 + j][:].rearrange("p (h m) -> p h m", m=S) for j in range(2)], amx, xs, "a_xs")
                if c is not None:
                    route_rows(c)
                if b is not None:
                    for q in (0, 2):
                        v.wait_ge(s["b_pT_ps"], 4 * b + q + 1)
                        v.tensor_copy(apT[:, 4 * q:4 * q + 4, :], bank[4][:]).then_inc(s["b_pT_v"], 1)
                    for q in range(4):
                        v.wait_ge(s["b_av_ps"], 4 * b + q + 1)
                        av = bank[6 + q % 2][:, 0:4 * (A + 1)].rearrange("p (h e) -> p h e", e=A + 1)
                        vb.did(v.reciprocal(brc[:, 4 * q:4 * q + 4].unsqueeze(2), av[:, :, A:A + 1]))
                        vb.wait_last()
                        v.tensor_tensor(z[:, 4 * q:4 * q + 4, :], av[:, :, 0:A],
                                        brc[:, 4 * q:4 * q + 4].unsqueeze(2).broadcast_to((P, 4, A)), ALU.mult)\
                            .then_inc(s["b_z"], 1)
                if a is not None:
                    for q in (0, 2):
                        v.wait_ge(s["a_pT_ps"], 4 * a + q + 1)
                        v.tensor_copy(xpT[:, 4 * q:4 * q + 4, :], bank[2][:]).then_inc(s["a_pT_v"], 1)
                    v.wait_ge(s["a_av_ps"], a + 1)
                    av = bank[0][:, 0:H * (XD + 1)].rearrange("p (h e) -> p h e", e=XD + 1)
                    va.did(v.reciprocal(arc[:].unsqueeze(2), av[:, :, XD:XD + 1]))
                    va.wait_last()
                    v.tensor_tensor(ao[:], av[:, :, 0:XD], arc[:].unsqueeze(2).broadcast_to((P, H, XD)), ALU.mult)\
                        .then_inc(s["a_ao"], 1)
                    v.wait_ge(s["a_wc_ps"], a + 1)
                    v.tensor_tensor(xblk(a), xblk(a), bank[0][:, 0:D], ALU.add).then_inc(s["a_x1"], 1)
                    hold(v, "dve", s["a_x1"], a + 1)
                    norm(va, a, xblk(a), st2, "b_var", "b_rstd", xn2[:], "b_xn")
                if b is not None:
                    v.wait_ge(s["b_o_ps"], b + 1)
                    v.wait_ge(s["b_xb"], b + 1)
                    v.tensor_tensor(xblk(b), xblk(b), bank[6][:, 0:D], ALU.add).then_inc(s["b_x2"], 1)
                    hold(v, "dve", s["b_x2"], b + 1)
                    vb.did(v.bn_stats(st3[:, 0:6], xblk(b)))
                    vb.hold_last(passed_by["dve"])
                    v.bn_aggr(st3[:, 6:8], st3[:, 0:6]).then_inc(s["c_var"], 1)
                    wait(v, s["c_scatter"], 32 * b)
                    wait(v, s["c_target"], 16 * b)
                    v.wait_ge(s["c_rstd"], 2 * b + 2)
                    v.tensor_scalar(row0[:, 0:D], xblk(b), st3[:, 6:7], st3[:, 9:10], ALU.subtract, ALU.mult).then_inc(s["c_xn"], 1)

            v.wait_ge(k_pool, K_POOL)
            v.wait_ge(ld_x, 32)
            v.wait_ge(ld_small, N_SMALL)
            v.wait_ge(bo_ps, 1)
            v.tensor_tensor(bo_all[:], bo_all[:], bank[7][:, 0:D], ALU.add).then_inc(bo_done, 1)
            pipeline(v, iteration)
            for st in (va, vb, vc):
                st.end()

            vm = Steps(v, m_dve, 18)
            vm.begin(0)

            def step(ins):
                vm.did(ins)
                vm.wait_last()
            step(v.tensor_tensor(cum2[:], run[:], region[:], ALU.add))
            step(v.tensor_copy(padrow_i[:], cum2[:]))
            step(v.tensor_scalar(tiles_i[:], run[:], float(P - 1), None, ALU.add))
            step(v.tensor_scalar(tiles_i[:], tiles_i[:], P.bit_length() - 1, None, ALU.arith_shift_right))
            step(v.tensor_copy(tiles[:], tiles_i[:]))
            step(v.tensor_copy(cum[:], tiles[:]))
            for e in range(1, E):
                step(v.tensor_tensor(cum[:, e:e + 1], cum[:, e:e + 1], cum[:, e - 1:e], ALU.add))
            over = (P, TILES, E - 1)
            step(v.tensor_tensor(passed, iota_t[:].unsqueeze(2).broadcast_to(over),
                                 cum[:, 0:E - 1].unsqueeze(1).broadcast_to(over), ALU.is_ge))
            vm.did(v.tensor_reduce(tile_e[:], passed, AX_X, ALU.add))
            step(v.tensor_tensor(passed_tiles, passed, tiles[:, 0:E - 1].unsqueeze(1).broadcast_to(over), ALU.mult))
            step(v.tensor_reduce(tile_s[:], passed_tiles, AX_X, ALU.add))
            step(v.tensor_tensor(tile_s[:], iota_t[:], tile_s[:], ALU.subtract))
            v.tensor_scalar(tile_idle[:], iota_t[:], cum[:, E - 1:E], float(2 * E * REG), ALU.is_ge, ALU.mult)
            v.tensor_scalar(passed[:, :, 0], tile_s[:], float(P), None, ALU.mult)
            v.tensor_copy(tile_ei[:], tile_e[:]).then_inc(s["m_hist"], 1)
            v.wait_ge(s["m_hist"], 1)
            v.scalar_tensor_tensor(out=tile_s[:], in0=tile_e[:], scalar=float(REG), in1=passed[:, :, 0], op0=ALU.mult, op1=ALU.add)\
                .then_inc(s["m_hist"], 1)
            v.wait_ge(s["m_hist"], 2)
            v.tensor_tensor(tile_s[:], tile_s[:], tile_idle[:], ALU.add).then_inc(s["m_hist"], 1)
            v.wait_ge(s["m_hist"], 3)
            v.tensor_scalar(tile_ri[:], tile_s[:], float(E * REG), None, ALU.min).then_inc(s["m_plan"], 1)
            v.wait_ge(s["m_plan"], 1)
            vm.end()

            def tile_in(t):
                v.wait_ge(s["f_xg"], 16 * t + 16)
                v.tensor_copy(meta[:, bass.ds(t, 1), :], xg[:, D:D + 2]).then_inc(s["f_meta"], 1)
                v.wait_ge(s["f_xT_ps"], t + 1)
                v.tensor_copy(xgT, bank[0][:, 0:D].rearrange("p (k t) -> p k t", t=P)).then_inc(s["f_xT"], 1)

            def hidden_out(t):
                v.wait_ge(s["f_h_ps"], 2 * t + 2)
                v.tensor_copy(hs[:, 512:1024], bank[3][:]).then_inc(s["f_hs_v"], 1)

            def hidden_relu(t):
                e = v.value_load(tile_ei[0:1, bass.ds(t, 1)], min_val=0, max_val=E - 1)
                v.wait_ge(s["f_hT_ps"], 2 * t + 2)
                for c in range(4):
                    i = v.tensor_scalar(hT[:, 4 + c, :], bank[5][:, c * P:(c + 1) * P],
                                        b1T[:, bass.ds(e * KF + 4 + c, 1)], 0.0, ALU.add, ALU.max)
                i.then_inc(s["f_hT_v"], 1)

            def result_out(t):
                e = v.value_load(tile_ei[0:1, bass.ds(t, 1)], min_val=0, max_val=E - 1)
                v.wait_ge(s["f_o_ps"], t + 1)
                wait(v, s["f_yw"], t)
                v.tensor_tensor(yb, bank[6][:, 0:D], b2_all[:, bass.ds(e * D, D)], ALU.add).then_inc(s["f_yb"], 1)
                wait(v, s["f_out"], 16 * t)
                v.tensor_copy(target_row[:], meta[:, bass.ds(t, 1), 1]).then_inc(s["f_row"], 1)

            tile_in(0)
            hidden_out(0)
            tile_in(1)
            hidden_relu(0)
            hidden_out(1)
            tile_in(2)
            result_out(0)
            hidden_relu(1)
            with v.Fori(2, LAST) as t:
                hidden_out(t)
                tile_in(t + 1)
                result_out(t - 1)
                hidden_relu(t)
            hidden_out(LAST)
            result_out(LAST - 1)
            hidden_relu(LAST)
            result_out(LAST)

            vy = Steps(v, y_dve, 3)
            v.wait_ge(s["m_tgt"], 32)
            v.wait_ge(s["m_gb"], 32)
            v.wait_ge(s["m_bx"], 1)
            for n in range(BLK):
                vy.begin(n)
                st = st1 if n % 2 else st2
                y = ypair[n // YG % 2][:, n % YG]
                v.wait_ge(s["y_sum"], n + 1)
                vy.did(v.tensor_tensor(y[:, 0, :], y[:, 0, :], tgt[n // (BLK // 2)][:, n % (BLK // 2), :], ALU.add))
                vy.wait_last()
                vy.did(v.bn_stats(st[:, 0:6], y[:, 0, :]))
                vy.wait_last()
                v.bn_aggr(st[:, 6:8], st[:, 0:6]).then_inc(s["y_var"], 1)
                v.wait_ge(s["y_var"], n + 1)
                vy.did(v.scalar_tensor_tensor(out=y[:, 1, :], in0=y[:, 0, :], scalar=st[:, 6:7], in1=gamma_all,
                                              op0=ALU.subtract, op1=ALU.mult))
                vy.wait_last()
                v.wait_ge(s["y_rstd"], 2 * n + 2)
                v.scalar_tensor_tensor(out=xall[:, n, :], in0=y[:, 1, :], scalar=st[:, 9:10], in1=xall[:, n, :],
                                       op0=ALU.mult, op1=ALU.add).then_inc(s["y_out"], 1)
            vy.end()

        @block.tensor
        def _(pe):
            mm = nc.tensor.matmul
            tr = nc.tensor.transpose

            def bo_through_values():
                pe.wait_ge(bvrep_done, 1)
                for c in range(HP):
                    i = mm(bank[7][:, 0:D], zT[:, c, :], awo[:, c, :], start=c == 0, stop=c == HP - 1)
                i.then_inc(bo_ps, 1)

            def place(h):
                return h % 2 * (H // 2) + h // 2

            def context(n):
                pe.wait_ge(ld_ctx, 16 * n + 16)
                wait(pe, s["a_aoT"], n)
                for b in range(BB):
                    for m in range(KM):
                        c = 256 + (b * KM + m) * 2 * XD
                        for k in range(KD):
                            i = mm(bank[1][:, c:c + 2 * XD], ctxb[:, b, k, m * P:(m + 1) * P], xwkv[:, k, :],
                                   start=k == 0, stop=k == KD - 1)
                i.then_inc(s["a_kv_ps"], 1)

            def turn(a, c):
                if a is not None:
                    wait(pe, s["a_x1"], a)
                if c is not None:
                    wait(pe, s["c_pos"], c)
                    pe.wait_ge(s["c_xn"], c + 1)
                    for k in range(KD):
                        i = tr(bank[0][:, D + k * P:D + (k + 1) * P], row0[:, k * P:(k + 1) * P], ident[:])
                    i.then_inc(s["c_xT_ps"], 1)
                if a is not None:
                    pe.wait_ge(s["a_xn"], a + 1)
                    for k in range(KD):
                        i = tr(bank[0][:, k * P:(k + 1) * P], xn[:, k * P:(k + 1) * P], ident[:])
                    i.then_inc(s["a_xT_ps"], 1)

            def queries(a, c):
                if a is not None:
                    pe.wait_ge(s["a_xT"], a + 1)
                    pe.wait_ge(s["a_kv"], a + 1)
                if c is not None:
                    pe.wait_ge(s["c_xT"], c + 1)
                    for k in range(KD):
                        i = mm(bank[1][:, 384:384 + E], x3T[:, k, :], wr[:, k, :], start=k == 0, stop=k == KD - 1)
                    i.then_inc(s["c_lg_ps"], 1)
                if a is not None:
                    for e in range(KD):
                        for k in range(KD):
                            i = mm(bank[1][:, e * P:(e + 1) * P], xwq[:, k, e * P:(e + 1) * P], xT[:, k, :],
                                   start=k == 0, stop=k == KD - 1)
                    i.then_inc(s["a_qpT_ps"], 1)

            def context_scores(n):
                pe.wait_ge(s["a_qpT"], n + 1)
                for b in range(BB):
                    for k in range(KD):
                        i = mm(bank[0][b * S:(b + 1) * S, 0:M], qpT[:, k, b * S:(b + 1) * S], ctxb[:, b, k, :],
                               start=k == 0, stop=k == KD - 1)
                i.then_inc(s["a_sc_ps"], 1)

            def onehot_turn(n):
                pe.wait_ge(s["a_onehot"], n + 1)
                for k in range(KM):
                    i = tr(bank[0][:, k * P:(k + 1) * P], onehot[:, k * P:(k + 1) * P], ident[:])
                i.then_inc(s["a_ohT_ps"], 1)

            def gather(a, c):
                pe.wait_ge(s["a_ohT"], a + 1)
                if c is not None:
                    pe.wait_ge(s["c_lg"], c + 1)
                for b in range(BB):
                    for k in range(KM):
                        mm(bank[1][:, b * S:(b + 1) * S], kvr[:, b, k].rearrange("p r d -> p (r d)"), ohT[:, k, b * S:(b + 1) * S],
                           start=k == 0, stop=k == KM - 1)
                for b in range(BB):
                    for k in range(KM):
                        i = mm(bank[1][b * S:(b + 1) * S, 128:128 + XD], ohT[:, k, b * S:(b + 1) * S], kvv[:, b, k, :],
                               start=k == 0, stop=k == KM - 1)
                i.then_inc(s["a_mem_ps"], 1)

            def cross_scores(n):
                pe.wait_ge(s["a_mkb"], n + 1)
                for b in range(BB):
                    for e in range(KD):
                        i = mm(bank[2 + e][b * S:(b + 1) * S, :], qpT[:, e, b * S:(b + 1) * S],
                               mkb[:, b].rearrange("p h m -> p (h m)"), start=True, stop=True)
                i.then_inc(s["a_log_ps"], 1)

            def cross_turn(n):
                pe.wait_ge(s["a_prob"], 2 * n + 2)
                for q in range(4):
                    if q == 2:
                        pe.wait_ge(s["a_pT_v"], 2 * n + 1)
                    if q == 3:
                        pe.wait_ge(s["a_pT_s"], 2 * n + 1)
                    for h in range(4):
                        i = tr(bank[2 + q % 2][:, h * P:(h + 1) * P], xprob[:, 4 * q + h, :], ident[:])
                    i.then_inc(s["a_pT_ps"], 1)

            def cross_values(a, c):
                pe.wait_ge(s["a_pT_v"], 2 * a + 2)
                pe.wait_ge(s["a_pT_s"], 2 * a + 2)
                if c is not None:
                    pe.wait_ge(s["c_pos"], c + 1)
                for h in range(H):
                    i = mm(bank[0][:, h * (XD + 1):(h + 1) * (XD + 1)], xpT[:, h, :], mvb[:], start=True, stop=True)
                i.then_inc(s["a_av_ps"], 1)

            def cross_out_turn(n):
                pe.wait_ge(s["a_ao"], n + 1)
                for k in range(KD):
                    i = tr(bank[1][:, k * P:(k + 1) * P], ao[:].rearrange("p h e -> p (h e)")[:, k * P:(k + 1) * P], ident[:])
                i.then_inc(s["a_aoT_ps"], 1)

            def cross_out(n):
                pe.wait_ge(s["a_aoT"], n + 1)
                for k in range(KD):
                    i = mm(bank[0][:, 0:D], aoT[:, k, :], xwc[:, k, :], start=k == 0, stop=k == KD - 1)
                i.then_inc(s["a_wc_ps"], 1)

            def self_turn(n):
                pe.wait_ge(s["b_xn"], n + 1)
                wait(pe, s["b_x2"], n)
                for k in range(KD):
                    i = tr(bank[6][:, k * P:(k + 1) * P], xn2[:, k * P:(k + 1) * P], ident[:])
                i.then_inc(s["b_xT_ps"], 1)

            def project(n, c):
                if c == 0:
                    pe.wait_ge(s["b_xT"], n + 1)
                if c >= 2:
                    pe.wait_ge(s["b_q"], 4 * n + c - 1)
                w = (awq, awk)[c // 2]
                for j in range(4):
                    f = (4 * (c % 2) + j) * P
                    for k in range(KD):
                        i = mm(bank[6 + c % 2][:, j * P:(j + 1) * P], w[:, k, f:f + P], x2T[:, k, :],
                               start=k == 0, stop=k == KD - 1)
                i.then_inc(s["b_q_ps"], 1)

            def values(n, j):
                pe.wait_ge(s["b_q"], 4 * n + 3 + j)
                for k in range(KD):
                    i = mm(bank[6 + j][:], x2T[:, k, :], awv[:, k, j * 512:(j + 1) * 512], start=k == 0, stop=k == KD - 1)
                i.then_inc(s["b_v_ps"], 1)

            def self_scores(n):
                hold(pe, "pe", s["b_q"], 4 * n + 4)
                for h in range(H):
                    hp = slice(A * (h % 2), A * (h % 2) + A)
                    for b in range(BB):
                        i = mm(bank[4 + h % 2][b * S:(b + 1) * S, (h // 2) * S:(h // 2 + 1) * S],
                               qT[hp, h // 2, b * S:(b + 1) * S], kT[hp, h // 2, b * S:(b + 1) * S], start=True, stop=True)
                i.then_inc(s["b_s_ps"], 1)

            def self_turn_weights(n):
                pe.wait_ge(s["b_prob"], 2 * n + 2)
                for q in range(4):
                    if q == 2:
                        pe.wait_ge(s["b_pT_v"], 2 * n + 1)
                    if q == 3:
                        pe.wait_ge(s["b_pT_s"], 2 * n + 1)
                    for h in range(4):
                        i = tr(bank[4 + q % 2][:, h * P:(h + 1) * P], aprob[:, place(4 * q + h), :], ident[:])
                    i.then_inc(s["b_pT_ps"], 1)

            def self_values(n):
                pe.wait_ge(s["b_v"], 2 * n + 2)
                for q in range(4):
                    pe.wait_ge(s["b_pT_s" if q % 2 else "b_pT_v"], 2 * n + q // 2 + 1)
                    if q >= 2:
                        pe.wait_ge(s["b_z"], 4 * n + q - 1)
                    for h in range(4):
                        i = mm(bank[6 + q % 2][:, h * (A + 1):(h + 1) * (A + 1)], apT[:, 4 * q + h, :], vs[:, 4 * q + h, :],
                               start=True, stop=True)
                    i.then_inc(s["b_av_ps"], 1)

            def self_out_turn(n):
                for j in range(2):
                    pe.wait_ge(s["b_z"], 4 * n + 3 + j)
                    for c in range(4):
                        i = tr(bank[6 + j][:, c * P:(c + 1) * P],
                               z.rearrange("p h a -> p (h a)")[:, (4 * j + c) * P:(4 * j + c + 1) * P], ident[:])
                    i.then_inc(s["b_zT_ps"], 1)

            def self_out(n, j):
                pe.wait_ge(s["b_zT"], 2 * n + j + 1)
                for c in range(4 * j, 4 * j + 4):
                    i = mm(bank[6][:, 0:D], zT[:, c, :], awo[:, c, :], start=c == 0, stop=c == HP - 1)
                if j:
                    i.then_inc(s["b_o_ps"], 1)

            def count(n):
                pe.wait_ge(s["c_ohs"], n + 1)
                mm(bank[0][:, 272:272 + E], before[:], ohs[:], start=True, stop=True)
                mm(bank[0][:, 288:288 + E], ones[:], ohs[:], start=True, stop=True).then_inc(s["c_pos_ps"], 1)

            def iteration(a=None, b=None, c=None):
                A_, B_, C_ = a is not None, b is not None, c is not None
                if A_:
                    context(a)
                if B_:
                    self_turn(b)
                    project(b, 0)
                turn(a, c)
                if B_:
                    project(b, 1)
                queries(a, c)
                if B_:
                    project(b, 2)
                if A_:
                    context_scores(a)
                if B_:
                    project(b, 3)
                if A_:
                    onehot_turn(a)
                if B_:
                    values(b, 0)
                if A_:
                    gather(a, c)
                if B_:
                    self_scores(b)
                if A_:
                    cross_scores(a)
                if C_:
                    count(c)
                if B_:
                    values(b, 1)
                    self_turn_weights(b)
                    self_values(b)
                if A_:
                    cross_turn(a)
                    cross_values(a, c)
                if B_:
                    self_out_turn(b)
                if A_:
                    cross_out_turn(a)
                if B_:
                    self_out(b, 0)
                if A_:
                    cross_out(a)
                if B_:
                    self_out(b, 1)

            pe.wait_ge(k_pool, K_POOL)
            pe.wait_ge(ld_xw, 48)
            pe.wait_ge(ld_aw, 80)
            bo_through_values()
            pipeline(pe, iteration)

            def tile_in(t):
                pe.wait_ge(s["f_xg"], 16 * t + 16)
                wait(pe, s["f_xT"], t)
                for k in range(KD):
                    i = tr(bank[0][:, k * P:(k + 1) * P], xg[:, k * P:(k + 1) * P], ident[:])
                i.then_inc(s["f_xT_ps"], 1)

            def up(t):
                e = pe.value_load(tile_ei[0:1, bass.ds(t, 1)], min_val=0, max_val=E - 1)
                pe.wait_ge(s["f_xT"], t + 1)
                for j in range(FH):
                    wait(pe, s["f_hs_v" if j else "f_hs_s"], t)
                    for k in range(KD):
                        i = mm(bank[2 + j][:], xgT[:, k, :], w1[:, bass.ds(e, 1), k, j * 512:(j + 1) * 512],
                               start=k == 0, stop=k == KD - 1)
                    i.then_inc(s["f_h_ps"], 1)

            def hidden_turn(t):
                for j in range(FH):
                    pe.wait_ge(s["f_hs_v" if j else "f_hs_s"], t + 1)
                    wait(pe, s["f_hT_v" if j else "f_hT_s"], t)
                    for c in range(4):
                        i = tr(bank[4 + j][:, c * P:(c + 1) * P], hs[:, (4 * j + c) * P:(4 * j + c + 1) * P], ident[:])
                    i.then_inc(s["f_hT_ps"], 1)

            def down(t):
                e = pe.value_load(tile_ei[0:1, bass.ds(t, 1)], min_val=0, max_val=E - 1)
                wait(pe, s["f_yb"], t)
                for c in range(KF):
                    if c % 4 == 0:
                        pe.wait_ge(s["f_hT_v" if c else "f_hT_s"], t + 1)
                    i = mm(bank[6][:, 0:D], hT[:, c, :], w2[:, bass.ds(e, 1), c, :], start=c == 0, stop=c == KF - 1)
                i.then_inc(s["f_o_ps"], 1)

            pe.wait_ge(s["m_plan"], 1)
            pe.wait_ge(s["m_w1"], 16 * E)
            tile_in(0)
            up(0)
            tile_in(1)
            hidden_turn(0)
            pe.wait_ge(s["m_w2"], 16 * E)
            up(1)
            tile_in(2)
            down(0)
            hidden_turn(1)
            with pe.Fori(2, LAST) as t:
                up(t)
                tile_in(t + 1)
                down(t - 1)
                hidden_turn(t)
            up(LAST)
            down(LAST - 1)
            hidden_turn(LAST)
            down(LAST)


def kernel(**inputs):
    import numpy as np
    import concourse.bacc as bacc
    from concourse.bass_utils import run_bass_kernel_spmd

    def lay(a):
        return np.ascontiguousarray(a)

    g = {k: np.asarray(v) for k, v in inputs.items()}
    D = g["x"].shape[-1]
    arrays = {
        "x": lay(g["x"]),
        "ctxT": lay(g["ctx_1024"].transpose(0, 2, 1)),
        "xWqT": lay(g["L0_xattn_Wq"].T),
        "xWkvT": lay(g["L0_xattn_Wkv"].T),
        "xWcT": lay(g["L0_xattn_Wc"].T),
        "aWq": lay(g["L0_attn_Wq"].transpose(1, 0, 2).reshape(D, -1)),
        "aWk": lay(g["L0_attn_Wk"].transpose(1, 0, 2).reshape(D, -1)),
        "aWv": lay(g["L0_attn_Wv"].transpose(1, 0, 2).reshape(D, -1)),
        "aWo": lay(g["L0_attn_Wo"].reshape(-1, D)),
        "bq": lay(g["L0_attn_bq"].reshape(-1)),
        "bk": lay(g["L0_attn_bk"].reshape(-1)),
        "bv": lay(g["L0_attn_bv"].reshape(-1)),
        "bo": lay(g["L0_attn_bo"]),
        "WrT": lay(g["L0_ffn_Wr"].T),
        "br": lay(g["L0_ffn_br"]),
        "W1T": lay(g["L0_ffn_W1"].transpose(0, 2, 1)),
        "b1": lay(g["L0_ffn_b1"].reshape(-1)),
        "W2T": lay(g["L0_ffn_W2"].transpose(0, 2, 1)),
        "b2": lay(g["L0_ffn_b2"].reshape(-1)),
        "gamma": lay(g["L0_ffn_gamma"]),
        "beta": lay(g["L0_ffn_beta"]),
    }
    nc = bacc.Bacc("TRN2", target_bir_lowering=False, num_devices=1)
    aps = {k: nc.dram_tensor(k, a.shape, mybir.dt.from_np(a.dtype), kind="ExternalInput").ap() for k, a in arrays.items()}
    out = nc.dram_tensor("out", g["x"].shape, F32, kind="ExternalOutput").ap()
    perceiver_layer(nc, out=out, **aps)
    return run_bass_kernel_spmd(nc, [arrays], core_ids=[0]).results[0]["out"]
```

```python
from contextlib import ExitStack

import concourse.bass as bass
from concourse import mybir

F32 = mybir.dt.float32
I32 = mybir.dt.int32
U32 = mybir.dt.uint32
ALU = mybir.AluOpType
ACT = mybir.ActivationFunctionType
AX_X = mybir.AxisListType.X
P = 128


class Steps:

    def __init__(self, engine, sem, per_block):
        self.engine, self.sem, self.per_block = engine, sem, per_block

    def begin(self, n):
        self.base, self.count = n * self.per_block, 0

    def did(self, instruction):
        self.count += 1
        instruction.then_inc(self.sem, 1)

    def wait_last(self):
        self.engine.wait_ge(self.sem, self.base + self.count)

    def hold_last(self, beside):
        self.wait_last()
        if not isinstance(self.base, int):
            self.engine.sem_inc(beside, 1)

    def end(self):
        assert self.count == self.per_block, (self.sem, self.count)


def perceiver_layer(nc, x, ctxT, ctxR, xWqT, xWkvT, xWcT, aWq, aWk, aWv, aWo, bq, bk, bv, bo,
                    WrT, br, W1T, b1, W2T, b2, gamma, beta, out):
    NB, S, D = x.shape
    M = ctxT.shape[2]
    TOK = NB * S
    BLK = TOK // P
    BB = P // S
    KD = D // P
    KM = M // P
    H = 16
    XD = D // H
    HA = aWq.shape[1]
    A = HA // H
    HP = HA // P
    E = WrT.shape[1]
    F = W1T.shape[2]
    KF = F // P
    FH = F // 512
    ROW = D + 2
    REG = TOK + P
    TILES = 2 * TOK // P + E - 1
    EPS = 1e-5
    MASKED = -100000.0 * float(A) ** 0.5
    FAR = 1 << 24

    routed = nc.dram_tensor("routed", (E * REG + P, ROW), F32, kind="Internal").ap()
    target = nc.dram_tensor("target", (TOK, D), F32, kind="Internal").ap()
    expert_out = nc.dram_tensor("expert_out", (2 * TOK, D), F32, kind="Internal").ap()

    ctx = ExitStack()
    with ctx:
        def sb(name, shape, dt=F32):
            return ctx.enter_context(nc.sbuf_tensor(name, shape, dt))

        def sem(name):
            return ctx.enter_context(nc.semaphore(name))

        w1 = sb("w1", [P, E, KD, F])
        xall = sb("xall", [P, BLK, D])
        xwq, xwkv, xwc = sb("xwq", [P, KD, D]), sb("xwkv", [P, KD, 2 * XD]), sb("xwc", [P, KD, D])
        awq, awk, awv = (sb(n, [P, KD, HA]) for n in ("awq", "awk", "awv"))
        awo = sb("awo", [P, HP, D])
        bqT, bkT, bvT = (sb(n, [P, HP]) for n in ("bqT", "bkT", "bvT"))
        bo_all = sb("bo_all", [P, D])
        wr, br_all = sb("wr", [P, KD, E]), sb("br_all", [P, E])
        b1T = sb("b1T", [P, E * KF])
        b2_all = sb("b2_all", [P, E * D])
        gamma_all, beta_all = xwq[:, 0, :], xwq[:, 1, :]
        ident = sb("ident", [P, P])
        rowbase = sb("rowbase", [P, BLK])
        wk_rep = sb("wk_rep", [P, KD, P // XD, XD])
        iota_e = sb("iota_e", [P, E])
        region = sb("region", [P, E])
        causal = sb("causal", [P, S])
        headmask = sb("headmask", [P, P // XD])
        before = sb("before", [P, P])
        ones = sb("ones", [P, P])
        minus_half = sb("minus_half", [P, 1])
        dest = sb("dest", [P, BLK, 2])
        meta = sb("meta", [P, TILES, 2])
        target_row = sb("target_row", [P, 1], U32)
        row0, row1 = sb("row0", [P, ROW]), sb("row1", [P, ROW])
        x3T, lgr = sb("x3T", [P, KD, P]), sb("lgr", [P, E])
        ystat = sb("ystat", [P, 2, BLK // 4, 10])
        st1, st2, st3 = (sb(n, [P, 16]) for n in ("st1", "st2", "st3"))
        lg, rv8, ri8 = sb("lg", [P, E]), sb("rv8", [P, 8]), sb("ri8", [P, 8], U32)
        oh0, oh1, ohs, pos = (sb(n, [P, E]) for n in ("oh0", "oh1", "ohs", "pos"))
        run = sb("run", [P, E])
        rtmp, rsc = sb("rtmp", [P, E]), sb("rsc", [P, 8])
        slot = sb("slot", [P, 2], U32)
        pad = sb("pad", [P, ROW])
        iota_t = sb("iota_t", [P, TILES])
        tiles_i, tiles, cum, cum2 = sb("tiles_i", [P, E], I32), sb("tiles", [P, E]), sb("cum", [P, E]), sb("cum2", [P, E])
        padrow_i = sb("padrow_i", [P, E], I32)
        tile_e, tile_s, tile_idle = (sb(n, [P, TILES]) for n in ("tile_e", "tile_s", "tile_idle"))
        tile_ei, tile_ri = sb("tile_ei", [P, TILES], I32), sb("tile_ri", [P, TILES], I32)
        with nc.sbuf_tensor("w2", [P, E, KF, D], F32) as w2:
            pass
        ctxb = sb("ctxb", [P, BB, KD, M])
        xn, xT, qpT = sb("xn", [P, D]), sb("xT", [P, KD, P]), sb("qpT", [P, KD, P])
        sc = sb("sc", [P, M])
        mem, memT = sb("mem", [P, D]), sb("memT", [P, KD, P])
        mkb = sb("mkb", [P, BB, P // XD, S])
        mvw = sb("mvw", [P, BB, 6 * XD])
        xs = sb("xs", [P, H, S])
        xpT = sb("xpT", [P, HP, P])
        aoT = sb("aoT", [P, KD, P])
        mx8, ix8, gidx = sb("mx8", [P, 8]), sb("ix8", [P, 8], U32), sb("gidx", [P, 1], U32)
        amx, arc = sb("amx", [P, H]), sb("arc", [P, H])
        xn2, x2T = sb("xn2", [P, D]), sb("x2T", [P, KD, P])
        qT = sb("qT", [P, HP, P])
        vs = sb("vs", [P, H, A])
        as_ = sb("as_", [P, H, S])
        aprob = sb("aprob", [P, H, P])
        apT = sb("apT", [P, H, P])
        kT = sb("kT", [P, HP, P])
        zT = kT
        bmx, brc = sb("bmx", [P, H]), sb("brc", [P, H])
        hs, hT = awv[:, 0, :], awv[:, 1, :].rearrange("p (c t) -> p c t", t=P)
        spare = awo[:].rearrange("p c d -> p (c d)")
        passed, passed_tiles = (awv[:, j, 0:TILES * (E - 1)].rearrange("p (t e) -> p t e", e=E - 1) for j in range(2))
        xg, xgT = spare[:, 0:ROW], spare[:, 512:768].rearrange("p (k t) -> p k t", t=P)
        yb, yw = spare[:, 768:1024], spare[:, 1024:1280]
        YG = BLK // 4
        tgt = [w[:].rearrange("p k f -> p (k f)").rearrange("p (n d) -> p n d", d=D) for w in (awq, awk)]
        ypair = w1[:].rearrange("p e k f -> p (e k f)")[:, 0:2 * BLK * D].rearrange("p (n k d) -> p n k d", k=2, d=D)

        bank = [ctx.enter_context(nc.psum_tensor(f"bank{i}", [P, 512], F32)) for i in range(8)]

        ld_x, ld_ctx, ld_xw, ld_aw, ld_small = (sem(n) for n in ("ld_x", "ld_ctx", "ld_xw", "ld_aw", "ld_small"))
        ld_x0, xw_ready, ident_ready, ld_b12 = sem("ld_x0"), sem("xw_ready"), sem("ident_ready"), sem("ld_b12")
        bo_ps, bo_done, bvrep_done = sem("bo_ps"), sem("bo_done"), sem("bvrep_done")
        a_dve, m_dve, b_dve, c_dve, k_pool = (sem(n) for n in ("a_dve", "m_dve", "b_dve", "c_dve", "k_pool"))
        names_a = ("a_var", "a_rstd", "a_xn", "a_xT_ps", "a_xT", "a_qpT_ps", "a_qpT", "a_sc_ps", "a_sc", "a_idx", "a_mem",
                   "a_memT_ps", "a_memT", "a_mkv_ps", "a_mkb", "a_log_ps", "a_xs", "a_exp", "a_prob", "a_pT_ps",
                   "a_pT", "a_av_ps", "a_aoT", "a_wc_ps", "a_x1")
        names_b = ("b_var", "b_rstd", "b_xn", "b_xb", "b_xT_ps", "b_xT", "b_q_ps", "b_q", "b_v_ps", "b_v", "b_s_ps", "b_mask",
                   "b_as", "b_exp", "b_prob", "b_pT_ps", "b_pT", "b_av_ps", "b_zT_s", "b_zT_v", "b_o_ps", "b_x2")
        names_c = ("c_var", "c_rstd", "c_xn", "c_xT_ps", "c_xT", "c_lg_ps", "c_lg", "c_d", "c_exp", "c_ohs", "c_pos_ps", "c_pos",
                   "c_row1", "c_weight", "c_scatter", "c_target")
        names_m = ("m_hist", "m_plan", "m_pads", "m_w1", "m_w2", "m_tgt", "m_gb", "m_bx")
        names_f = ("f_xg", "f_meta", "f_xT_ps", "f_xT", "f_h_ps", "f_hs_s", "f_hs_v", "f_hT_ps", "f_hT_s", "f_hT_v",
                   "f_o_ps", "f_yb", "f_yw", "f_row", "f_out")
        names_y = ("y_pair0", "y_pair1", "y_pair2", "y_pair3", "y_sum", "y_var", "y_rstd", "y_out", "y_store")
        s = {n: sem(n) for n in names_a + names_b + names_c + names_m + names_f + names_y}
        passed_by = {e: sem(f"passed_by_{e}") for e in ("dve", "pool", "pe")}
        n_dve, p_dve, y_dve = sem("n_dve"), sem("p_dve"), sem("y_dve")
        LAST = TILES - 1
        K_POOL = 20
        N_SMALL = 5 * 16
        PT_BANK = (4, 5, 2, 3)
        block = ctx.enter_context(nc.Block())

        def wait(engine, semaphore, value):
            if not isinstance(value, int) or value > 0:
                engine.wait_ge(semaphore, value)

        def hold(engine, name, semaphore, value):
            if not isinstance(value, int):
                engine.wait_ge(semaphore, value)
                engine.sem_inc(passed_by[name], 1)
            else:
                wait(engine, semaphore, value)

        def following(a):
            return None if a is None or isinstance(a, int) and a + 1 == BLK else a + 1

        def pipeline(engine, iteration, between=None):
            iteration(a=0)
            iteration(a=1, m=0)
            if between is not None:
                between()
            iteration(a=2, m=1, b=0)
            with engine.Fori(3, BLK - 1) as n:
                iteration(a=n, m=n - 1, b=n - 2, c=n - 3)
            iteration(a=BLK - 1, m=BLK - 2, b=BLK - 3, c=BLK - 4)
            iteration(m=BLK - 1, b=BLK - 2, c=BLK - 3)
            iteration(b=BLK - 1, c=BLK - 2)
            iteration(c=BLK - 1)

        @block.sync
        def _(sp):
            def load_ctx(n):
                sp.dma_start(ctxb[:], ctxT[bass.ds(n * BB, BB)].rearrange("b (k p) m -> p b k m", p=P)).then_inc(ld_ctx, 16)

            def load_weights(pairs, loaded):
                for dst, src in pairs:
                    sp.dma_start(dst[:], src.rearrange("(k p) e -> p k e", p=P)).then_inc(loaded, 16)

            xv = x.rearrange("(n b) s d -> (b s) n d", b=BB)
            sp.dma_start(xall[:, 0:3, :], xv[:, 0:3, :]).then_inc(ld_x0, 16)
            load_weights(((xwq, xWqT), (xwkv, xWkvT)), ld_xw)
            load_ctx(0)
            load_weights(((xwc, xWcT),), ld_xw)
            with nc.allow_non_contiguous_dma(reason="small biases, once"):
                for dst, src in ((bqT, bq), (bkT, bk), (bvT, bv)):
                    sp.dma_start(dst[:], src.rearrange("(k p) -> p k", p=P)).then_inc(ld_small, 16)
            for dst, src in ((bo_all, bo), (br_all, br)):
                sp.dma_start(dst[:], src.partition_broadcast(P)).then_inc(ld_small, 16)

            def load_rest():
                sp.wait_ge(s["a_mem"], 16)
                load_weights(((awv, aWv), (awo, aWo), (awq, aWq), (awk, aWk), (wr, WrT)), ld_aw)
                sp.dma_start(xall[:, 3:BLK, :], xv[:, 3:BLK, :]).then_inc(ld_x, 16)
                with nc.allow_non_contiguous_dma(reason="small biases, once"):
                    sp.dma_start(b1T[:], b1.rearrange("(k p) -> p k", p=P)).then_inc(ld_b12, 16)
                sp.dma_start(b2_all[:], b2.partition_broadcast(P)).then_inc(ld_b12, 16)
                sp.wait_ge(k_pool, K_POOL)
                sp.dma_start(routed[E * REG:E * REG + P, :], pad[:]).then_inc(s["m_pads"], 16)

            def store_target(n):
                sp.wait_ge(s["c_xn"], n + 1)
                sp.dma_start(target[bass.ds(n * P, P), :], row0[:, 0:D]).then_inc(s["c_target"], 16)

            def iteration(a=None, m=None, b=None, c=None):
                if a is not None and (not isinstance(a, int) or a > 0):
                    sp.wait_ge(s["a_sc_ps"], a)
                    load_ctx(a)
                if c is not None:
                    store_target(c)
            iteration(a=0)
            iteration(a=1)
            load_rest()
            iteration(a=2)
            with sp.Fori(3, 3 + E) as n:
                iteration(a=n, c=n - 3)
                sp.dma_start(w1[:, bass.ds(n - 3, 1)].rearrange("p e k f -> p (e k) f"),
                             W1T[bass.ds(n - 3, 1)].rearrange("e (k p) f -> p (e k) f", p=P)).then_inc(s["m_w1"], 16)
            with sp.Fori(3 + E, BLK) as n:
                iteration(a=n, c=n - 3)
            def load_w2(e):
                if e:
                    sp.wait_ge(s["m_w2"], 16 * e)
                sp.dma_start(w2[:, e], W2T[e].rearrange("(k p) d -> p k d", p=P)).then_inc(s["m_w2"], 16)
            iteration(c=BLK - 3)
            sp.wait_ge(s["a_wc_ps"], BLK)
            load_w2(0)
            iteration(c=BLK - 2)
            load_w2(1)
            sp.wait_ge(s["b_xT_ps"], BLK)
            load_w2(2)
            for vector, dst in ((gamma, gamma_all), (beta, beta_all)):
                sp.dma_start(dst, vector.partition_broadcast(P)).then_inc(s["m_gb"], 16)
            sp.wait_ge(s["b_av_ps"], BLK)
            load_w2(3)
            iteration(c=BLK - 1)
            load_w2(4)
            sp.wait_ge(s["m_plan"], 1)
            for e in range(E):
                behind = sp.value_load(padrow_i[0:1, e:e + 1], min_val=e * REG, max_val=e * REG + TOK)
                sp.dma_start(routed[bass.ds(behind, P), :], pad[:]).then_inc(s["m_pads"], 16)
            load_w2(5)
            sp.wait_ge(s["m_pads"], 16 * (E + 1))
            sp.wait_ge(s["c_scatter"], 32 * BLK)

            def load_tile(t):
                first = sp.value_load(tile_ri[0:1, bass.ds(t, 1)], min_val=0, max_val=E * REG)
                sp.dma_start(xg, routed[bass.ds(first, P), :]).then_inc(s["f_xg"], 16)

            def next_tile(t):
                sp.wait_ge(s["f_xT_ps"], t)
                sp.wait_ge(s["f_meta"], t)
                load_tile(t)
            load_tile(0)
            for e in range(6, E):
                next_tile(e - 5)
                load_w2(e)
            sp.wait_ge(s["c_target"], 16 * BLK)
            for half in range(2):
                sp.dma_start(tgt[half], target[half * TOK // 2:(half + 1) * TOK // 2, :]
                             .rearrange("(n p) d -> p n d", p=P)).then_inc(s["m_tgt"], 16)
            with sp.Fori(E - 5, TILES) as t:
                next_tile(t)

            sp.wait_ge(s["f_out"], 16 * TILES)
            sp.wait_ge(s["f_yw"], TILES)
            pairs = expert_out.rearrange("(n p k) d -> p n k d", p=P, k=2)
            for g in range(BLK // YG):
                blocks = slice(g * YG, (g + 1) * YG)
                sp.dma_start(ypair[:, blocks], pairs[:, blocks]).then_inc(s[f"y_pair{g}"], 16)
            for g in range(BLK // YG):
                blocks = slice(g * YG, (g + 1) * YG)
                sp.wait_ge(s["y_out"], g + 1)
                sp.dma_start(out.rearrange("(n b) s d -> (b s) n d", b=BB)[:, blocks], xall[:, blocks]).then_inc(s["y_store"], 16)
            sp.wait_ge(s["y_store"], 16 * (BLK // YG))

        @block.gpsimd
        def _(g):
            cst = Steps(g, k_pool, K_POOL)
            cst.begin(0)

            def once(ins):
                cst.did(ins)
                cst.wait_last()
            once(g.memset(ident[:], 0.0))
            g.affine_select(out=ident[:], in_=ident[:], compare_op=ALU.not_equal, fill=1.0, base=0,
                            pattern=[[-1, P]], channel_multiplier=1).then_inc(ident_ready, 1)
            g.memset(minus_half[:], -0.5).then_inc(ident_ready, 1)
            for b in range(BB):
                once(g.iota(rowbase[b * S:(b + 1) * S, :], pattern=[[BB * M, BLK]], base=b * M, channel_multiplier=0,
                            allow_small_or_imprecise_dtypes=True))
            once(g.memset(headmask[:], 1.0))
            once(g.affine_select(out=headmask[:], in_=headmask[:], compare_op=ALU.is_ge, fill=0.0, base=0,
                                 pattern=[[-XD, P // XD]], channel_multiplier=1))
            once(g.affine_select(out=headmask[:], in_=headmask[:], compare_op=ALU.is_ge, fill=0.0, base=XD - 1,
                                 pattern=[[XD, P // XD]], channel_multiplier=-1))
            once(g.memset(mvw[:], 0.0))
            once(g.memset(causal[:], 3e38))
            for b in range(BB):
                once(g.affine_select(out=causal[b * S:(b + 1) * S, :], in_=causal[b * S:(b + 1) * S, :], compare_op=ALU.is_ge,
                                     fill=MASKED, base=0, pattern=[[-1, S]], channel_multiplier=1))
            once(g.memset(aprob[:], 0.0))
            once(g.iota(iota_e[:], pattern=[[1, E]], base=0, channel_multiplier=0, allow_small_or_imprecise_dtypes=True))
            once(g.iota(region[:], pattern=[[REG, E]], base=0, channel_multiplier=0, allow_small_or_imprecise_dtypes=True))
            once(g.memset(ones[:], 1.0))
            once(g.affine_select(out=before[:], in_=ones[:], compare_op=ALU.is_ge, fill=0.0, base=-1,
                                 pattern=[[1, P]], channel_multiplier=-1))
            once(g.memset(run[:], 0.0))
            once(g.iota(dest[:], pattern=[[2 * P, BLK], [1, 2]], base=0, channel_multiplier=2,
                        allow_small_or_imprecise_dtypes=True))
            once(g.iota(iota_t[:], pattern=[[1, TILES]], base=0, channel_multiplier=0, allow_small_or_imprecise_dtypes=True))
            once(g.memset(pad[:], 0.0))
            once(g.memset(pad[:, D + 1:D + 2], float(FAR)))
            cst.end()

            def rstd(st, ready, done, n):
                hold(g, "pool", s[ready], n + 1)
                g.tensor_scalar(st[:, 8:9], st[:, 7:8], EPS, None, ALU.add).then_inc(s[done], 1)
                g.wait_ge(s[done], 2 * n + 1)
                g.tensor_tensor(st[:, 9:10], st[:, 8:9], minus_half[:], ALU.pow).then_inc(s[done], 1)

            def iteration(a=None, m=None, b=None, c=None):
                ahead = following(a)
                if ahead is not None:
                    rstd(st1, "a_var", "a_rstd", ahead)
                if b is not None:
                    xb = xall[:, bass.ds(b, 1), :].rearrange("p a d -> p (a d)")
                    g.wait_ge(s["b_xn"], b + 1)
                    g.wait_ge(bo_done, 1)
                    g.tensor_tensor(xb, xb, bo_all[:], ALU.add).then_inc(s["b_xb"], 1)
                if a is not None:
                    hold(g, "pool", s["a_idx"], a + 1)
                    g.indirect_dma_start(mem[:], None, ctxR[:, :], bass.IndirectOffsetOnAxis(ap=gidx[:], axis=0))\
                        .then_inc(s["a_mem"], 16)
                if c is not None:
                    g.wait_ge(s["c_row1"], c + 1)
                    hold(g, "pool", s["c_weight"], c + 1)
                    for k, row in enumerate((row0, row1)):
                        g.indirect_dma_start(routed[:, :], bass.IndirectOffsetOnAxis(ap=slot[:, k:k + 1], axis=0),
                                             row[:, :], None).then_inc(s["c_scatter"], 16)
                if m is not None:
                    rstd(st2, "b_var", "b_rstd", m)
                if b is not None:
                    rstd(st3, "c_var", "c_rstd", b)

            rstd(st1, "a_var", "a_rstd", 0)
            pipeline(g, iteration)

            g.wait_ge(s["m_gb"], 32)
            g.wait_ge(s["b_x2"], BLK)
            g.wait_ge(s["c_xn"], BLK)
            g.tensor_tensor(xall[:], xall[:], beta_all.unsqueeze(1).broadcast_to((P, BLK, D)), ALU.add)\
                .then_inc(s["m_bx"], 1)

            def scatter_results(t):
                g.wait_ge(s["f_row"], t + 1)
                hold(g, "pool", s["f_yw"], t + 1)
                g.indirect_dma_start(expert_out[:, :], bass.IndirectOffsetOnAxis(ap=target_row[:], axis=0),
                                     yw, None, bounds_check=2 * TOK - 1, oob_is_err=False).then_inc(s["f_out"], 16)
            with g.Fori(0, TILES) as t:
                scatter_results(t)

            for group in range(BLK // YG):
                y, st = ypair[:, group * YG:(group + 1) * YG], ystat[:, group % 2]
                g.wait_ge(s[f"y_pair{group}"], 16)
                g.tensor_tensor(y[:, :, 0, :], y[:, :, 0, :], y[:, :, 1, :], ALU.add).then_inc(s["y_sum"], 1)
                g.wait_ge(s["y_var"], group + 1)
                g.tensor_scalar(st[:, :, 8:9], st[:, :, 7:8], EPS, None, ALU.add).then_inc(s["y_rstd"], 1)
                g.wait_ge(s["y_rstd"], 2 * group + 1)
                g.tensor_tensor(st[:, :, 9:10], st[:, :, 8:9], minus_half[:].unsqueeze(1).broadcast_to((P, YG, 1)), ALU.pow)\
                    .then_inc(s["y_rstd"], 1)

        @block.scalar
        def _(act):
            def bv_columns():
                act.wait_ge(ld_small, N_SMALL)
                act.activation(zT[:], bvT[:].unsqueeze(2).broadcast_to((P, HP, P)), ACT.Copy).then_inc(bvrep_done, 1)

            def iteration(a=None, m=None, b=None, c=None):
                A_, M_, B_, C_ = (i is not None for i in (a, m, b, c))
                if B_:
                    act.wait_ge(s["b_xT_ps"], b + 1)
                    act.activation(x2T[:], bank[6][:, 0:D], ACT.Copy).then_inc(s["b_xT"], 1)
                if C_:
                    act.wait_ge(s["c_xT_ps"], c + 1)
                if A_:
                    act.wait_ge(s["a_xT_ps"], a + 1)
                    act.activation(xT[:], bank[0][:, 0:D], ACT.Copy).then_inc(s["a_xT"], 1)
                if C_:
                    act.activation(x3T[:], bank[0][:, D:2 * D], ACT.Copy).then_inc(s["c_xT"], 1)
                    act.wait_ge(s["c_xn"], c + 1)
                    wait(act, s["c_scatter"], 32 * c)
                    act.activation(row1[:, 0:D], row0[:, 0:D], ACT.Copy).then_inc(s["c_row1"], 1)
                    act.wait_ge(s["c_lg_ps"], c + 1)
                    act.activation(lgr[:], bank[1][:, 384:384 + E], ACT.Copy).then_inc(s["c_lg"], 1)
                if A_:
                    act.wait_ge(s["a_qpT_ps"], a + 1)
                    act.activation(qpT[:], bank[1][:, 0:D], ACT.Copy).then_inc(s["a_qpT"], 1)
                if M_:
                    act.wait_ge(s["a_xs"], m + 1)
                    act.activation(xs[:], xs[:], ACT.Exp, scale=float(XD) ** -0.5).then_inc(s["a_exp"], 1)
                if C_:
                    act.wait_ge(s["c_d"], c + 1)
                    act.activation(rsc[:, 1:2], rsc[:, 0:1], ACT.Exp).then_inc(s["c_exp"], 1)
                if A_:
                    act.wait_ge(s["a_sc_ps"], a + 1)
                    act.activation(sc[:], bank[0][:, 0:M], ACT.Copy).then_inc(s["a_sc"], 1)
                if M_:
                    for j in range(2):
                        act.wait_ge(s["a_pT_ps"], 2 * m + j + 1)
                        act.activation(xpT[:, 4 * j:4 * j + 4, :], bank[2 + j][:], ACT.Copy).then_inc(s["a_pT"], 1)

                def exponents(j):
                    act.wait_ge(s["b_as"], 2 * b + j + 1)
                    act.activation(as_[:, 8 * j:8 * j + 8, :], as_[:, 8 * j:8 * j + 8, :], ACT.Exp, scale=float(A) ** -0.5)\
                        .then_inc(s["b_exp"], 1)

                def values(j):
                    act.wait_ge(s["b_v_ps"], 2 * b + j + 1)
                    act.activation(vs[:, j * H // 2:(j + 1) * H // 2, :], bank[6 + j][:], ACT.Copy).then_inc(s["b_v"], 1)
                if B_:
                    exponents(0)
                    values(0)
                    exponents(1)
                    values(1)
                def turned(q):
                    act.wait_ge(s["b_pT_ps"], 4 * b + q + 1)
                    act.activation(apT[:, 4 * q:4 * q + 4, :], bank[PT_BANK[q]][:], ACT.Copy).then_inc(s["b_pT"], 1)
                if M_:
                    act.wait_ge(s["a_av_ps"], m + 1)
                    act.activation(aoT[:], bank[1][:, 0:D], ACT.Copy).then_inc(s["a_aoT"], 1)
                if B_:
                    turned(0)
                    turned(1)
                    turned(2)
                    turned(3)
                    act.wait_ge(s["b_av_ps"], b + 1)
                    act.activation(zT[:, 0:4, :], bank[6][:], ACT.Copy).then_inc(s["b_zT_s"], 1)
                if A_:
                    act.wait_ge(s["a_memT_ps"], a + 1)
                    act.activation(memT[:], bank[1][:, 0:D], ACT.Copy).then_inc(s["a_memT"], 1)

            act.wait_ge(ld_xw, 48)
            act.activation(wk_rep[:], xwkv[:, :, 0:XD].unsqueeze(2).broadcast_to((P, KD, P // XD, XD)), ACT.Copy)\
                .then_inc(xw_ready, 1)
            pipeline(act, iteration, bv_columns)

            def hidden_out(t):
                act.wait_ge(s["f_h_ps"], 2 * t + 1)
                act.activation(hs[:, 0:512], bank[2][:], ACT.Copy).then_inc(s["f_hs_s"], 1)

            def hidden_relu(t):
                e = act.value_load(tile_ei[0:1, bass.ds(t, 1)], min_val=0, max_val=E - 1)
                act.wait_ge(s["f_hT_ps"], 2 * t + 1)
                for c in range(4):
                    i = act.activation(hT[:, c, :], bank[4][:, c * P:(c + 1) * P], ACT.Relu,
                                       bias=b1T[:, bass.ds(e * KF + c, 1)])
                i.then_inc(s["f_hT_s"], 1)

            def weigh(t):
                act.wait_ge(s["f_yb"], t + 1)
                wait(act, s["f_out"], 16 * t)
                act.activation(yw, yb, ACT.Copy, scale=meta[:, bass.ds(t, 1), 0]).then_inc(s["f_yw"], 1)

            act.wait_ge(ld_b12, 32)
            act.wait_ge(s["m_plan"], 1)
            hidden_out(0)
            hidden_relu(0)
            hidden_out(1)
            weigh(0)
            hidden_relu(1)
            with act.Fori(2, TILES) as t:
                hidden_out(t)
                weigh(t - 1)
                hidden_relu(t)
            weigh(LAST)

        @block.vector
        def _(v):
            vn = Steps(v, n_dve, 1)
            va, vm, vb, vc = Steps(v, a_dve, 4), Steps(v, m_dve, 5), Steps(v, b_dve, 9), Steps(v, c_dve, 14)

            def xblk(n):
                return xall[:, bass.ds(n, 1), :].rearrange("p a d -> p (a d)")

            def stats(steps, n, src, st, var):
                steps.did(v.bn_stats(st[:, 0:6], src))
                steps.hold_last(passed_by["dve"])
                v.bn_aggr(st[:, 6:8], st[:, 0:6]).then_inc(s[var], 1)

            def norm(n, src, st, rstd, dst, xn_sem):
                v.wait_ge(s[rstd], 2 * n + 2)
                v.tensor_scalar(dst, src, st[:, 6:7], st[:, 9:10], ALU.subtract, ALU.mult).then_inc(s[xn_sem], 1)

            def softmax_shift(steps, n, parts, mx, dst, done):
                hh = H // len(parts)
                for j, part in enumerate(parts):
                    steps.did(v.tensor_reduce(mx[:, j * hh:(j + 1) * hh], part, AX_X, ALU.max))
                steps.wait_last()
                for j, part in enumerate(parts):
                    i = v.tensor_tensor(dst[:, j * hh:(j + 1) * hh, :], part,
                                        mx[:, j * hh:(j + 1) * hh].unsqueeze(2).broadcast_to((P, hh, S)), ALU.subtract)
                    if j == len(parts) - 1:
                        i.then_inc(s[done], 1)

            def softmax_sums(steps, probs, rc):
                steps.did(v.tensor_reduce(rc, probs, AX_X, ALU.add))
                steps.wait_last()
                steps.did(v.reciprocal(rc, rc))
                steps.wait_last()

            def argmax(n):
                hold(v, "dve", s["a_sc"], n + 1)
                va.did(v.max(mx8[:], sc[:]))
                va.hold_last(passed_by["dve"])
                va.did(v.max_index(ix8[:], mx8[:], sc[:]))
                va.wait_last()
                va.did(v.tensor_copy(mx8[:, 0:1], ix8[:, 0:1]))
                va.wait_last()
                va.did(v.tensor_tensor(mx8[:, 1:2], mx8[:, 0:1], rowbase[:, bass.ds(n, 1)], ALU.add))
                va.wait_last()
                v.tensor_copy(gidx[:], mx8[:, 1:2]).then_inc(s["a_idx"], 1)

            def memory(n):
                v.wait_ge(s["a_mkv_ps"], n + 1)
                for b in range(BB):
                    v.tensor_tensor(mkb[:, b], bank[1][:, b * S:(b + 1) * S].unsqueeze(1).broadcast_to((P, P // XD, S)),
                                    headmask[:].unsqueeze(2).broadcast_to((P, P // XD, S)), ALU.mult)
                for r in range(2):
                    i = v.tensor_copy(mvw[r * S:(r + 1) * S, :, (2 + r) * XD:(3 + r) * XD],
                                      bank[1][r * S:(r + 1) * S, P:P + BB * XD].rearrange("p (b e) -> p b e", e=XD))
                i.then_inc(s["a_mkb"], 1)

            def project(n, c):
                v.wait_ge(s["b_q_ps"], 4 * n + c + 1)
                dst, bias = ((qT, bqT), (kT, bkT))[c // 2]
                hp = slice(4 * (c % 2), 4 * (c % 2) + 4)
                v.tensor_tensor(dst[:, hp, :], bank[6 + c % 2][:].rearrange("p (h t) -> p h t", t=P),
                                bias[:, hp].unsqueeze(2).broadcast_to((P, 4, P)), ALU.add).then_inc(s["b_q"], 1)

            def masked_shift(n, j):
                hh = slice(8 * j, 8 * j + 8)
                v.wait_ge(s["b_s_ps"], 2 * n + j + 1)
                vb.did(v.tensor_tensor(as_[:, hh, :], bank[4 + j][:].rearrange("p (h t) -> p h t", t=S),
                                       causal[:].unsqueeze(1).broadcast_to((P, 8, S)), ALU.min))
                vb.wait_last()
                vb.did(v.tensor_reduce(bmx[:, hh], as_[:, hh, :], AX_X, ALU.max))
                vb.wait_last()
                v.tensor_tensor(as_[:, hh, :], as_[:, hh, :], bmx[:, hh].unsqueeze(2).broadcast_to((P, 8, S)), ALU.subtract)\
                    .then_inc(s["b_as"], 1)

            def self_weights(n, j):
                hh = slice(8 * j, 8 * j + 8)
                v.wait_ge(s["b_exp"], 2 * n + j + 1)
                softmax_sums(vb, as_[:, hh, :], brc[:, hh])
                for i in range(BB):
                    r = slice(i * S, (i + 1) * S)
                    v.tensor_tensor(aprob[r, hh, r], as_[r, hh], brc[r, hh].unsqueeze(2).broadcast_to((S, 8, S)), ALU.mult)\
                        .then_inc(s["b_prob"], 1)

            def route_weights(n):
                vc.begin(n)
                v.wait_ge(s["c_lg"], n + 1)
                vc.did(v.tensor_tensor(lg[:], lgr[:], br_all[:], ALU.add))
                vc.hold_last(passed_by["dve"])
                vc.did(v.max(rv8[:], lg[:]))
                vc.hold_last(passed_by["dve"])
                v.tensor_tensor(rsc[:, 0:1], rv8[:, 1:2], rv8[:, 0:1], ALU.subtract).then_inc(s["c_d"], 1)
                vc.did(v.max_index(ri8[:], rv8[:], lg[:]))
                vc.wait_last()
                vc.did(v.tensor_copy(rsc[:, 4:6], ri8[:, 0:2]))
                vc.wait_last()
                vc.did(v.tensor_scalar(oh0[:], iota_e[:], rsc[:, 4:5], None, ALU.is_equal))
                vc.did(v.tensor_scalar(oh1[:], iota_e[:], rsc[:, 5:6], None, ALU.is_equal))
                vc.wait_last()
                v.tensor_tensor(ohs[:], oh0[:], oh1[:], ALU.add).then_inc(s["c_ohs"], 1)

            def route_rows(n):
                v.wait_ge(s["c_exp"], n + 1)
                v.wait_ge(s["c_row1"], n + 1)
                vc.did(v.tensor_scalar(rsc[:, 2:3], rsc[:, 1:2], 1.0, None, ALU.add))
                vc.wait_last()
                vc.did(v.reciprocal(row0[:, D:D + 1], rsc[:, 2:3]))
                vc.wait_last()
                v.tensor_tensor(row1[:, D:D + 1], rsc[:, 1:2], row0[:, D:D + 1], ALU.mult)
                v.tensor_copy(row0[:, D + 1:D + 2], dest[:, bass.ds(n, 1), 0])
                v.tensor_copy(row1[:, D + 1:D + 2], dest[:, bass.ds(n, 1), 1])
                v.wait_ge(s["c_pos_ps"], n + 1)
                vc.did(v.tensor_tensor(pos[:], bank[0][:, 272:272 + E], run[:], ALU.add))
                vc.wait_last()
                v.tensor_tensor(run[:], run[:], bank[0][:, 288:288 + E], ALU.add).then_inc(s["c_pos"], 1)
                vc.did(v.tensor_tensor(pos[:], pos[:], region[:], ALU.add))
                vc.wait_last()
                for k, oh in enumerate((oh0, oh1)):
                    vc.did(v.tensor_tensor(rtmp[:], pos[:], oh[:], ALU.mult))
                    vc.wait_last()
                    vc.did(v.tensor_reduce(rsc[:, 6 + k:7 + k], rtmp[:], AX_X, ALU.add))
                    vc.wait_last()
                v.tensor_copy(slot[:], rsc[:, 6:8]).then_inc(s["c_weight"], 1)

            def iteration(a=None, m=None, b=None, c=None):
                A_, M_, B_, C_ = (i is not None for i in (a, m, b, c))
                ahead = following(a)
                if A_:
                    va.begin(a)
                if M_:
                    vm.begin(m)
                    memory(m)
                if B_:
                    vb.begin(b)
                    project(b, 0)
                if ahead is not None:
                    vn.begin(ahead)
                    stats(vn, ahead, xblk(ahead), st1, "a_var")
                if B_:
                    project(b, 1)
                if C_:
                    route_weights(c)
                if M_:
                    v.wait_ge(s["a_log_ps"], m + 1)
                    softmax_shift(vm, m, [bank[2 + j][:].rearrange("p (h m) -> p h m", m=S) for j in range(2)], amx, xs, "a_xs")
                if ahead is not None:
                    v.wait_ge(s["a_xT_ps"], a + 1)
                    norm(ahead, xblk(ahead), st1, "a_rstd", xn[:], "a_xn")
                if B_:
                    project(b, 2)
                if B_:
                    project(b, 3)
                if M_:
                    v.wait_ge(s["a_exp"], m + 1)
                    softmax_sums(vm, xs[:], arc[:])
                    v.tensor_tensor(xs[:], xs[:], arc[:].unsqueeze(2).broadcast_to((P, H, S)), ALU.mult).then_inc(s["a_prob"], 1)
                if B_:
                    for j in range(2):
                        masked_shift(b, j)
                    self_weights(b, 0)
                if A_:
                    argmax(a)
                if B_:
                    self_weights(b, 1)
                if C_:
                    route_rows(c)
                if B_:
                    v.wait_ge(s["b_av_ps"], b + 1)
                    v.tensor_copy(zT[:, 4:8, :], bank[7][:]).then_inc(s["b_zT_v"], 1)
                if M_:
                    v.wait_ge(s["a_wc_ps"], m + 1)
                    v.tensor_tensor(xblk(m), xblk(m), bank[0][:, 0:D], ALU.add).then_inc(s["a_x1"], 1)
                    hold(v, "dve", s["a_x1"], m + 1)
                    stats(vm, m, xblk(m), st2, "b_var")
                    norm(m, xblk(m), st2, "b_rstd", xn2[:], "b_xn")
                if B_:
                    v.wait_ge(s["b_o_ps"], b + 1)
                    v.wait_ge(s["b_xb"], b + 1)
                    v.tensor_tensor(xblk(b), xblk(b), bank[5][:, 0:D], ALU.add).then_inc(s["b_x2"], 1)
                    hold(v, "dve", s["b_x2"], b + 1)
                    stats(vb, b, xblk(b), st3, "c_var")
                    wait(v, s["c_scatter"], 32 * b)
                    wait(v, s["c_row1"], b)
                    wait(v, s["c_target"], 16 * b)
                    norm(b, xblk(b), st3, "c_rstd", row0[:, 0:D], "c_xn")

            def output_bias():
                v.wait_ge(ld_small, N_SMALL)
                v.wait_ge(ld_x, 16)
                v.wait_ge(bo_ps, 1)
                v.tensor_tensor(bo_all[:], bo_all[:], bank[7][:, 0:D], ALU.add).then_inc(bo_done, 1)

            v.wait_ge(ld_x0, 16)
            v.wait_ge(k_pool, K_POOL)
            vn.begin(0)
            stats(vn, 0, xblk(0), st1, "a_var")
            norm(0, xblk(0), st1, "a_rstd", xn[:], "a_xn")
            pipeline(v, iteration, output_bias)
            for st in (va, vm, vb, vc):
                st.end()

            vm = Steps(v, p_dve, 18)
            vm.begin(0)

            def step(ins):
                vm.did(ins)
                vm.wait_last()
            step(v.tensor_tensor(cum2[:], run[:], region[:], ALU.add))
            step(v.tensor_copy(padrow_i[:], cum2[:]))
            step(v.tensor_scalar(tiles_i[:], run[:], float(P - 1), None, ALU.add))
            step(v.tensor_scalar(tiles_i[:], tiles_i[:], P.bit_length() - 1, None, ALU.arith_shift_right))
            step(v.tensor_copy(tiles[:], tiles_i[:]))
            step(v.tensor_copy(cum[:], tiles[:]))
            for e in range(1, E):
                step(v.tensor_tensor(cum[:, e:e + 1], cum[:, e:e + 1], cum[:, e - 1:e], ALU.add))
            over = (P, TILES, E - 1)
            step(v.tensor_tensor(passed, iota_t[:].unsqueeze(2).broadcast_to(over),
                                 cum[:, 0:E - 1].unsqueeze(1).broadcast_to(over), ALU.is_ge))
            vm.did(v.tensor_reduce(tile_e[:], passed, AX_X, ALU.add))
            step(v.tensor_tensor(passed_tiles, passed, tiles[:, 0:E - 1].unsqueeze(1).broadcast_to(over), ALU.mult))
            step(v.tensor_reduce(tile_s[:], passed_tiles, AX_X, ALU.add))
            step(v.tensor_tensor(tile_s[:], iota_t[:], tile_s[:], ALU.subtract))
            v.tensor_scalar(tile_idle[:], iota_t[:], cum[:, E - 1:E], float(2 * E * REG), ALU.is_ge, ALU.mult)
            v.tensor_scalar(passed[:, :, 0], tile_s[:], float(P), None, ALU.mult)
            v.tensor_copy(tile_ei[:], tile_e[:]).then_inc(s["m_hist"], 1)
            v.wait_ge(s["m_hist"], 1)
            v.scalar_tensor_tensor(out=tile_s[:], in0=tile_e[:], scalar=float(REG), in1=passed[:, :, 0], op0=ALU.mult, op1=ALU.add)\
                .then_inc(s["m_hist"], 1)
            v.wait_ge(s["m_hist"], 2)
            v.tensor_tensor(tile_s[:], tile_s[:], tile_idle[:], ALU.add).then_inc(s["m_hist"], 1)
            v.wait_ge(s["m_hist"], 3)
            v.tensor_scalar(tile_ri[:], tile_s[:], float(E * REG), None, ALU.min).then_inc(s["m_plan"], 1)
            v.wait_ge(s["m_plan"], 1)
            vm.end()

            v.wait_ge(ld_b12, 32)

            def tile_in(t):
                v.wait_ge(s["f_xg"], 16 * t + 16)
                v.tensor_copy(meta[:, bass.ds(t, 1), :], xg[:, D:D + 2]).then_inc(s["f_meta"], 1)
                v.wait_ge(s["f_xT_ps"], t + 1)
                v.tensor_copy(xgT, bank[0][:, 0:D].rearrange("p (k t) -> p k t", t=P)).then_inc(s["f_xT"], 1)

            def hidden_out(t):
                v.wait_ge(s["f_h_ps"], 2 * t + 2)
                v.tensor_copy(hs[:, 512:1024], bank[3][:]).then_inc(s["f_hs_v"], 1)

            def hidden_relu(t):
                e = v.value_load(tile_ei[0:1, bass.ds(t, 1)], min_val=0, max_val=E - 1)
                v.wait_ge(s["f_hT_ps"], 2 * t + 2)
                for c in range(4):
                    i = v.tensor_scalar(hT[:, 4 + c, :], bank[5][:, c * P:(c + 1) * P],
                                        b1T[:, bass.ds(e * KF + 4 + c, 1)], 0.0, ALU.add, ALU.max)
                i.then_inc(s["f_hT_v"], 1)

            def result_out(t):
                e = v.value_load(tile_ei[0:1, bass.ds(t, 1)], min_val=0, max_val=E - 1)
                v.wait_ge(s["f_o_ps"], t + 1)
                wait(v, s["f_yw"], t)
                v.tensor_tensor(yb, bank[6][:, 0:D], b2_all[:, bass.ds(e * D, D)], ALU.add).then_inc(s["f_yb"], 1)
                wait(v, s["f_out"], 16 * t)
                v.tensor_copy(target_row[:], meta[:, bass.ds(t, 1), 1]).then_inc(s["f_row"], 1)

            tile_in(0)
            hidden_out(0)
            tile_in(1)
            hidden_relu(0)
            hidden_out(1)
            tile_in(2)
            result_out(0)
            hidden_relu(1)
            with v.Fori(2, LAST) as t:
                hidden_out(t)
                tile_in(t + 1)
                result_out(t - 1)
                hidden_relu(t)
            hidden_out(LAST)
            result_out(LAST - 1)
            hidden_relu(LAST)
            result_out(LAST)

            vy = Steps(v, y_dve, 1 + 2 * YG)
            v.wait_ge(s["m_tgt"], 32)
            v.wait_ge(s["m_gb"], 32)
            v.wait_ge(s["m_bx"], 1)
            for group in range(BLK // YG):
                vy.begin(group)
                st = ystat[:, group % 2]
                y = ypair[:, group * YG:(group + 1) * YG]
                t = tgt[group // 2][:, group % 2 * YG:(group % 2 + 1) * YG]
                v.wait_ge(s["y_sum"], group + 1)
                vy.did(v.tensor_tensor(y[:, :, 0, :], y[:, :, 0, :], t, ALU.add))
                vy.wait_last()
                for j in range(YG):
                    vy.did(v.bn_stats(st[:, j, 0:6], y[:, j, 0, :]))
                vy.wait_last()
                for j in range(YG):
                    i = v.bn_aggr(st[:, j, 6:8], st[:, j, 0:6])
                i.then_inc(s["y_var"], 1)
                v.wait_ge(s["y_var"], group + 1)
                for j in range(YG):
                    vy.did(v.scalar_tensor_tensor(out=y[:, j, 1, :], in0=y[:, j, 0, :], scalar=st[:, j, 6:7], in1=gamma_all,
                                                  op0=ALU.subtract, op1=ALU.mult))
                vy.wait_last()
                v.wait_ge(s["y_rstd"], 2 * group + 2)
                for j in range(YG):
                    n = group * YG + j
                    i = v.scalar_tensor_tensor(out=xall[:, n, :], in0=y[:, j, 1, :], scalar=st[:, j, 9:10], in1=xall[:, n, :],
                                               op0=ALU.mult, op1=ALU.add)
                i.then_inc(s["y_out"], 1)
            vy.end()

        @block.tensor
        def _(pe):
            mm = nc.tensor.matmul
            tr = nc.tensor.transpose

            def bo_through_values():
                pe.wait_ge(bvrep_done, 1)
                for c in range(HP):
                    i = mm(bank[7][:, 0:D], zT[:, c, :], awo[:, c, :], start=c == 0, stop=c == HP - 1)
                i.then_inc(bo_ps, 1)

            def turn(a, m, c):
                if m is not None:
                    wait(pe, s["a_x1"], m)
                if c is not None:
                    pe.wait_ge(s["c_xn"], c + 1)
                    for k in range(KD):
                        i = tr(bank[0][:, D + k * P:D + (k + 1) * P], row0[:, k * P:(k + 1) * P], ident[:])
                    i.then_inc(s["c_xT_ps"], 1)
                if a is not None:
                    pe.wait_ge(s["a_xn"], a + 1)
                    for k in range(KD):
                        i = tr(bank[0][:, k * P:(k + 1) * P], xn[:, k * P:(k + 1) * P], ident[:])
                    i.then_inc(s["a_xT_ps"], 1)

            def logits(n):
                pe.wait_ge(s["c_xT"], n + 1)
                for k in range(KD):
                    i = mm(bank[1][:, 384:384 + E], x3T[:, k, :], wr[:, k, :], start=k == 0, stop=k == KD - 1)
                i.then_inc(s["c_lg_ps"], 1)

            def queries(a, m, c):
                if m is not None:
                    pe.wait_ge(s["a_mkb"], m + 1)
                if c is not None:
                    pe.wait_ge(s["c_lg"], c + 1)
                pe.wait_ge(s["a_xT"], a + 1)
                for e in range(KD):
                    for k in range(KD):
                        i = mm(bank[1][:, e * P:(e + 1) * P], xwq[:, k, e * P:(e + 1) * P], xT[:, k, :],
                               start=k == 0, stop=k == KD - 1)
                i.then_inc(s["a_qpT_ps"], 1)

            def context_scores(n):
                pe.wait_ge(ld_ctx, 16 * n + 16)
                pe.wait_ge(s["a_qpT"], n + 1)
                for b in range(BB):
                    for k in range(KD):
                        i = mm(bank[0][b * S:(b + 1) * S, 0:M], qpT[:, k, b * S:(b + 1) * S], ctxb[:, b, k, :],
                               start=k == 0, stop=k == KD - 1)
                i.then_inc(s["a_sc_ps"], 1)

            def memory_turn(n):
                pe.wait_ge(s["a_mem"], 16 * n + 16)
                wait(pe, s["a_aoT"], n)
                for k in range(KD):
                    i = tr(bank[1][:, k * P:(k + 1) * P], mem[:, k * P:(k + 1) * P], ident[:])
                i.then_inc(s["a_memT_ps"], 1)

            def memory_project(n):
                hold(pe, "pe", s["a_memT"], n + 1)
                for k in range(KD):
                    mm(bank[1][:, 0:P], wk_rep[:, k].rearrange("p r d -> p (r d)"), memT[:, k, :], start=k == 0, stop=k == KD - 1)
                for r in range(2):
                    for b in range(BB):
                        for k in range(KD):
                            i = mm(bank[1][r * S:(r + 1) * S, P + b * XD:P + (b + 1) * XD], memT[:, k, b * S:(b + 1) * S],
                                   xwkv[:, k, XD:], start=k == 0, stop=k == KD - 1)
                i.then_inc(s["a_mkv_ps"], 1)

            def cross_scores(n):
                pe.wait_ge(s["a_mkb"], n + 1)
                for b in range(BB):
                    for e in range(KD):
                        i = mm(bank[2 + e][b * S:(b + 1) * S, :], qpT[:, e, b * S:(b + 1) * S],
                               mkb[:, b].rearrange("p h m -> p (h m)"), start=True, stop=True)
                i.then_inc(s["a_log_ps"], 1)

            def cross_turn(n):
                pe.wait_ge(s["a_prob"], n + 1)
                for j in range(2):
                    for h in range(4):
                        c = 2 * (4 * j + h)
                        i = tr(bank[2 + j][:, h * P:(h + 1) * P], xs[:, c:c + 2, :].rearrange("p h m -> p (h m)"), ident[:])
                    i.then_inc(s["a_pT_ps"], 1)

            def cross_values(a):
                hold(pe, "pe", s["a_pT"], 2 * a + 2)
                for k in range(KD):
                    for u in range(2):
                        for b in range(BB):
                            for w in range(2):
                                i = mm(bank[1][u * S:(u + 1) * S, k * P + b * S:k * P + (b + 1) * S],
                                       mvw[:, b, (2 - 2 * w) * XD:(6 - 2 * w) * XD],
                                       xpT[:, 4 * k + 2 * u + w, b * S:(b + 1) * S], start=w == 0, stop=w == 1)
                i.then_inc(s["a_av_ps"], 1)

            def cross_out(n, c, k):
                if k == 0:
                    pe.wait_ge(s["a_aoT"], n + 1)
                    if c is not None:
                        pe.wait_ge(s["c_pos"], c + 1)
                i = mm(bank[0][:, 0:D], aoT[:, k, :], xwc[:, k, :], start=k == 0, stop=k == KD - 1)
                if k == KD - 1:
                    i.then_inc(s["a_wc_ps"], 1)

            def self_turn(n):
                pe.wait_ge(s["b_xn"], n + 1)
                for k in range(KD):
                    i = tr(bank[6][:, k * P:(k + 1) * P], xn2[:, k * P:(k + 1) * P], ident[:])
                i.then_inc(s["b_xT_ps"], 1)

            def project(n, c):
                if c == 0:
                    pe.wait_ge(s["b_xT"], n + 1)
                if c >= 2:
                    pe.wait_ge(s["b_q"], 4 * n + c - 1)
                w = (awq, awk)[c // 2]
                for j in range(4):
                    f = (4 * (c % 2) + j) * P
                    for k in range(KD):
                        i = mm(bank[6 + c % 2][:, j * P:(j + 1) * P], w[:, k, f:f + P], x2T[:, k, :],
                               start=k == 0, stop=k == KD - 1)
                i.then_inc(s["b_q_ps"], 1)

            def values(n, j):
                pe.wait_ge(s["b_q"], 4 * n + 3 + j)
                for k in range(KD):
                    i = mm(bank[6 + j][:], x2T[:, k, :], awv[:, k, j * 512:(j + 1) * 512], start=k == 0, stop=k == KD - 1)
                i.then_inc(s["b_v_ps"], 1)

            def self_scores(n):
                hold(pe, "pe", s["b_q"], 4 * n + 4)
                for r in range(2):
                    if r:
                        hold(pe, "pe", s["b_x2"], n)
                    for h in range(r, H, 2):
                        hp = slice(A * r, A * r + A)
                        for b in range(BB):
                            i = mm(bank[4 + r][b * S:(b + 1) * S, (h // 2) * S:(h // 2 + 1) * S],
                                   qT[hp, h // 2, b * S:(b + 1) * S], kT[hp, h // 2, b * S:(b + 1) * S], start=True, stop=True)
                    i.then_inc(s["b_s_ps"], 1)

            def self_turn_weights(n, q):
                pe.wait_ge(s["b_prob"], 4 * n + 2 + 2 * (q // 2))
                for h in range(4):
                    i = tr(bank[PT_BANK[q]][:, h * P:(h + 1) * P], aprob[:, 4 * q + h, :], ident[:])
                i.then_inc(s["b_pT_ps"], 1)

            def self_values(n, q):
                if q == 0:
                    pe.wait_ge(s["b_v"], 2 * n + 2)
                hold(pe, "pe", s["b_pT"], 4 * n + q + 1)
                for j in range(4 * q, 4 * q + 4):
                    r, c = j // HP, j % HP
                    i = mm(bank[6 + c // 4][r * A:(r + 1) * A, c % 4 * P:(c % 4 + 1) * P],
                           vs[:, 2 * c + r, :], apT[:, j, :], start=True, stop=True)
                if q == 3:
                    i.then_inc(s["b_av_ps"], 1)

            def self_out(n, j):
                pe.wait_ge(s["b_zT_v" if j else "b_zT_s"], n + 1)
                for c in range(4 * j, 4 * j + 4):
                    i = mm(bank[5][:, 0:D], zT[:, c, :], awo[:, c, :], start=c == 0, stop=c == HP - 1)
                if j:
                    i.then_inc(s["b_o_ps"], 1)

            def count(n, a):
                pe.wait_ge(s["c_ohs"], n + 1)
                if a is not None:
                    pe.wait_ge(s["a_sc"], a + 1)
                mm(bank[0][:, 272:272 + E], before[:], ohs[:], start=True, stop=True)
                mm(bank[0][:, 288:288 + E], ones[:], ohs[:], start=True, stop=True).then_inc(s["c_pos_ps"], 1)

            def iteration(a=None, m=None, b=None, c=None):
                A_, M_, B_, C_ = (i is not None for i in (a, m, b, c))
                if B_:
                    self_turn(b)
                if M_:
                    memory_project(m)
                if B_:
                    project(b, 0)
                turn(a, m, c)
                if B_:
                    project(b, 1)
                if C_:
                    if M_:
                        pe.wait_ge(s["a_mkb"], m + 1)
                    logits(c)
                if M_:
                    cross_scores(m)
                if A_:
                    queries(a, m, c)
                if B_:
                    project(b, 2)
                    project(b, 3)
                if A_:
                    context_scores(a)
                if B_:
                    self_scores(b)
                if M_:
                    cross_turn(m)
                if B_:
                    values(b, 0)
                    values(b, 1)
                if C_:
                    count(c, a)
                if M_:
                    cross_values(m)
                if B_:
                    self_turn_weights(b, 0)
                    self_turn_weights(b, 1)
                    self_values(b, 0)
                    self_values(b, 1)
                    self_turn_weights(b, 2)
                    self_turn_weights(b, 3)
                if M_:
                    cross_out(m, c, 0)
                if B_:
                    self_values(b, 2)
                    self_values(b, 3)
                if M_:
                    cross_out(m, c, 1)
                if B_:
                    self_out(b, 0)
                if A_:
                    memory_turn(a)
                if B_:
                    self_out(b, 1)

            def output_bias():
                pe.wait_ge(ld_aw, 80)
                bo_through_values()
                pe.wait_ge(bo_done, 1)

            pe.wait_ge(ident_ready, 2)
            pe.wait_ge(ld_xw, 48)
            pe.wait_ge(xw_ready, 1)
            pe.wait_ge(k_pool, K_POOL)
            pipeline(pe, iteration, output_bias)

            def tile_in(t):
                pe.wait_ge(s["f_xg"], 16 * t + 16)
                wait(pe, s["f_xT"], t)
                for k in range(KD):
                    i = tr(bank[0][:, k * P:(k + 1) * P], xg[:, k * P:(k + 1) * P], ident[:])
                i.then_inc(s["f_xT_ps"], 1)

            def up(t):
                e = pe.value_load(tile_ei[0:1, bass.ds(t, 1)], min_val=0, max_val=E - 1)
                pe.wait_ge(s["f_xT"], t + 1)
                for j in range(FH):
                    wait(pe, s["f_hs_v" if j else "f_hs_s"], t)
                    for k in range(KD):
                        i = mm(bank[2 + j][:], xgT[:, k, :], w1[:, bass.ds(e, 1), k, j * 512:(j + 1) * 512],
                               start=k == 0, stop=k == KD - 1)
                    i.then_inc(s["f_h_ps"], 1)

            def hidden_turn(t):
                for j in range(FH):
                    pe.wait_ge(s["f_hs_v" if j else "f_hs_s"], t + 1)
                    wait(pe, s["f_hT_v" if j else "f_hT_s"], t)
                    for c in range(4):
                        i = tr(bank[4 + j][:, c * P:(c + 1) * P], hs[:, (4 * j + c) * P:(4 * j + c + 1) * P], ident[:])
                    i.then_inc(s["f_hT_ps"], 1)

            def down(t):
                e = pe.value_load(tile_ei[0:1, bass.ds(t, 1)], min_val=0, max_val=E - 1)
                wait(pe, s["f_yb"], t)
                pe.wait_ge(s["m_w2"], e * 16 + 16)
                for c in range(KF):
                    if c % 4 == 0:
                        pe.wait_ge(s["f_hT_v" if c else "f_hT_s"], t + 1)
                    i = mm(bank[6][:, 0:D], hT[:, c, :], w2[:, bass.ds(e, 1), c, :], start=c == 0, stop=c == KF - 1)
                i.then_inc(s["f_o_ps"], 1)

            pe.wait_ge(s["m_plan"], 1)
            pe.wait_ge(s["m_w1"], 16 * E)
            tile_in(0)
            up(0)
            tile_in(1)
            hidden_turn(0)
            up(1)
            tile_in(2)
            down(0)
            hidden_turn(1)
            with pe.Fori(2, LAST) as t:
                up(t)
                tile_in(t + 1)
                down(t - 1)
                hidden_turn(t)
            up(LAST)
            down(LAST - 1)
            hidden_turn(LAST)
            down(LAST)


def kernel(**inputs):
    import numpy as np
    import concourse.bacc as bacc
    from concourse.bass_utils import run_bass_kernel_spmd

    def lay(a):
        return np.ascontiguousarray(a)

    g = {k: np.asarray(v) for k, v in inputs.items()}
    D = g["x"].shape[-1]
    arrays = {
        "x": lay(g["x"]),
        "ctxT": lay(g["ctx_1024"].transpose(0, 2, 1)),
        "ctxR": lay(g["ctx_1024"].reshape(-1, D)),
        "xWqT": lay(g["L0_xattn_Wq"].T),
        "xWkvT": lay(g["L0_xattn_Wkv"].T),
        "xWcT": lay(g["L0_xattn_Wc"].T),
        "aWq": lay(g["L0_attn_Wq"].transpose(1, 0, 2).reshape(D, -1)),
        "aWk": lay(g["L0_attn_Wk"].transpose(1, 0, 2).reshape(D, -1)),
        "aWv": lay(g["L0_attn_Wv"].transpose(1, 0, 2).reshape(D, -1)),
        "aWo": lay(g["L0_attn_Wo"].reshape(-1, D)),
        "bq": lay(g["L0_attn_bq"].reshape(-1)),
        "bk": lay(g["L0_attn_bk"].reshape(-1)),
        "bv": lay(g["L0_attn_bv"].reshape(-1)),
        "bo": lay(g["L0_attn_bo"]),
        "WrT": lay(g["L0_ffn_Wr"].T),
        "br": lay(g["L0_ffn_br"]),
        "W1T": lay(g["L0_ffn_W1"].transpose(0, 2, 1)),
        "b1": lay(g["L0_ffn_b1"].reshape(-1)),
        "W2T": lay(g["L0_ffn_W2"].transpose(0, 2, 1)),
        "b2": lay(g["L0_ffn_b2"].reshape(-1)),
        "gamma": lay(g["L0_ffn_gamma"]),
        "beta": lay(g["L0_ffn_beta"]),
    }
    nc = bacc.Bacc("TRN2", target_bir_lowering=False, num_devices=1)
    aps = {k: nc.dram_tensor(k, a.shape, mybir.dt.from_np(a.dtype), kind="ExternalInput").ap() for k, a in arrays.items()}
    out = nc.dram_tensor("out", g["x"].shape, F32, kind="ExternalOutput").ap()
    perceiver_layer(nc, out=out, **aps)
    return run_bass_kernel_spmd(nc, [arrays], core_ids=[0]).results[0]["out"]
```

```python
from contextlib import ExitStack

import concourse.bass as bass
from concourse import mybir

F32 = mybir.dt.float32
F32R = mybir.dt.float32r
I32 = mybir.dt.int32
U32 = mybir.dt.uint32
ALU = mybir.AluOpType
ACT = mybir.ActivationFunctionType
AX_X = mybir.AxisListType.X
P = 128


class Steps:

    def __init__(self, engine, sem, per_block):
        self.engine, self.sem, self.per_block = engine, sem, per_block

    def begin(self, n):
        self.base, self.count = n * self.per_block, 0

    def did(self, instruction):
        self.count += 1
        instruction.then_inc(self.sem, 1)

    def wait_last(self):
        self.engine.wait_ge(self.sem, self.base + self.count)

    def hold_last(self, beside):
        self.wait_last()
        if not isinstance(self.base, int):
            self.engine.sem_inc(beside, 1)

    def end(self):
        assert self.count == self.per_block, (self.sem, self.count)


def perceiver_layer(nc, x, ctxT, ctxR, xWqT, xWkvT, xWcT, aWq, aWk, aWv, aWo, bq, bk, bv, bo,
                    WrT, br, W1T, b1, W2T, b2, gamma, beta, out):
    NB, S, D = x.shape
    M = ctxT.shape[2]
    TOK = NB * S
    BLK = TOK // P
    BB = P // S
    KD = D // P
    KM = M // P
    H = 16
    XD = D // H
    HA = aWq.shape[1]
    A = HA // H
    HP = HA // P
    E = WrT.shape[1]
    F = W1T.shape[2]
    KF = F // P
    FH = F // 512
    ROW = D + 2
    REG = TOK + P
    TILES = 2 * TOK // P + E - 1
    EPS = 1e-5
    MASKED = -100000.0 * float(A) ** 0.5
    FAR = 1 << 24

    routed = nc.dram_tensor("routed", (E * REG + P, ROW), F32, kind="Internal").ap()
    target = nc.dram_tensor("target", (TOK, D), F32, kind="Internal").ap()
    expert_out = nc.dram_tensor("expert_out", (2 * TOK, D), F32, kind="Internal").ap()

    ctx = ExitStack()
    with ctx:
        def sb(name, shape, dt=F32):
            return ctx.enter_context(nc.sbuf_tensor(name, shape, dt))

        def sem(name):
            return ctx.enter_context(nc.semaphore(name))

        under = ExitStack()

        def below(name, shape, dt):
            return under.enter_context(nc.sbuf_tensor(name, shape, dt))

        below("last_experts", [P, E - 2, KD, F], F32)
        awv_lead, awo_lead = below("awv_lead", [P, KD, HA], F32R), below("awo_lead", [P, HP, D], F32R)
        under.close()
        w1 = sb("w1", [P, E, KD, F])
        xall = sb("xall", [P, BLK, D])
        xwq, xwkv, xwc = sb("xwq", [P, KD, D]), sb("xwkv", [P, KD, 2 * XD]), sb("xwc", [P, KD, D])
        awq, awk = (sb(n, [P, KD, HA]) for n in ("awq", "awk"))
        awv_rest, awo_rest = below("awv_rest", [P, KD, HA], F32R), below("awo_rest", [P, HP, D], F32R)
        under.close()
        awv = sb("awv", [P, KD, HA])
        awo = sb("awo", [P, HP, D])
        bqT, bkT, bvT = (sb(n, [P, HP]) for n in ("bqT", "bkT", "bvT"))
        bo_all = sb("bo_all", [P, D])
        wr, br_all = sb("wr", [P, KD, E]), sb("br_all", [P, E])
        b1T = sb("b1T", [P, E * KF])
        b2_all = sb("b2_all", [P, E * D])
        gamma_all, beta_all = xwq[:, 0, :], xwq[:, 1, :]
        ident = sb("ident", [P, P])
        rowbase = sb("rowbase", [P, BLK])
        wk_rep = sb("wk_rep", [P, KD, P // XD, XD])
        iota_e = sb("iota_e", [P, E])
        region = sb("region", [P, E])
        causal = sb("causal", [P, S])
        headmask = sb("headmask", [P, P // XD])
        before = sb("before", [P, P])
        ones = sb("ones", [P, P])
        minus_half = sb("minus_half", [P, 1])
        dest = sb("dest", [P, BLK, 2])
        meta = sb("meta", [P, TILES, 2])
        target_row = sb("target_row", [P, 1], U32)
        xn3 = sb("xn3", [P, D])
        row0, row1 = sb("row0", [P, ROW]), sb("row1", [P, ROW])
        x3T, lgr = sb("x3T", [P, KD, P]), sb("lgr", [P, E])
        YG = BLK // 8
        NG = BLK // YG
        ystat = sb("ystat", [P, 2, YG, 10])
        st1, st2, st3 = (sb(n, [P, 16]) for n in ("st1", "st2", "st3"))
        lg, rv8, ri8 = sb("lg", [P, E]), sb("rv8", [P, 8]), sb("ri8", [P, 8], U32)
        oh0, oh1, ohs, pos = (sb(n, [P, E]) for n in ("oh0", "oh1", "ohs", "pos"))
        run = sb("run", [P, E])
        rtmp, rsc = sb("rtmp", [P, E]), sb("rsc", [P, 8])
        slot = sb("slot", [P, 2], U32)
        pad = sb("pad", [P, ROW])
        iota_t = sb("iota_t", [P, TILES])
        tiles_i, tiles, cum, cum2 = sb("tiles_i", [P, E], I32), sb("tiles", [P, E]), sb("cum", [P, E]), sb("cum2", [P, E])
        padrow_i = sb("padrow_i", [P, E], I32)
        tile_e, tile_s, tile_idle = (sb(n, [P, TILES]) for n in ("tile_e", "tile_s", "tile_idle"))
        tile_ei, tile_ri = sb("tile_ei", [P, TILES], I32), sb("tile_ri", [P, TILES], I32)
        with nc.sbuf_tensor("w2", [P, E, KF, D], F32) as w2:
            pass
        ctxb = sb("ctxb", [P, BB, KD, M])
        xn, xT, qpT = sb("xn", [P, D]), sb("xT", [P, KD, P]), sb("qpT", [P, KD, P])
        sc = sb("sc", [P, M])
        mem, memT = sb("mem", [P, D]), sb("memT", [P, KD, P])
        mkb = sb("mkb", [P, BB, P // XD, S])
        mvw = sb("mvw", [P, BB, 6 * XD])
        xs = sb("xs", [P, H, S])
        xpT = sb("xpT", [P, HP, P])
        aoT = sb("aoT", [P, KD, P])
        mx8, ix8, gidx = sb("mx8", [P, 8]), sb("ix8", [P, 8], U32), sb("gidx", [P, 1], U32)
        amx, arc = sb("amx", [P, H]), sb("arc", [P, H])
        xn2, x2T = sb("xn2", [P, D]), sb("x2T", [P, KD, P])
        z_rest = below("z_rest", [P, HP, P], F32R)
        under.close()
        qT = sb("qT", [P, HP, P])
        x2_lead, x2_rest = sb("x2_lead", [P, KD, P], F32R), sb("x2_rest", [P, KD, P], F32R)
        vs = sb("vs", [P, H, A])
        as_ = sb("as_", [P, H, S])
        aprob = sb("aprob", [P, H, P])
        apT = sb("apT", [P, H, P])
        z_lead = below("z_lead", [P, HP, P], F32R)
        under.close()
        kT = sb("kT", [P, HP, P]) 
        bmx, brc = sb("bmx", [P, H]), sb("brc", [P, H])
        hs, hT = awv[:, 0, :], awv[:, 1, :].rearrange("p (c t) -> p c t", t=P)
        spare = awo[:].rearrange("p c d -> p (c d)")
        passed, passed_tiles = (awv[:, j, 0:TILES * (E - 1)].rearrange("p (t e) -> p t e", e=E - 1) for j in range(2))
        xg, xgT = spare[:, 0:ROW], spare[:, 512:768].rearrange("p (k t) -> p k t", t=P)
        yb, yw = spare[:, 768:1024], spare[:, 1024:1280]
        tgt = [w[:].rearrange("p k f -> p (k f)").rearrange("p (n d) -> p n d", d=D) for w in (awq, awk)]
        ypair = w1[:].rearrange("p e k f -> p (e k f)")[:, 0:2 * BLK * D].rearrange("p (n k d) -> p n k d", k=2, d=D)

        bank = [ctx.enter_context(nc.psum_tensor(f"bank{i}", [P, 512], F32)) for i in range(8)]

        ld_x, ld_ctx, ld_xw, ld_aw, ld_small = (sem(n) for n in ("ld_x", "ld_ctx", "ld_xw", "ld_aw", "ld_small"))
        ld_x0, xw_ready, ident_ready = sem("ld_x0"), sem("xw_ready"), sem("ident_ready")
        ld_b12, ld_avo = sem("ld_b12"), sem("ld_avo")
        w_lead, w_rest = sem("w_lead"), sem("w_rest")
        bo_ps, bo_done, bvrep_done = sem("bo_ps"), sem("bo_done"), sem("bvrep_done")
        a_dve, m_dve, b_dve, c_dve, k_pool = (sem(n) for n in ("a_dve", "m_dve", "b_dve", "c_dve", "k_pool"))
        names_a = ("a_var", "a_rstd", "a_xn", "a_xT_ps", "a_xT", "a_qpT_ps", "a_qpT", "a_sc_ps", "a_sc", "a_idx", "a_mem",
                   "a_memT_ps", "a_memT", "a_mkv_ps", "a_mkb", "a_log_ps", "a_xs", "a_exp", "a_prob", "a_pT_ps",
                   "a_pT", "a_av_ps", "a_aoT", "a_wc_ps", "a_x1")
        names_b = ("b_var", "b_rstd", "b_xn", "b_xb", "b_xT_ps", "b_xT", "b_xlead", "b_xrest", "b_q_ps", "b_q", "b_k",
                   "b_v_ps", "b_v", "b_s_ps", "b_as", "b_exp", "b_prob", "b_pT_ps", "b_pT", "b_av_ps", "b_zlead", "b_zrest", "b_o_ps", "b_x2")
        names_c = ("c_var", "c_rstd", "c_xn", "c_xT_ps", "c_xT", "c_lg_ps", "c_lg", "c_d", "c_exp", "c_ohs", "c_pos_ps", "c_pos",
                   "c_rows", "c_weight", "c_scatter", "c_target")
        names_m = ("m_hist", "m_padrow", "m_plan", "m_pads", "m_w1", "m_w2", "m_tgt", "m_gb", "m_bx")
        names_f = ("f_xg", "f_meta", "f_xT_ps", "f_xT", "f_h_ps", "f_hs_s", "f_hs_v", "f_hT_ps", "f_hT_s", "f_hT_v",
                   "f_o_ps", "f_yb", "f_yw", "f_row", "f_out")
        names_y = tuple(f"y_pair{g}" for g in range(NG)) + ("y_sum", "y_var", "y_rstd", "y_shift", "y_norm", "y_gamma", "y_out", "y_store")
        s = {n: sem(n) for n in names_a + names_b + names_c + names_m + names_f + names_y}
        passed_by = {e: sem(f"passed_by_{e}") for e in ("dve", "pool", "pe")}
        n_dve, p_dve, y_dve = sem("n_dve"), sem("p_dve"), sem("y_dve")
        LAST = TILES - 1
        K_POOL = 20
        N_SMALL = 5 * 16
        PT_BANK = (4, 5, 2, 3)
        block = ctx.enter_context(nc.Block())

        def wait(engine, semaphore, value):
            if not isinstance(value, int) or value > 0:
                engine.wait_ge(semaphore, value)

        def hold(engine, name, semaphore, value):
            if not isinstance(value, int):
                engine.wait_ge(semaphore, value)
                engine.sem_inc(passed_by[name], 1)
            else:
                wait(engine, semaphore, value)

        def following(a):
            return None if a is None or isinstance(a, int) and a + 1 == BLK else a + 1

        def pipeline(engine, iteration, between=None, before_last=None):
            iteration(a=0)
            iteration(a=1, m=0)
            if between is not None:
                between()
            iteration(a=2, m=1, b=0)
            iteration(a=3, m=2, b=1, c=0)
            with engine.Fori(4, BLK - 1) as n:
                iteration(a=n, m=n - 1, b=n - 2, c=n - 3)
            iteration(a=BLK - 1, m=BLK - 2, b=BLK - 3, c=BLK - 4)
            iteration(m=BLK - 1, b=BLK - 2, c=BLK - 3)
            iteration(b=BLK - 1, c=BLK - 2)
            if before_last is not None:
                before_last()
            iteration(c=BLK - 1)

        @block.sync
        def _(sp):
            def load_ctx(n):
                sp.dma_start(ctxb[:], ctxT[bass.ds(n * BB, BB)].rearrange("b (k p) m -> p b k m", p=P)).then_inc(ld_ctx, 16)

            def load_weights(pairs, loaded):
                for dst, src in pairs:
                    sp.dma_start(dst[:], src.rearrange("(k p) e -> p k e", p=P)).then_inc(loaded, 16)

            xv = x.rearrange("(n b) s d -> (b s) n d", b=BB)
            sp.dma_start(xall[:, 0:3, :], xv[:, 0:3, :]).then_inc(ld_x0, 16)
            load_weights(((xwq, xWqT), (xwkv, xWkvT)), ld_xw)
            load_ctx(0)
            load_weights(((xwc, xWcT),), ld_xw)
            with nc.allow_non_contiguous_dma(reason="small biases, once"):
                for dst, src in ((bqT, bq), (bkT, bk), (bvT, bv)):
                    sp.dma_start(dst[:], src.rearrange("(k p) -> p k", p=P)).then_inc(ld_small, 16)
            for dst, src in ((bo_all, bo), (br_all, br)):
                sp.dma_start(dst[:], src.partition_broadcast(P)).then_inc(ld_small, 16)

            def load_rest():
                sp.wait_ge(s["a_mem"], 16)
                load_weights(((awv, aWv), (awo, aWo)), ld_avo)
                load_weights(((awq, aWq), (awk, aWk), (wr, WrT)), ld_aw)

            def load_more():
                sp.wait_ge(s["a_mem"], 32)
                sp.dma_start(xall[:, 3:BLK, :], xv[:, 3:BLK, :]).then_inc(ld_x, 16)
                with nc.allow_non_contiguous_dma(reason="small biases, once"):
                    sp.dma_start(b1T[:], b1.rearrange("(k p) -> p k", p=P)).then_inc(ld_b12, 16)
                sp.dma_start(b2_all[:], b2.partition_broadcast(P)).then_inc(ld_b12, 16)
                sp.wait_ge(k_pool, K_POOL)
                sp.dma_start(routed[E * REG:E * REG + P, :], pad[:]).then_inc(s["m_pads"], 16)

            def store_target(n):
                sp.wait_ge(s["c_xn"], n + 1)
                sp.dma_start(target[bass.ds(n * P, P), :], xn3[:]).then_inc(s["c_target"], 16)

            def iteration(a=None, m=None, b=None, c=None):
                if a is not None and (not isinstance(a, int) or a > 0):
                    sp.wait_ge(s["a_sc_ps"], a)
                    load_ctx(a)
                if c is not None:
                    store_target(c)
            iteration(a=0)
            iteration(a=1)
            load_rest()
            iteration(a=2)
            load_more()
            sp.dma_start(w1[:, 0], W1T[0].rearrange("(k p) f -> p k f", p=P)).then_inc(s["m_w1"], 16)
            with sp.Fori(3, E) as n:
                iteration(a=n, c=n - 3)
                sp.wait_ge(s["m_w1"], 16 * (n - 2))
                sp.dma_start(w1[:, bass.ds(n - 2, 1)].rearrange("p e k f -> p (e k) f"),
                             W1T[bass.ds(n - 2, 1)].rearrange("e (k p) f -> p (e k) f", p=P)).then_inc(s["m_w1"], 16)
            with sp.Fori(E, BLK) as n:
                iteration(a=n, c=n - 3)
            def load_w2(e):
                if e:
                    sp.wait_ge(s["m_w2"], 16 * e)
                sp.dma_start(w2[:, e], W2T[e].rearrange("(k p) d -> p k d", p=P)).then_inc(s["m_w2"], 16)
            iteration(c=BLK - 3)
            sp.wait_ge(s["a_wc_ps"], BLK)
            load_w2(0)
            iteration(c=BLK - 2)
            load_w2(1)
            sp.wait_ge(s["b_xT_ps"], BLK)
            load_w2(2)
            for vector, dst in ((gamma, gamma_all), (beta, beta_all)):
                sp.dma_start(dst, vector.partition_broadcast(P)).then_inc(s["m_gb"], 16)
            sp.wait_ge(s["b_o_ps"], BLK)
            load_w2(3)
            iteration(c=BLK - 1)
            load_w2(4)
            sp.wait_ge(s["m_padrow"], 1)
            for e in range(0, E, 2):
                behind = sp.value_load(padrow_i[0:1, e:e + 1], min_val=e * REG, max_val=e * REG + TOK)
                sp.dma_start(routed[bass.ds(behind, P), :], pad[:]).then_inc(s["m_pads"], 16)
            sp.wait_ge(s["m_pads"], 16 * (E + 1))
            sp.wait_ge(s["c_scatter"], 32 * BLK)
            sp.wait_ge(s["m_plan"], 1)

            def load_tile(t):
                first = sp.value_load(tile_ri[0:1, bass.ds(t, 1)], min_val=0, max_val=E * REG)
                sp.dma_start(xg, routed[bass.ds(first, P), :]).then_inc(s["f_xg"], 16)

            def next_tile(t):
                sp.wait_ge(s["f_xT_ps"], t)
                sp.wait_ge(s["f_meta"], t)
                load_tile(t)
            load_tile(0)
            load_w2(5)
            for e in range(6, E):
                next_tile(e - 5)
                load_w2(e)
            sp.wait_ge(s["c_target"], 16 * BLK)
            for half in range(2):
                sp.dma_start(tgt[half], target[half * TOK // 2:(half + 1) * TOK // 2, :]
                             .rearrange("(n p) d -> p n d", p=P)).then_inc(s["m_tgt"], 16)
            with sp.Fori(E - 5, TILES) as t:
                next_tile(t)

            sp.wait_ge(s["f_out"], 16 * TILES)
            sp.wait_ge(s["f_yw"], TILES)
            pairs = expert_out.rearrange("(n p k) d -> p n k d", p=P, k=2)
            for g in range(NG):
                blocks = slice(g * YG, (g + 1) * YG)
                sp.dma_start(ypair[:, blocks], pairs[:, blocks]).then_inc(s[f"y_pair{g}"], 16)
            for g in range(NG):
                blocks = slice(g * YG, (g + 1) * YG)
                sp.wait_ge(s["y_out"], g + 1)
                sp.dma_start(out.rearrange("(n b) s d -> (b s) n d", b=BB)[:, blocks], xall[:, blocks]).then_inc(s["y_store"], 16)
            sp.wait_ge(s["y_store"], 16 * (NG))

        @block.gpsimd
        def _(g):
            cst = Steps(g, k_pool, K_POOL)
            cst.begin(0)

            def rstd(st, ready, done, n):
                hold(g, "pool", s[ready], n + 1)
                g.tensor_scalar(st[:, 8:9], st[:, 7:8], EPS, None, ALU.add).then_inc(s[done], 1)
                g.wait_ge(s[done], 2 * n + 1)
                g.tensor_tensor(st[:, 9:10], st[:, 8:9], minus_half[:], ALU.pow).then_inc(s[done], 1)

            def once(ins):
                cst.did(ins)
                cst.wait_last()
            once(g.memset(ident[:], 0.0))
            g.affine_select(out=ident[:], in_=ident[:], compare_op=ALU.not_equal, fill=1.0, base=0,
                            pattern=[[-1, P]], channel_multiplier=1).then_inc(ident_ready, 1)
            g.memset(minus_half[:], -0.5).then_inc(ident_ready, 1)
            for b in range(BB):
                once(g.iota(rowbase[b * S:(b + 1) * S, :], pattern=[[BB * M, BLK]], base=b * M, channel_multiplier=0,
                            allow_small_or_imprecise_dtypes=True))
            once(g.memset(headmask[:], 1.0))
            once(g.affine_select(out=headmask[:], in_=headmask[:], compare_op=ALU.is_ge, fill=0.0, base=0,
                                 pattern=[[-XD, P // XD]], channel_multiplier=1))
            once(g.affine_select(out=headmask[:], in_=headmask[:], compare_op=ALU.is_ge, fill=0.0, base=XD - 1,
                                 pattern=[[XD, P // XD]], channel_multiplier=-1))
            once(g.memset(mvw[:], 0.0))
            rstd(st1, "a_var", "a_rstd", 0)
            once(g.memset(causal[:], 3e38))
            for b in range(BB):
                once(g.affine_select(out=causal[b * S:(b + 1) * S, :], in_=causal[b * S:(b + 1) * S, :], compare_op=ALU.is_ge,
                                     fill=MASKED, base=0, pattern=[[-1, S]], channel_multiplier=1))
            once(g.memset(aprob[:], 0.0))
            once(g.iota(iota_e[:], pattern=[[1, E]], base=0, channel_multiplier=0, allow_small_or_imprecise_dtypes=True))
            once(g.iota(region[:], pattern=[[REG, E]], base=0, channel_multiplier=0, allow_small_or_imprecise_dtypes=True))
            once(g.memset(ones[:], 1.0))
            once(g.affine_select(out=before[:], in_=ones[:], compare_op=ALU.is_ge, fill=0.0, base=-1,
                                 pattern=[[1, P]], channel_multiplier=-1))
            once(g.memset(run[:], 0.0))
            once(g.iota(dest[:], pattern=[[2 * P, BLK], [1, 2]], base=0, channel_multiplier=2,
                        allow_small_or_imprecise_dtypes=True))
            once(g.iota(iota_t[:], pattern=[[1, TILES]], base=0, channel_multiplier=0, allow_small_or_imprecise_dtypes=True))
            once(g.memset(pad[:], 0.0))
            once(g.memset(pad[:, D + 1:D + 2], float(FAR)))
            cst.end()

            def iteration(a=None, m=None, b=None, c=None):
                ahead = following(a)
                if ahead is not None:
                    rstd(st1, "a_var", "a_rstd", ahead)
                if b is not None:
                    xb = xall[:, bass.ds(b, 1), :].rearrange("p a d -> p (a d)")
                    g.wait_ge(s["b_xn"], b + 1)
                    g.wait_ge(bo_done, 1)
                    g.tensor_tensor(xb, xb, bo_all[:], ALU.add).then_inc(s["b_xb"], 1)
                if a is not None:
                    hold(g, "pool", s["a_idx"], a + 1)
                    g.indirect_dma_start(mem[:], None, ctxR[:, :], bass.IndirectOffsetOnAxis(ap=gidx[:], axis=0))\
                        .then_inc(s["a_mem"], 16)
                if m is not None:
                    rstd(st2, "b_var", "b_rstd", m)
                if b is not None:
                    rstd(st3, "c_var", "c_rstd", b)
                if c is not None:
                    g.wait_ge(s["c_rows"], c + 1)
                    hold(g, "pool", s["c_weight"], c + 1)
                    for k, row in enumerate((row0, row1)):
                        g.indirect_dma_start(routed[:, :], bass.IndirectOffsetOnAxis(ap=slot[:, k:k + 1], axis=0),
                                             row[:, :], None).then_inc(s["c_scatter"], 16)


            def rest_of_weights():
                g.wait_ge(w_lead, 2)
                g.tensor_tensor(awv_rest[:], awv[:], awv_lead[:].bitcast(F32), ALU.subtract).then_inc(w_rest, 1)
                g.wait_ge(bo_ps, 1)
                g.tensor_tensor(awo_rest[:], awo[:], awo_lead[:].bitcast(F32), ALU.subtract).then_inc(w_rest, 1)
            pipeline(g, iteration, rest_of_weights)

            g.wait_ge(s["m_gb"], 32)
            g.wait_ge(s["b_x2"], BLK)
            g.wait_ge(s["c_xn"], BLK)
            g.tensor_tensor(xall[:], xall[:], beta_all.unsqueeze(1).broadcast_to((P, BLK, D)), ALU.add)\
                .then_inc(s["m_bx"], 1)

            def scatter_results(t):
                g.wait_ge(s["f_row"], t + 1)
                hold(g, "pool", s["f_yw"], t + 1)
                g.indirect_dma_start(expert_out[:, :], bass.IndirectOffsetOnAxis(ap=target_row[:], axis=0),
                                     yw, None, bounds_check=2 * TOK - 1, oob_is_err=False).then_inc(s["f_out"], 16)
            with g.Fori(0, TILES) as t:
                scatter_results(t)

            def sum_pairs(group):
                y = ypair[:, group * YG:(group + 1) * YG]
                g.wait_ge(s[f"y_pair{group}"], 16)
                g.tensor_tensor(y[:, :, 0, :], y[:, :, 0, :], y[:, :, 1, :], ALU.add).then_inc(s["y_sum"], 1)

            sum_pairs(0)
            for group in range(NG):
                if group + 1 < NG:
                    sum_pairs(group + 1)
                st = ystat[:, group % 2]
                g.wait_ge(s["y_var"], group + 1)
                g.tensor_scalar(st[:, :, 8:9], st[:, :, 7:8], EPS, None, ALU.add).then_inc(s["y_rstd"], 1)
                g.wait_ge(s["y_rstd"], 2 * group + 1)
                g.tensor_tensor(st[:, :, 9:10], st[:, :, 8:9], minus_half[:].unsqueeze(1).broadcast_to((P, YG, 1)), ALU.pow)\
                    .then_inc(s["y_rstd"], 1)

        @block.scalar
        def _(act):
            def bv_columns():
                act.wait_ge(ld_small, N_SMALL)
                act.activation(kT[:], bvT[:].unsqueeze(2).broadcast_to((P, HP, P)), ACT.Copy).then_inc(bvrep_done, 1)

            def lead_weights():
                act.wait_ge(ld_avo, 32)
                act.activation(awv_lead[:], awv[:], ACT.Copy).then_inc(w_lead, 1)
                act.activation(awo_lead[:], awo[:], ACT.Copy).then_inc(w_lead, 1)

            def iteration(a=None, m=None, b=None, c=None):
                A_, M_, B_, C_ = (i is not None for i in (a, m, b, c))
                if isinstance(a, int) and a == 1:
                    bv_columns()
                if B_:
                    act.wait_ge(s["b_xT_ps"], b + 1)
                    act.activation(x2T[:], bank[6][:, 0:D], ACT.Copy).then_inc(s["b_xT"], 1)
                if B_:
                    act.wait_ge(s["b_xT"], b + 1)
                    act.activation(x2_lead[:], x2T[:], ACT.Copy).then_inc(s["b_xlead"], 1)
                if C_:
                    act.wait_ge(s["c_xT_ps"], c + 1)
                if A_:
                    act.wait_ge(s["a_xT_ps"], a + 1)
                    act.activation(xT[:], bank[0][:, 0:D], ACT.Copy).then_inc(s["a_xT"], 1)
                if C_:
                    act.activation(x3T[:], bank[0][:, D:2 * D], ACT.Copy).then_inc(s["c_xT"], 1)
                    act.wait_ge(s["c_lg_ps"], c + 1)
                    act.activation(lgr[:], bank[1][:, 384:384 + E], ACT.Copy).then_inc(s["c_lg"], 1)
                if A_:
                    act.wait_ge(s["a_qpT_ps"], a + 1)
                    act.activation(qpT[:], bank[1][:, 0:D], ACT.Copy).then_inc(s["a_qpT"], 1)
                if M_:
                    act.wait_ge(s["a_xs"], m + 1)
                    act.activation(xs[:], xs[:], ACT.Exp, scale=float(XD) ** -0.5).then_inc(s["a_exp"], 1)
                if isinstance(m, int) and m == 0:
                    lead_weights()
                if B_:
                    act.wait_ge(s["b_q_ps"], 4 * b + 4)
                    for j in range(4):
                        i = act.activation(kT[:, 4 + j, :], bank[7][:, j * P:(j + 1) * P], ACT.Identity,
                                           bias=bkT[:, 4 + j:5 + j])
                    i.then_inc(s["b_k"], 1)
                if C_:
                    act.wait_ge(s["c_d"], c + 1)
                    act.activation(rsc[:, 1:2], rsc[:, 0:1], ACT.Exp).then_inc(s["c_exp"], 1)
                if A_:
                    act.wait_ge(s["a_sc_ps"], a + 1)
                    act.activation(sc[:], bank[0][:, 0:M], ACT.Copy).then_inc(s["a_sc"], 1)
                if M_:
                    for j in range(2):
                        act.wait_ge(s["a_pT_ps"], 2 * m + j + 1)
                        act.activation(xpT[:, 4 * j:4 * j + 4, :], bank[2 + j][:], ACT.Copy).then_inc(s["a_pT"], 1)

                def exponents(j):
                    act.wait_ge(s["b_as"], 2 * b + j + 1)
                    act.activation(as_[:, 8 * j:8 * j + 8, :], as_[:, 8 * j:8 * j + 8, :], ACT.Exp, scale=float(A) ** -0.5)\
                        .then_inc(s["b_exp"], 1)

                def values(j):
                    act.wait_ge(s["b_v_ps"], 2 * b + j + 1)
                    act.activation(vs[:, j * H // 2:(j + 1) * H // 2, :], bank[6 + j][:], ACT.Copy).then_inc(s["b_v"], 1)
                if B_:
                    exponents(0)
                    values(0)
                    exponents(1)
                    values(1)
                def turned(q):
                    act.wait_ge(s["b_pT_ps"], 4 * b + q + 1)
                    act.activation(apT[:, 4 * q:4 * q + 4, :], bank[PT_BANK[q]][:], ACT.Copy).then_inc(s["b_pT"], 1)
                if C_:
                    act.wait_ge(s["c_xn"], c + 1)
                    wait(act, s["c_scatter"], 32 * c)
                    act.activation(row0[:, 0:D], xn3[:], ACT.Copy)
                    act.activation(row1[:, 0:D], xn3[:], ACT.Copy).then_inc(s["c_rows"], 1)
                if M_:
                    act.wait_ge(s["a_av_ps"], m + 1)
                    act.activation(aoT[:], bank[1][:, 0:D], ACT.Copy).then_inc(s["a_aoT"], 1)
                if B_:
                    turned(0)
                    turned(1)
                    turned(2)
                    turned(3)
                    for j in range(2):
                        act.wait_ge(s["b_av_ps"], 2 * b + j + 1)
                        act.activation(z_lead[:, 4 * j:4 * j + 4, :], bank[6 + j][:].rearrange("p (c t) -> p c t", t=P),
                                       ACT.Copy).then_inc(s["b_zlead"], 1)
                if A_:
                    act.wait_ge(s["a_memT_ps"], a + 1)
                    act.activation(memT[:], bank[1][:, 0:D], ACT.Copy).then_inc(s["a_memT"], 1)

            act.wait_ge(ld_xw, 48)
            act.activation(wk_rep[:], xwkv[:, :, 0:XD].unsqueeze(2).broadcast_to((P, KD, P // XD, XD)), ACT.Copy)\
                .then_inc(xw_ready, 1)

            def last_first_weights():
                for e, (done, count) in ((E - 2, ("b_v_ps", 2 * BLK)), (E - 1, ("b_o_ps", BLK))):
                    act.wait_ge(s[done], count)
                    act.wait_ge(s["m_w1"], 16 * e)
                    act.dma_start(w1[:, e], W1T[e].rearrange("(k p) f -> p k f", p=P)).then_inc(s["m_w1"], 16)
            pipeline(act, iteration, before_last=last_first_weights)

            def hidden_out(t):
                act.wait_ge(s["f_h_ps"], 2 * t + 1)
                act.activation(hs[:, 0:512], bank[2][:], ACT.Copy).then_inc(s["f_hs_s"], 1)

            def hidden_relu(t):
                e = act.value_load(tile_ei[0:1, bass.ds(t, 1)], min_val=0, max_val=E - 1)
                act.wait_ge(s["f_hT_ps"], 2 * t + 1)
                for c in range(4):
                    i = act.activation(hT[:, c, :], bank[4][:, c * P:(c + 1) * P], ACT.Relu,
                                       bias=b1T[:, bass.ds(e * KF + c, 1)])
                i.then_inc(s["f_hT_s"], 1)

            def weigh(t):
                act.wait_ge(s["f_yb"], t + 1)
                wait(act, s["f_out"], 16 * t)
                act.activation(yw, yb, ACT.Copy, scale=meta[:, bass.ds(t, 1), 0]).then_inc(s["f_yw"], 1)

            act.wait_ge(ld_b12, 32)
            act.wait_ge(s["m_padrow"], 1)
            for e in range(1, E, 2):
                behind = act.value_load(padrow_i[0:1, e:e + 1], min_val=e * REG, max_val=e * REG + TOK)
                act.dma_start(routed[bass.ds(behind, P), :], pad[:]).then_inc(s["m_pads"], 16)
            act.wait_ge(s["m_plan"], 1)
            hidden_out(0)
            hidden_relu(0)
            hidden_out(1)
            weigh(0)
            hidden_relu(1)
            with act.Fori(2, TILES) as t:
                hidden_out(t)
                weigh(t - 1)
                hidden_relu(t)
            weigh(LAST)

            for group in range(NG):
                y, st = ypair[:, group * YG:(group + 1) * YG], ystat[:, group % 2]
                act.wait_ge(s["y_shift"], group + 1)
                for j in range(YG):
                    i = act.activation(y[:, j, 1, :], y[:, j, 0, :], ACT.Identity, scale=st[:, j, 9:10], bias=st[:, j, 8:9])
                i.then_inc(s["y_norm"], 1)

        @block.vector
        def _(v):
            vn = Steps(v, n_dve, 1)
            va, vm, vb, vc = Steps(v, a_dve, 4), Steps(v, m_dve, 5), Steps(v, b_dve, 9), Steps(v, c_dve, 14)

            def xblk(n):
                return xall[:, bass.ds(n, 1), :].rearrange("p a d -> p (a d)")

            def stats(steps, n, src, st, var):
                steps.did(v.bn_stats(st[:, 0:6], src))
                steps.hold_last(passed_by["dve"])
                v.bn_aggr(st[:, 6:8], st[:, 0:6]).then_inc(s[var], 1)

            def norm(n, src, st, rstd, dst, xn_sem):
                v.wait_ge(s[rstd], 2 * n + 2)
                v.tensor_scalar(dst, src, st[:, 6:7], st[:, 9:10], ALU.subtract, ALU.mult).then_inc(s[xn_sem], 1)

            def softmax_shift(steps, n, parts, mx, dst, done):
                hh = H // len(parts)
                for j, part in enumerate(parts):
                    steps.did(v.tensor_reduce(mx[:, j * hh:(j + 1) * hh], part, AX_X, ALU.max))
                steps.wait_last()
                for j, part in enumerate(parts):
                    i = v.tensor_tensor(dst[:, j * hh:(j + 1) * hh, :], part,
                                        mx[:, j * hh:(j + 1) * hh].unsqueeze(2).broadcast_to((P, hh, S)), ALU.subtract)
                    if j == len(parts) - 1:
                        i.then_inc(s[done], 1)

            def softmax_sums(steps, probs, rc):
                steps.did(v.tensor_reduce(rc, probs, AX_X, ALU.add))
                steps.wait_last()
                steps.did(v.reciprocal(rc, rc))
                steps.wait_last()

            def argmax(n):
                hold(v, "dve", s["a_sc"], n + 1)
                va.did(v.max(mx8[:], sc[:]))
                va.hold_last(passed_by["dve"])
                va.did(v.max_index(ix8[:], mx8[:], sc[:]))
                va.wait_last()
                va.did(v.tensor_copy(mx8[:, 0:1], ix8[:, 0:1]))
                va.wait_last()
                va.did(v.tensor_tensor(mx8[:, 1:2], mx8[:, 0:1], rowbase[:, bass.ds(n, 1)], ALU.add))
                va.wait_last()
                v.tensor_copy(gidx[:], mx8[:, 1:2]).then_inc(s["a_idx"], 1)

            def memory(n):
                v.wait_ge(s["a_mkv_ps"], n + 1)
                for b in range(BB):
                    v.tensor_tensor(mkb[:, b], bank[1][:, b * S:(b + 1) * S].unsqueeze(1).broadcast_to((P, P // XD, S)),
                                    headmask[:].unsqueeze(2).broadcast_to((P, P // XD, S)), ALU.mult)
                for r in range(2):
                    i = v.tensor_copy(mvw[r * S:(r + 1) * S, :, (2 + r) * XD:(3 + r) * XD],
                                      bank[1][r * S:(r + 1) * S, P:P + BB * XD].rearrange("p (b e) -> p b e", e=XD))
                i.then_inc(s["a_mkb"], 1)

            def project(n, c):
                v.wait_ge(s["b_q_ps"], 4 * n + c + 1)
                dst, bias = ((qT, bqT), (kT, bkT))[c // 2]
                hp = slice(4 * (c % 2), 4 * (c % 2) + 4)
                v.tensor_tensor(dst[:, hp, :], bank[6 + c % 2][:].rearrange("p (h t) -> p h t", t=P),
                                bias[:, hp].unsqueeze(2).broadcast_to((P, 4, P)), ALU.add).then_inc(s["b_q"], 1)

            def masked_shift(n, j):
                hh = slice(8 * j, 8 * j + 8)
                v.wait_ge(s["b_s_ps"], 2 * n + j + 1)
                vb.did(v.tensor_tensor(as_[:, hh, :], bank[4 + j][:].rearrange("p (h t) -> p h t", t=S),
                                       causal[:].unsqueeze(1).broadcast_to((P, 8, S)), ALU.min))
                vb.wait_last()
                vb.did(v.tensor_reduce(bmx[:, hh], as_[:, hh, :], AX_X, ALU.max))
                vb.wait_last()
                v.tensor_tensor(as_[:, hh, :], as_[:, hh, :], bmx[:, hh].unsqueeze(2).broadcast_to((P, 8, S)), ALU.subtract)\
                    .then_inc(s["b_as"], 1)

            def self_weights(n, j):
                hh = slice(8 * j, 8 * j + 8)
                v.wait_ge(s["b_exp"], 2 * n + j + 1)
                softmax_sums(vb, as_[:, hh, :], brc[:, hh])
                for i in range(BB):
                    r = slice(i * S, (i + 1) * S)
                    v.tensor_tensor(aprob[r, hh, r], as_[r, hh], brc[r, hh].unsqueeze(2).broadcast_to((S, 8, S)), ALU.mult)\
                        .then_inc(s["b_prob"], 1)

            def route_weights(n):
                vc.begin(n)
                v.wait_ge(s["c_lg"], n + 1)
                vc.did(v.tensor_tensor(lg[:], lgr[:], br_all[:], ALU.add))
                vc.hold_last(passed_by["dve"])
                vc.did(v.max(rv8[:], lg[:]))
                vc.hold_last(passed_by["dve"])
                v.tensor_tensor(rsc[:, 0:1], rv8[:, 1:2], rv8[:, 0:1], ALU.subtract).then_inc(s["c_d"], 1)
                vc.did(v.max_index(ri8[:], rv8[:], lg[:]))
                vc.wait_last()
                vc.did(v.tensor_copy(rsc[:, 4:6], ri8[:, 0:2]))
                vc.wait_last()
                vc.did(v.tensor_scalar(oh0[:], iota_e[:], rsc[:, 4:5], None, ALU.is_equal))
                vc.did(v.tensor_scalar(oh1[:], iota_e[:], rsc[:, 5:6], None, ALU.is_equal))
                vc.wait_last()
                v.tensor_tensor(ohs[:], oh0[:], oh1[:], ALU.add).then_inc(s["c_ohs"], 1)

            def route_counts(n):
                v.wait_ge(s["c_pos_ps"], n + 1)
                vc.did(v.tensor_tensor(pos[:], bank[1][:, 400:400 + E], run[:], ALU.add))
                vc.wait_last()
                v.tensor_tensor(run[:], run[:], bank[1][:, 416:416 + E], ALU.add).then_inc(s["c_pos"], 1)

            def route_slots(n):
                vc.did(v.tensor_tensor(pos[:], pos[:], region[:], ALU.add))
                vc.wait_last()
                for k, oh in enumerate((oh0, oh1)):
                    vc.did(v.tensor_tensor(rtmp[:], pos[:], oh[:], ALU.mult))
                    vc.wait_last()
                    vc.did(v.tensor_reduce(rsc[:, 6 + k:7 + k], rtmp[:], AX_X, ALU.add))
                    vc.wait_last()
                v.wait_ge(s["c_rows"], n + 1)
                v.tensor_copy(slot[:], rsc[:, 6:8])

            def route_rows(n):
                v.wait_ge(s["c_exp"], n + 1)
                vc.did(v.tensor_scalar(rsc[:, 2:3], rsc[:, 1:2], 1.0, None, ALU.add))
                vc.wait_last()
                vc.did(v.reciprocal(row0[:, D:D + 1], rsc[:, 2:3]))
                vc.wait_last()
                v.tensor_tensor(row1[:, D:D + 1], rsc[:, 1:2], row0[:, D:D + 1], ALU.mult)
                v.tensor_copy(row0[:, D + 1:D + 2], dest[:, bass.ds(n, 1), 0])
                v.tensor_copy(row1[:, D + 1:D + 2], dest[:, bass.ds(n, 1), 1]).then_inc(s["c_weight"], 1)

            def iteration(a=None, m=None, b=None, c=None):
                A_, M_, B_, C_ = (i is not None for i in (a, m, b, c))
                ahead = following(a)
                if A_:
                    va.begin(a)
                if C_:
                    wait(v, s["c_rows"], c)
                    wait(v, s["c_target"], 16 * c)
                    norm(c, xblk(c), st3, "c_rstd", xn3[:], "c_xn")
                if M_:
                    vm.begin(m)
                    memory(m)
                if B_:
                    vb.begin(b)
                    v.wait_ge(s["b_xlead"], b + 1)
                    v.tensor_tensor(x2_rest[:], x2T[:], x2_lead[:].bitcast(F32), ALU.subtract).then_inc(s["b_xrest"], 1)
                    project(b, 0)
                if isinstance(ahead, int) and ahead == 3:
                    v.wait_ge(ld_x, 16)
                if ahead is not None:
                    vn.begin(ahead)
                    stats(vn, ahead, xblk(ahead), st1, "a_var")
                if B_:
                    project(b, 1)
                if C_:
                    route_weights(c)
                if M_:
                    v.wait_ge(s["a_log_ps"], m + 1)
                    softmax_shift(vm, m, [bank[2 + j][:].rearrange("p (h m) -> p h m", m=S) for j in range(2)], amx, xs, "a_xs")
                if ahead is not None:
                    v.wait_ge(s["a_xT_ps"], a + 1)
                    norm(ahead, xblk(ahead), st1, "a_rstd", xn[:], "a_xn")
                if B_:
                    project(b, 2)
                if M_:
                    v.wait_ge(s["a_exp"], m + 1)
                    softmax_sums(vm, xs[:], arc[:])
                    v.tensor_tensor(xs[:], xs[:], arc[:].unsqueeze(2).broadcast_to((P, H, S)), ALU.mult).then_inc(s["a_prob"], 1)
                if C_:
                    route_counts(c)
                if B_:
                    for j in range(2):
                        masked_shift(b, j)
                    self_weights(b, 0)
                if B_:
                    self_weights(b, 1)
                if A_:
                    argmax(a)
                if C_:
                    route_slots(c)
                if M_:
                    v.wait_ge(s["a_wc_ps"], m + 1)
                    v.tensor_tensor(xblk(m), xblk(m), bank[0][:, 0:D], ALU.add).then_inc(s["a_x1"], 1)
                    hold(v, "dve", s["a_x1"], m + 1)
                    stats(vm, m, xblk(m), st2, "b_var")
                if B_:
                    for j in range(2):
                        v.wait_ge(s["b_zlead"], 2 * b + j + 1)
                        v.tensor_tensor(z_rest[:, 4 * j:4 * j + 4, :], bank[6 + j][:].rearrange("p (c t) -> p c t", t=P),
                                        z_lead[:, 4 * j:4 * j + 4, :].bitcast(F32), ALU.subtract).then_inc(s["b_zrest"], 1)
                if M_:
                    norm(m, xblk(m), st2, "b_rstd", xn2[:], "b_xn")
                if C_:
                    route_rows(c)
                if B_:
                    v.wait_ge(s["b_o_ps"], b + 1)
                    v.wait_ge(s["b_xb"], b + 1)
                    v.tensor_tensor(xblk(b), xblk(b), bank[5][:, 0:D], ALU.add).then_inc(s["b_x2"], 1)
                    hold(v, "dve", s["b_x2"], b + 1)
                    stats(vb, b, xblk(b), st3, "c_var")

            def output_bias():
                v.wait_ge(ld_small, N_SMALL)
                v.wait_ge(bo_ps, 1)
                v.tensor_tensor(bo_all[:], bo_all[:], bank[7][:, 0:D], ALU.add).then_inc(bo_done, 1)

            v.wait_ge(ld_x0, 16)
            vn.begin(0)
            stats(vn, 0, xblk(0), st1, "a_var")
            norm(0, xblk(0), st1, "a_rstd", xn[:], "a_xn")
            v.wait_ge(k_pool, K_POOL)
            pipeline(v, iteration, output_bias)
            for st in (va, vm, vb, vc):
                st.end()

            vm = Steps(v, p_dve, 17)
            vm.begin(0)

            def step(ins):
                vm.did(ins)
                vm.wait_last()
            step(v.tensor_tensor(cum2[:], run[:], region[:], ALU.add))
            v.tensor_copy(padrow_i[:], cum2[:]).then_inc(s["m_padrow"], 1)
            step(v.tensor_scalar(tiles_i[:], run[:], float(P - 1), None, ALU.add))
            step(v.tensor_scalar(tiles_i[:], tiles_i[:], P.bit_length() - 1, None, ALU.arith_shift_right))
            step(v.tensor_copy(tiles[:], tiles_i[:]))
            step(v.tensor_copy(cum[:], tiles[:]))
            for e in range(1, E):
                step(v.tensor_tensor(cum[:, e:e + 1], cum[:, e:e + 1], cum[:, e - 1:e], ALU.add))
            over = (P, TILES, E - 1)
            step(v.tensor_tensor(passed, iota_t[:].unsqueeze(2).broadcast_to(over),
                                 cum[:, 0:E - 1].unsqueeze(1).broadcast_to(over), ALU.is_ge))
            vm.did(v.tensor_reduce(tile_e[:], passed, AX_X, ALU.add))
            step(v.tensor_tensor(passed_tiles, passed, tiles[:, 0:E - 1].unsqueeze(1).broadcast_to(over), ALU.mult))
            step(v.tensor_reduce(tile_s[:], passed_tiles, AX_X, ALU.add))
            step(v.tensor_tensor(tile_s[:], iota_t[:], tile_s[:], ALU.subtract))
            v.tensor_scalar(tile_idle[:], iota_t[:], cum[:, E - 1:E], float(2 * E * REG), ALU.is_ge, ALU.mult)
            v.tensor_scalar(passed[:, :, 0], tile_s[:], float(P), None, ALU.mult)
            v.tensor_copy(tile_ei[:], tile_e[:]).then_inc(s["m_hist"], 1)
            v.wait_ge(s["m_hist"], 1)
            v.scalar_tensor_tensor(out=tile_s[:], in0=tile_e[:], scalar=float(REG), in1=passed[:, :, 0], op0=ALU.mult, op1=ALU.add)\
                .then_inc(s["m_hist"], 1)
            v.wait_ge(s["m_hist"], 2)
            v.tensor_tensor(tile_s[:], tile_s[:], tile_idle[:], ALU.add).then_inc(s["m_hist"], 1)
            v.wait_ge(s["m_hist"], 3)
            v.tensor_scalar(tile_ri[:], tile_s[:], float(E * REG), None, ALU.min).then_inc(s["m_plan"], 1)
            v.wait_ge(s["m_plan"], 1)
            vm.end()

            v.wait_ge(ld_b12, 32)

            def tile_in(t):
                v.wait_ge(s["f_xg"], 16 * t + 16)
                v.tensor_copy(meta[:, bass.ds(t, 1), :], xg[:, D:D + 2]).then_inc(s["f_meta"], 1)
                v.wait_ge(s["f_xT_ps"], t + 1)
                v.tensor_copy(xgT, bank[0][:, 0:D].rearrange("p (k t) -> p k t", t=P)).then_inc(s["f_xT"], 1)

            def hidden_out(t):
                v.wait_ge(s["f_h_ps"], 2 * t + 2)
                v.tensor_copy(hs[:, 512:1024], bank[3][:]).then_inc(s["f_hs_v"], 1)

            def hidden_relu(t):
                e = v.value_load(tile_ei[0:1, bass.ds(t, 1)], min_val=0, max_val=E - 1)
                v.wait_ge(s["f_hT_ps"], 2 * t + 2)
                for c in range(4):
                    i = v.tensor_scalar(hT[:, 4 + c, :], bank[5][:, c * P:(c + 1) * P],
                                        b1T[:, bass.ds(e * KF + 4 + c, 1)], 0.0, ALU.add, ALU.max)
                i.then_inc(s["f_hT_v"], 1)

            def result_out(t):
                e = v.value_load(tile_ei[0:1, bass.ds(t, 1)], min_val=0, max_val=E - 1)
                v.wait_ge(s["f_o_ps"], t + 1)
                wait(v, s["f_yw"], t)
                v.tensor_tensor(yb, bank[6][:, 0:D], b2_all[:, bass.ds(e * D, D)], ALU.add).then_inc(s["f_yb"], 1)
                wait(v, s["f_out"], 16 * t)
                v.tensor_copy(target_row[:], meta[:, bass.ds(t, 1), 1]).then_inc(s["f_row"], 1)

            tile_in(0)
            hidden_out(0)
            tile_in(1)
            hidden_relu(0)
            hidden_out(1)
            tile_in(2)
            result_out(0)
            hidden_relu(1)
            with v.Fori(2, LAST) as t:
                hidden_out(t)
                tile_in(t + 1)
                result_out(t - 1)
                hidden_relu(t)
            hidden_out(LAST)
            result_out(LAST - 1)
            hidden_relu(LAST)
            result_out(LAST)

            vy = Steps(v, y_dve, 1 + YG)
            v.wait_ge(s["m_tgt"], 32)
            v.wait_ge(s["m_gb"], 32)
            v.wait_ge(s["m_bx"], 1)
            wide = (P, YG, D)

            def gamma_residual(group):
                y = ypair[:, group * YG:(group + 1) * YG]
                blocks = xall[:, group * YG:(group + 1) * YG, :]
                v.wait_ge(s["y_norm"], group + 1)
                v.tensor_tensor(y[:, :, 1, :], y[:, :, 1, :], gamma_all.unsqueeze(1).broadcast_to(wide), ALU.mult)\
                    .then_inc(s["y_gamma"], 1)
                v.wait_ge(s["y_gamma"], group + 1)
                v.tensor_tensor(blocks, blocks, y[:, :, 1, :], ALU.add).then_inc(s["y_out"], 1)

            for group in range(NG):
                vy.begin(group)
                st = ystat[:, group % 2]
                y = ypair[:, group * YG:(group + 1) * YG]
                t = tgt[group * 2 // NG][:, group % (NG // 2) * YG:(group % (NG // 2) + 1) * YG]
                v.wait_ge(s["y_sum"], group + 1)
                vy.did(v.tensor_tensor(y[:, :, 0, :], y[:, :, 0, :], t, ALU.add))
                vy.wait_last()
                for j in range(YG):
                    vy.did(v.bn_stats(st[:, j, 0:6], y[:, j, 0, :]))
                vy.wait_last()
                for j in range(YG):
                    i = v.bn_aggr(st[:, j, 6:8], st[:, j, 0:6])
                i.then_inc(s["y_var"], 1)
                if group:
                    gamma_residual(group - 1)
                v.wait_ge(s["y_rstd"], 2 * group + 2)
                v.scalar_tensor_tensor(out=st[:, :, 8:9], in0=st[:, :, 6:7], scalar=-1.0, in1=st[:, :, 9:10],
                                       op0=ALU.mult, op1=ALU.mult).then_inc(s["y_shift"], 1)
            gamma_residual(NG - 1)
            vy.end()

        @block.tensor
        def _(pe):
            mm = nc.tensor.matmul
            tr = nc.tensor.transpose

            def output_bias():
                pe.wait_ge(k_pool, K_POOL)
                pe.wait_ge(bvrep_done, 1)
                pe.wait_ge(ld_avo, 32)
                for c in range(HP):
                    i = mm(bank[7][:, 0:D], kT[:, c, :], awo[:, c, :], start=c == 0, stop=c == HP - 1)
                i.then_inc(bo_ps, 1)

            def turn(a, m, c):
                if m is not None:
                    wait(pe, s["a_x1"], m)
                if c is not None:
                    pe.wait_ge(s["c_xn"], c + 1)
                    for k in range(KD):
                        i = tr(bank[0][:, D + k * P:D + (k + 1) * P], xn3[:, k * P:(k + 1) * P], ident[:])
                    i.then_inc(s["c_xT_ps"], 1)
                if a is not None:
                    pe.wait_ge(s["a_xn"], a + 1)
                    for k in range(KD):
                        i = tr(bank[0][:, k * P:(k + 1) * P], xn[:, k * P:(k + 1) * P], ident[:])
                    i.then_inc(s["a_xT_ps"], 1)

            def logits(n):
                pe.wait_ge(s["c_xT"], n + 1)
                for k in range(KD):
                    i = mm(bank[1][:, 384:384 + E], x3T[:, k, :], wr[:, k, :], start=k == 0, stop=k == KD - 1)
                i.then_inc(s["c_lg_ps"], 1)

            def queries(a, m, c):
                if m is not None:
                    pe.wait_ge(s["a_mkb"], m + 1)
                if c is not None:
                    pe.wait_ge(s["c_lg"], c + 1)
                pe.wait_ge(s["a_xT"], a + 1)
                for e in range(KD):
                    for k in range(KD):
                        i = mm(bank[1][:, e * P:(e + 1) * P], xwq[:, k, e * P:(e + 1) * P], xT[:, k, :],
                               start=k == 0, stop=k == KD - 1)
                i.then_inc(s["a_qpT_ps"], 1)

            def context_scores(n):
                pe.wait_ge(ld_ctx, 16 * n + 16)
                pe.wait_ge(s["a_qpT"], n + 1)
                for b in range(BB):
                    for k in range(KD):
                        i = mm(bank[0][b * S:(b + 1) * S, 0:M], qpT[:, k, b * S:(b + 1) * S], ctxb[:, b, k, :],
                               start=k == 0, stop=k == KD - 1)
                i.then_inc(s["a_sc_ps"], 1)

            def memory_turn(n):
                pe.wait_ge(s["a_mem"], 16 * n + 16)
                wait(pe, s["a_aoT"], n)
                for k in range(KD):
                    i = tr(bank[1][:, k * P:(k + 1) * P], mem[:, k * P:(k + 1) * P], ident[:])
                i.then_inc(s["a_memT_ps"], 1)

            def memory_project(n):
                hold(pe, "pe", s["a_memT"], n + 1)
                for k in range(KD):
                    mm(bank[1][:, 0:P], wk_rep[:, k].rearrange("p r d -> p (r d)"), memT[:, k, :], start=k == 0, stop=k == KD - 1)
                for r in range(2):
                    for b in range(BB):
                        for k in range(KD):
                            i = mm(bank[1][r * S:(r + 1) * S, P + b * XD:P + (b + 1) * XD], memT[:, k, b * S:(b + 1) * S],
                                   xwkv[:, k, XD:], start=k == 0, stop=k == KD - 1)
                i.then_inc(s["a_mkv_ps"], 1)

            def cross_scores(n):
                pe.wait_ge(s["a_mkb"], n + 1)
                for b in range(BB):
                    for e in range(KD):
                        i = mm(bank[2 + e][b * S:(b + 1) * S, :], qpT[:, e, b * S:(b + 1) * S],
                               mkb[:, b].rearrange("p h m -> p (h m)"), start=True, stop=True)
                i.then_inc(s["a_log_ps"], 1)

            def cross_turn(n):
                pe.wait_ge(s["a_prob"], n + 1)
                for j in range(2):
                    for h in range(4):
                        c = 2 * (4 * j + h)
                        i = tr(bank[2 + j][:, h * P:(h + 1) * P], xs[:, c:c + 2, :].rearrange("p h m -> p (h m)"), ident[:])
                    i.then_inc(s["a_pT_ps"], 1)

            def cross_values(a, c):
                hold(pe, "pe", s["a_pT"], 2 * a + 2)
                if c is not None:
                    hold(pe, "pe", s["c_pos"], c + 1)
                for k in range(KD):
                    for u in range(2):
                        for b in range(BB):
                            for w in range(2):
                                i = mm(bank[1][u * S:(u + 1) * S, k * P + b * S:k * P + (b + 1) * S],
                                       mvw[:, b, (2 - 2 * w) * XD:(6 - 2 * w) * XD],
                                       xpT[:, 4 * k + 2 * u + w, b * S:(b + 1) * S], start=w == 0, stop=w == 1)
                i.then_inc(s["a_av_ps"], 1)

            def cross_out(n, k):
                if k == 0:
                    pe.wait_ge(s["a_aoT"], n + 1)
                i = mm(bank[0][:, 0:D], aoT[:, k, :], xwc[:, k, :], start=k == 0, stop=k == KD - 1)
                if k == KD - 1:
                    i.then_inc(s["a_wc_ps"], 1)

            def self_turn(n):
                pe.wait_ge(s["b_xn"], n + 1)
                for k in range(KD):
                    i = tr(bank[6][:, k * P:(k + 1) * P], xn2[:, k * P:(k + 1) * P], ident[:])
                i.then_inc(s["b_xT_ps"], 1)

            def project(n, c):
                if c == 0:
                    pe.wait_ge(s["b_xT"], n + 1)
                if c >= 2:
                    pe.wait_ge(s["b_q"], 3 * n + c - 1)
                w = (awq, awk)[c // 2]
                for j in range(4):
                    f = (4 * (c % 2) + j) * P
                    for k in range(KD):
                        i = mm(bank[6 + c % 2][:, j * P:(j + 1) * P], w[:, k, f:f + P], x2T[:, k, :],
                               start=k == 0, stop=k == KD - 1)
                i.then_inc(s["b_q_ps"], 1)

            def values(n, j):
                pe.wait_ge(s["b_q"], 3 * n + 3)
                if j:
                    pe.wait_ge(s["b_k"], n + 1)
                else:
                    hold(pe, "pe", s["b_xrest"], n + 1)
                f = slice(j * 512, (j + 1) * 512)
                terms = [(x, w, k) for x, w in ((x2_lead, awv_lead), (x2_lead, awv_rest), (x2_rest, awv_lead)) for k in range(KD)]
                for t, (x, w, k) in enumerate(terms):
                    i = mm(bank[6 + j][:], x[:, k, :], w[:, k, f], start=t == 0, stop=t == len(terms) - 1)
                i.then_inc(s["b_v_ps"], 1)

            def self_scores(n, r):
                if r:
                    hold(pe, "pe", s["b_x2"], n)
                else:
                    hold(pe, "pe", s["b_q"], 3 * n + 3)
                    hold(pe, "pe", s["b_k"], n + 1)
                for h in range(r, H, 2):
                    hp = slice(A * r, A * r + A)
                    for b in range(BB):
                        i = mm(bank[4 + r][b * S:(b + 1) * S, (h // 2) * S:(h // 2 + 1) * S],
                               qT[hp, h // 2, b * S:(b + 1) * S], kT[hp, h // 2, b * S:(b + 1) * S], start=True, stop=True)
                i.then_inc(s["b_s_ps"], 1)

            def self_turn_weights(n, q):
                pe.wait_ge(s["b_prob"], 4 * n + 2 + 2 * (q // 2))
                for h in range(4):
                    i = tr(bank[PT_BANK[q]][:, h * P:(h + 1) * P], aprob[:, 4 * q + h, :], ident[:])
                i.then_inc(s["b_pT_ps"], 1)

            def self_values(n, q):
                if q == 0:
                    pe.wait_ge(s["b_v"], 2 * n + 2)
                hold(pe, "pe", s["b_pT"], 4 * n + q + 1)
                for j in range(4 * q, 4 * q + 4):
                    r, c = j // HP, j % HP
                    i = mm(bank[6 + c // 4][r * A:(r + 1) * A, c % 4 * P:(c % 4 + 1) * P],
                           vs[:, 2 * c + r, :], apT[:, j, :], start=True, stop=True)
                if q >= 2:
                    i.then_inc(s["b_av_ps"], 1)

            def self_out(n, j):
                hold(pe, "pe", s["b_zlead"], 2 * n + j + 1)
                for w in (awo_lead, awo_rest):
                    for c in range(4 * j, 4 * j + 4):
                        mm(bank[5][:, 0:D], z_lead[:, c, :], w[:, c, :], start=c == 0 and w is awo_lead, stop=False)

            def self_out_rest(n):
                hold(pe, "pe", s["b_zrest"], 2 * n + 2)
                for c in range(HP):
                    i = mm(bank[5][:, 0:D], z_rest[:, c, :], awo_lead[:, c, :], start=False, stop=c == HP - 1)
                i.then_inc(s["b_o_ps"], 1)

            def count(n, a):
                pe.wait_ge(s["c_ohs"], n + 1)
                if a is not None:
                    pe.wait_ge(s["a_qpT"], a + 1)
                mm(bank[1][:, 400:400 + E], before[:], ohs[:], start=True, stop=True)
                mm(bank[1][:, 416:416 + E], ones[:], ohs[:], start=True, stop=True).then_inc(s["c_pos_ps"], 1)

            def iteration(a=None, m=None, b=None, c=None):
                A_, M_, B_, C_ = (i is not None for i in (a, m, b, c))
                if isinstance(b, int) and b == 0:
                    pe.wait_ge(bo_done, 1)
                    pe.wait_ge(ld_aw, 48)
                if B_:
                    self_turn(b)
                if M_:
                    memory_project(m)
                if B_:
                    project(b, 0)
                turn(a, m, c)
                if B_:
                    project(b, 1)
                if C_:
                    if M_:
                        pe.wait_ge(s["a_mkb"], m + 1)
                    logits(c)
                if M_:
                    cross_scores(m)
                if A_:
                    queries(a, m, c)
                if B_:
                    project(b, 2)
                    project(b, 3)
                if A_:
                    context_scores(a)
                if C_:
                    count(c, a)
                if B_:
                    self_scores(b, 0)
                if M_:
                    cross_turn(m)
                if B_:
                    self_scores(b, 1)
                    if isinstance(b, int) and b == 0:
                        pe.wait_ge(w_rest, 2)
                    values(b, 0)
                    values(b, 1)
                if M_:
                    cross_values(m, c)
                if B_:
                    self_turn_weights(b, 0)
                    self_turn_weights(b, 1)
                if M_:
                    cross_out(m, 0)
                if B_:
                    self_values(b, 0)
                    self_values(b, 1)
                    self_turn_weights(b, 2)
                    self_turn_weights(b, 3)
                if M_:
                    cross_out(m, 1)
                if B_:
                    self_values(b, 2)
                    self_values(b, 3)
                    self_out(b, 0)
                    self_out(b, 1)
                if isinstance(m, int) and m == 0:
                    output_bias()
                if A_:
                    memory_turn(a)
                if B_:
                    self_out_rest(b)

            pe.wait_ge(ident_ready, 2)
            pe.wait_ge(ld_xw, 48)
            pe.wait_ge(xw_ready, 1)
            pipeline(pe, iteration)

            def tile_in(t):
                pe.wait_ge(s["f_xg"], 16 * t + 16)
                wait(pe, s["f_xT"], t)
                for k in range(KD):
                    i = tr(bank[0][:, k * P:(k + 1) * P], xg[:, k * P:(k + 1) * P], ident[:])
                i.then_inc(s["f_xT_ps"], 1)

            def up(t):
                e = pe.value_load(tile_ei[0:1, bass.ds(t, 1)], min_val=0, max_val=E - 1)
                pe.wait_ge(s["m_w1"], e * 16 + 16)
                pe.wait_ge(s["f_xT"], t + 1)
                for j in range(FH):
                    wait(pe, s["f_hs_v" if j else "f_hs_s"], t)
                    for k in range(KD):
                        i = mm(bank[2 + j][:], xgT[:, k, :], w1[:, bass.ds(e, 1), k, j * 512:(j + 1) * 512],
                               start=k == 0, stop=k == KD - 1)
                    i.then_inc(s["f_h_ps"], 1)

            def hidden_turn(t):
                for j in range(FH):
                    pe.wait_ge(s["f_hs_v" if j else "f_hs_s"], t + 1)
                    wait(pe, s["f_hT_v" if j else "f_hT_s"], t)
                    for c in range(4):
                        i = tr(bank[4 + j][:, c * P:(c + 1) * P], hs[:, (4 * j + c) * P:(4 * j + c + 1) * P], ident[:])
                    i.then_inc(s["f_hT_ps"], 1)

            def down(t):
                e = pe.value_load(tile_ei[0:1, bass.ds(t, 1)], min_val=0, max_val=E - 1)
                wait(pe, s["f_yb"], t)
                pe.wait_ge(s["m_w2"], e * 16 + 16)
                for c in range(KF):
                    if c % 4 == 0:
                        pe.wait_ge(s["f_hT_v" if c else "f_hT_s"], t + 1)
                    i = mm(bank[6][:, 0:D], hT[:, c, :], w2[:, bass.ds(e, 1), c, :], start=c == 0, stop=c == KF - 1)
                i.then_inc(s["f_o_ps"], 1)

            pe.wait_ge(s["m_plan"], 1)
            tile_in(0)
            up(0)
            tile_in(1)
            hidden_turn(0)
            up(1)
            tile_in(2)
            down(0)
            hidden_turn(1)
            with pe.Fori(2, LAST) as t:
                up(t)
                tile_in(t + 1)
                down(t - 1)
                hidden_turn(t)
            up(LAST)
            down(LAST - 1)
            hidden_turn(LAST)
            down(LAST)


def kernel(**inputs):
    import numpy as np
    import concourse.bacc as bacc
    from concourse.bass_utils import run_bass_kernel_spmd

    def lay(a):
        return np.ascontiguousarray(a)

    g = {k: np.asarray(v) for k, v in inputs.items()}
    D = g["x"].shape[-1]
    arrays = {
        "x": lay(g["x"]),
        "ctxT": lay(g["ctx_1024"].transpose(0, 2, 1)),
        "ctxR": lay(g["ctx_1024"].reshape(-1, D)),
        "xWqT": lay(g["L0_xattn_Wq"].T),
        "xWkvT": lay(g["L0_xattn_Wkv"].T),
        "xWcT": lay(g["L0_xattn_Wc"].T),
        "aWq": lay(g["L0_attn_Wq"].transpose(1, 0, 2).reshape(D, -1)),
        "aWk": lay(g["L0_attn_Wk"].transpose(1, 0, 2).reshape(D, -1)),
        "aWv": lay(g["L0_attn_Wv"].transpose(1, 0, 2).reshape(D, -1)),
        "aWo": lay(g["L0_attn_Wo"].reshape(-1, D)),
        "bq": lay(g["L0_attn_bq"].reshape(-1)),
        "bk": lay(g["L0_attn_bk"].reshape(-1)),
        "bv": lay(g["L0_attn_bv"].reshape(-1)),
        "bo": lay(g["L0_attn_bo"]),
        "WrT": lay(g["L0_ffn_Wr"].T),
        "br": lay(g["L0_ffn_br"]),
        "W1T": lay(g["L0_ffn_W1"].transpose(0, 2, 1)),
        "b1": lay(g["L0_ffn_b1"].reshape(-1)),
        "W2T": lay(g["L0_ffn_W2"].transpose(0, 2, 1)),
        "b2": lay(g["L0_ffn_b2"].reshape(-1)),
        "gamma": lay(g["L0_ffn_gamma"]),
        "beta": lay(g["L0_ffn_beta"]),
    }
    nc = bacc.Bacc("TRN2", target_bir_lowering=False, num_devices=1)
    aps = {k: nc.dram_tensor(k, a.shape, mybir.dt.from_np(a.dtype), kind="ExternalInput").ap() for k, a in arrays.items()}
    out = nc.dram_tensor("out", g["x"].shape, F32, kind="ExternalOutput").ap()
    perceiver_layer(nc, out=out, **aps)
    return run_bass_kernel_spmd(nc, [arrays], core_ids=[0]).results[0]["out"]
```
